# Optimizing a Trainium2 kernel written in Bass

```python
import numpy as np
import jax
import jax.numpy as jnp

def _softmax(x, axis=-1):
    return jax.nn.softmax(x, axis=axis)

def _gelu(x):
    return jax.nn.gelu(x, approximate=True)

def _silu(x):
    return jax.nn.silu(x)

def _sigmoid(x):
    return jax.nn.sigmoid(x)

def _layernorm(x, axis=-1, eps=1e-05):
    m = jnp.mean(x, axis=axis, keepdims=True)
    v = jnp.var(x, axis=axis, keepdims=True)
    return (x - m) / jnp.sqrt(v + eps)

def _scatter_add(tgt, idx, src, axis=0):
    return tgt.at[idx].add(src)

def _segment_sum(src, seg, n):
    return jax.ops.segment_sum(src, seg, n)
kernel_name = 'mk_gps_d1_gnn_r16_c44b5e'

def setup_inputs(seed: int=0):
    np.random.seed(seed)
    _w = jnp.asarray

    def _rec_inputs():
        import jax
        import jax.numpy as jnp
        _gk = jax.random.key(seed)
        x = -6.415e-05 + 1 * jax.random.normal(jax.random.fold_in(_gk, 1), (3125, 512), jnp.float32)
        _s = jax.random.randint(jax.random.fold_in(_gk, 2), (25000,), 0, 3125, jnp.int32)
        _d = jax.random.randint(jax.random.fold_in(_gk, 3), (25000,), 0, 3125, jnp.int32)
        _loop = jnp.arange(3125, dtype=jnp.int32)
        src = jnp.concatenate([_s, _d, _loop])
        dst = jnp.concatenate([_d, _s, _loop])
        _o = jnp.argsort(dst, stable=True)
        src = src[_o]
        dst = dst[_o]
        return (x, src, dst)
    x, src, dst = _rec_inputs()

    def _L0_gnn_setup():
        import jax, jax.numpy as jnp
        import numpy as np
        D = 512
        H = 8
        DH = D // H
        F = 128
        L = 2
        N = 1250
        E = 20000
        EPS = 1e-05

        def _xavier(key, shape):
            fan_out, fan_in = (shape[-2], shape[-1])
            lim = float(np.sqrt(6.0 / (fan_in + fan_out)))
            return jax.random.uniform(key, shape, jnp.float32, -lim, lim)

        def _batchnorm(x, g, b):
            mu = jnp.mean(x, axis=0)
            var = jnp.mean(jnp.square(x - mu), axis=0)
            return (x - mu) * jax.lax.rsqrt(var + EPS) * g + b

        def _layernorm(x, g, b):
            mu = jnp.mean(x, axis=-1, keepdims=True)
            var = jnp.mean(jnp.square(x - mu), axis=-1, keepdims=True)
            return (x - mu) * jax.lax.rsqrt(var + EPS) * g + b
        key = jax.random.key(seed)
        ks = jax.random.split(key, 12)
        src = jax.random.normal(ks[0], (N, D), jnp.float32)
        edge_index = jax.random.randint(ks[1], (2, E), 0, N)
        return {'src': src, 'edge_index': edge_index, 'Wq': _xavier(ks[2], (L, D, D)), 'bq': jnp.zeros((L, D), jnp.float32), 'Wk': _xavier(ks[3], (L, D, D)), 'Wv': _xavier(ks[4], (L, D, D)), 'Wo': _xavier(ks[5], (L, D, D)), 'bo': jnp.zeros((L, D), jnp.float32), 'W1': _xavier(ks[6], (L, F, D)), 'b1': jnp.zeros((L, F), jnp.float32), 'W2': _xavier(ks[7], (L, D, F)), 'b2': jnp.zeros((L, D), jnp.float32), 'g1': jnp.ones((L, D), jnp.float32), 'beta1': jnp.zeros((L, D), jnp.float32), 'g2': jnp.ones((L, D), jnp.float32), 'beta2': jnp.zeros((L, D), jnp.float32), 'ln_g': jnp.ones((D,), jnp.float32), 'ln_b': jnp.zeros((D,), jnp.float32)}
    _L0_gnn_all = _L0_gnn_setup()
    _L0_gnn_in = {k: v for k, v in _L0_gnn_all.items() if k in ('Wq', 'bq', 'Wk', 'Wv', 'Wo', 'bo', 'W1', 'b1', 'W2', 'b2', 'g1', 'beta1', 'g2', 'beta2', 'ln_g', 'ln_b')}
    del _L0_gnn_all

    def _L0_mix_setup():
        import jax, jax.numpy as jnp
        import numpy as np
        DIM, HEADS, DIM_HEAD = (512, 8, 64)
        key = jax.random.key(seed)
        ks = jax.random.split(key, 9)
        B, T = (4, 256)
        s = 1.0 / np.sqrt(DIM)
        x = jax.random.normal(ks[0], (B, T, DIM), dtype=jnp.float32)
        Wq = jax.random.uniform(ks[1], (DIM, DIM), jnp.float32, -s, s)
        Wk = jax.random.uniform(ks[2], (DIM, DIM), jnp.float32, -s, s)
        Wv = jax.random.uniform(ks[3], (DIM, DIM), jnp.float32, -s, s)
        Wp = jax.random.uniform(ks[4], (DIM, DIM), jnp.float32, -s, s)
        bq = jax.random.uniform(ks[5], (DIM,), jnp.float32, -s, s)
        bk = jax.random.uniform(ks[6], (DIM,), jnp.float32, -s, s)
        bv = jax.random.uniform(ks[7], (DIM,), jnp.float32, -s, s)
        bp = jax.random.uniform(ks[8], (DIM,), jnp.float32, -s, s)
        return {'x': x, 'Wq': Wq, 'bq': bq, 'Wk': Wk, 'bk': bk, 'Wv': Wv, 'bv': bv, 'Wp': Wp, 'bp': bp}
    _L0_mix_all = _L0_mix_setup()
    _L0_mix_in = {k: v for k, v in _L0_mix_all.items() if k in ('Wq', 'bq', 'Wk', 'bk', 'Wv', 'bv', 'Wp', 'bp')}
    del _L0_mix_all

    def _L0_ffn_setup():
        import jax, jax.numpy as jnp
        import numpy as np
        NUM_EXPERTS = 8
        TOP_K = 2
        HIDDEN = 512
        INTERMEDIATE = 128
        BATCH, SEQ = (8, 128)
        key = jax.random.key(seed)
        ks = jax.random.split(key, 7)
        s_in = 1.0 / np.sqrt(HIDDEN)
        s_mid = 1.0 / np.sqrt(INTERMEDIATE)
        return {'x': jax.random.normal(ks[0], (BATCH, SEQ, HIDDEN), jnp.float32), 'Wg': jax.random.normal(ks[1], (HIDDEN, NUM_EXPERTS), jnp.float32) * s_in, 'bg': jnp.zeros((NUM_EXPERTS,), jnp.float32), 'W1': jax.random.normal(ks[2], (NUM_EXPERTS, HIDDEN, INTERMEDIATE), jnp.float32) * s_in, 'b1': jnp.zeros((NUM_EXPERTS, INTERMEDIATE), jnp.float32), 'W2': jax.random.normal(ks[3], (NUM_EXPERTS, INTERMEDIATE, HIDDEN), jnp.float32) * s_mid, 'b2': jnp.zeros((NUM_EXPERTS, HIDDEN), jnp.float32)}
    _L0_ffn_all = _L0_ffn_setup()
    _L0_ffn_in = {k: v for k, v in _L0_ffn_all.items() if k in ('Wg', 'bg', 'W1', 'b1', 'W2', 'b2')}
    del _L0_ffn_all
    return {'x': x, 'src': src, 'dst': dst, 'L0_gnn_Wq': _L0_gnn_in['Wq'], 'L0_gnn_bq': _L0_gnn_in['bq'], 'L0_gnn_Wk': _L0_gnn_in['Wk'], 'L0_gnn_Wv': _L0_gnn_in['Wv'], 'L0_gnn_Wo': _L0_gnn_in['Wo'], 'L0_gnn_bo': _L0_gnn_in['bo'], 'L0_gnn_W1': _L0_gnn_in['W1'], 'L0_gnn_b1': _L0_gnn_in['b1'], 'L0_gnn_W2': _L0_gnn_in['W2'], 'L0_gnn_b2': _L0_gnn_in['b2'], 'L0_gnn_g1': _L0_gnn_in['g1'], 'L0_gnn_beta1': _L0_gnn_in['beta1'], 'L0_gnn_g2': _L0_gnn_in['g2'], 'L0_gnn_beta2': _L0_gnn_in['beta2'], 'L0_gnn_ln_g': _L0_gnn_in['ln_g'], 'L0_gnn_ln_b': _L0_gnn_in['ln_b'], 'L0_mix_Wq': _L0_mix_in['Wq'], 'L0_mix_bq': _L0_mix_in['bq'], 'L0_mix_Wk': _L0_mix_in['Wk'], 'L0_mix_bk': _L0_mix_in['bk'], 'L0_mix_Wv': _L0_mix_in['Wv'], 'L0_mix_bv': _L0_mix_in['bv'], 'L0_mix_Wp': _L0_mix_in['Wp'], 'L0_mix_bp': _L0_mix_in['bp'], 'L0_ffn_Wg': _L0_ffn_in['Wg'], 'L0_ffn_bg': _L0_ffn_in['bg'], 'L0_ffn_W1': _L0_ffn_in['W1'], 'L0_ffn_b1': _L0_ffn_in['b1'], 'L0_ffn_W2': _L0_ffn_in['W2'], 'L0_ffn_b2': _L0_ffn_in['b2']}

def reference(x, src, dst, L0_gnn_Wq, L0_gnn_bq, L0_gnn_Wk, L0_gnn_Wv, L0_gnn_Wo, L0_gnn_bo, L0_gnn_W1, L0_gnn_b1, L0_gnn_W2, L0_gnn_b2, L0_gnn_g1, L0_gnn_beta1, L0_gnn_g2, L0_gnn_beta2, L0_gnn_ln_g, L0_gnn_ln_b, L0_mix_Wq, L0_mix_bq, L0_mix_Wk, L0_mix_bk, L0_mix_Wv, L0_mix_bv, L0_mix_Wp, L0_mix_bp, L0_ffn_Wg, L0_ffn_bg, L0_ffn_W1, L0_ffn_b1, L0_ffn_W2, L0_ffn_b2):
    import jax
    import jax.numpy as jnp

    def _L0_gnn_ref(src, edge_index, Wq, bq, Wk, Wv, Wo, bo, W1, b1, W2, b2, g1, beta1, g2, beta2, ln_g, ln_b):
        import jax, jax.numpy as jnp
        import numpy as np
        D = 512
        H = 8
        DH = D // H
        F = 128
        L = 2
        N = 1250
        E = 20000
        EPS = 1e-05

        def _xavier(key, shape):
            fan_out, fan_in = (shape[-2], shape[-1])
            lim = float(np.sqrt(6.0 / (fan_in + fan_out)))
            return jax.random.uniform(key, shape, jnp.float32, -lim, lim)

        def _batchnorm(x, g, b):
            mu = jnp.mean(x, axis=0)
            var = jnp.mean(jnp.square(x - mu), axis=0)
            return (x - mu) * jax.lax.rsqrt(var + EPS) * g + b

        def _layernorm(x, g, b):
            mu = jnp.mean(x, axis=-1, keepdims=True)
            var = jnp.mean(jnp.square(x - mu), axis=-1, keepdims=True)
            return (x - mu) * jax.lax.rsqrt(var + EPS) * g + b
        n = src.shape[0]
        scaling = float(DH) ** (-0.5)
        tgt = edge_index[1]
        srcidx = edge_index[0]
        x = src
        for l in range(L):
            q = ((x @ Wq[l].T + bq[l]) * scaling).reshape(n, H, DH)
            k = (x @ Wk[l].T).reshape(n, H, DH)
            v = (x @ Wv[l].T).reshape(n, H, DH)
            scores = jnp.einsum('ehd,ehd->eh', q[tgt], k[srcidx])
            m = jax.ops.segment_max(scores, tgt, num_segments=n)
            p = jnp.exp(scores - m[tgt])
            s = jax.ops.segment_sum(p, tgt, num_segments=n)
            w = p / (s[tgt] + 1e-16)
            agg = jax.ops.segment_sum(w[:, :, None] * v[srcidx], tgt, num_segments=n)
            attn = agg.reshape(n, D) @ Wo[l].T + bo[l]
            x = _batchnorm(x + attn, g1[l], beta1[l])
            ff = jax.nn.relu(x @ W1[l].T + b1[l]) @ W2[l].T + b2[l]
            x = _batchnorm(x + ff, g2[l], beta2[l])
        return _layernorm(x, ln_g, ln_b)

    def _L0_mix_ref(x, Wq, bq, Wk, bk, Wv, bv, Wp, bp):
        import jax, jax.numpy as jnp
        import numpy as np
        DIM, HEADS, DIM_HEAD = (512, 8, 64)
        B, T, _ = x.shape
        H, D = (HEADS, DIM_HEAD)

        def proj(W, b):
            return (x @ W.T + b).reshape(B, T, H, D).transpose(0, 2, 1, 3)
        q = jax.nn.softmax(proj(Wq, bq), axis=-1)
        k = jax.nn.softmax(proj(Wk, bk), axis=-1)
        v = proj(Wv, bv)
        k_sum = k.sum(axis=2, keepdims=True)
        D_inv = 1.0 / (q * k_sum).sum(axis=-1, keepdims=True)
        context = jnp.einsum('bhtd,bhte->bhde', k, v)
        out = jnp.einsum('bhtd,bhde->bhte', q, context) * D_inv + q
        out = out.transpose(0, 2, 1, 3).reshape(B, T, H * D)
        return out @ Wp.T + bp

    def _L0_ffn_ref(x, Wg, bg, W1, b1, W2, b2):
        import jax, jax.numpy as jnp
        import numpy as np
        NUM_EXPERTS = 8
        TOP_K = 2
        HIDDEN = 512
        INTERMEDIATE = 128
        BATCH, SEQ = (8, 128)
        B, S, H = x.shape
        xf = x.reshape(B * S, H)
        logits = xf @ Wg + bg
        probs = jax.nn.softmax(logits, axis=-1)
        _, top_idx = jax.lax.top_k(probs, TOP_K)
        mask = jnp.any(top_idx[:, :, None] == jnp.arange(NUM_EXPERTS)[None, None, :], axis=1)
        comb = probs * mask.astype(probs.dtype)
        out = jnp.zeros_like(xf)
        for e in range(NUM_EXPERTS):
            h = jax.nn.gelu(xf @ W1[e] + b1[e])
            y = h @ W2[e] + b2[e]
            out = out + comb[:, e:e + 1] * y
        return out.reshape(B, S, H)
    edge_index = jnp.stack([src, dst])
    xn = _layernorm(x, axis=-1)
    x = x + _L0_gnn_ref(xn, edge_index, L0_gnn_Wq, L0_gnn_bq, L0_gnn_Wk, L0_gnn_Wv, L0_gnn_Wo, L0_gnn_bo, L0_gnn_W1, L0_gnn_b1, L0_gnn_W2, L0_gnn_b2, L0_gnn_g1, L0_gnn_beta1, L0_gnn_g2, L0_gnn_beta2, L0_gnn_ln_g, L0_gnn_ln_b) + _L0_mix_ref(xn[None], L0_mix_Wq, L0_mix_bq, L0_mix_Wk, L0_mix_bk, L0_mix_Wv, L0_mix_bv, L0_mix_Wp, L0_mix_bp)[0]
    x = x + _L0_ffn_ref(_layernorm(x, axis=-1)[None], L0_ffn_Wg, L0_ffn_bg, L0_ffn_W1, L0_ffn_b1, L0_ffn_W2, L0_ffn_b2)[0]
    return x

_drawn_inputs = setup_inputs


def setup_inputs(seed=0):
    import zlib

    import numpy as np

    out = dict(_drawn_inputs(seed))
    spreads = {'L0_gnn_bq': (0.0, 0.283),
     'L0_gnn_bo': (0.0, 2.0),
     'L0_gnn_b1': (0.0, 0.277),
     'L0_gnn_b2': (0.0, 2.0),
     'L0_gnn_g1': (1.0, 0.2),
     'L0_gnn_beta1': (0.0, 0.1),
     'L0_gnn_g2': (1.0, 0.2),
     'L0_gnn_beta2': (0.0, 0.1),
     'L0_gnn_ln_g': (1.0, 0.2),
     'L0_gnn_ln_b': (0.0, 0.1),
     'L0_ffn_bg': (0.0, 0.298),
     'L0_ffn_b1': (0.0, 0.517),
     'L0_ffn_b2': (0.0, 0.338)}
    factors = {'L0_mix_Wq': 7.472,
     'L0_mix_bq': 8.0,
     'L0_mix_Wk': 8.0,
     'L0_mix_bk': 8.0,
     'L0_mix_Wv': 8.0,
     'L0_mix_bv': 4.355,
     'L0_mix_Wp': 3.381,
     'L0_mix_bp': 3.401}
    for name, (base, spread) in spreads.items():
        noise = np.random.default_rng([zlib.crc32(name.encode()), seed]).standard_normal(out[name].shape)
        drawn = base * np.exp(spread * noise) if base else spread * noise
        out[name] = jnp.asarray(drawn.astype(out[name].dtype))
    for name, factor in factors.items():
        out[name] = (out[name] * factor).astype(out[name].dtype)
    return out
```

```python
from contextlib import ExitStack

import concourse.bass as bass
from concourse import mybir

P = 128
N, D, H, DH = 3125, 512, 8, 64
NT = 25
ROWS = [min(P, N - P * t) for t in range(NT)]
CHUNKS = [(c, min(512, N - c)) for c in range(0, N, 512)]
NE = 53125
ET = 416
EP = ET * P
NCH = 16
NJ = ET // NCH
CH = NJ * P
TB, TP = 4, 104
AGG_B = 3200
AGG_ROWS = AGG_B + ET
FAR = 8192.0
BIG = 1.0e30
EPS = 1e-5

F32 = mybir.dt.float32
BF16 = mybir.dt.bfloat16
I32 = mybir.dt.int32
U32 = mybir.dt.uint32
U8 = mybir.dt.uint8
ALU = mybir.AluOpType
ACT = mybir.ActivationFunctionType
AXX = mybir.AxisListType.X

C_BO, C_B2, C_G1, C_E1, C_G2, C_E2, C_B1, C_MB1 = 0, 8, 16, 24, 32, 40, 48, 50


class Queue:

    def __init__(self, engine, sem):
        self.engine, self.sem, self.n, self.seen = engine, sem, 0, {}

    def wait(self, *marks):
        for m in marks:
            if m is None:
                continue
            if isinstance(m, list):
                self.wait(*m)
                continue
            sem, v = m
            if self.seen.get(id(sem), 0) < v:
                self.seen[id(sem)] = v
                self.engine.wait_ge(sem, v)

    def do(self, f, *marks):
        self.wait(*marks)
        self.n += 1
        f(self.engine).then_inc(self.sem, 1)
        return (self.sem, self.n)

    def quiet(self, f, *marks):
        self.wait(*marks)
        f(self.engine)


class Chan:

    def __init__(self, sem):
        self.sem, self.n = sem, 0

    def mark(self):
        return (self.sem, self.n) if self.n else None

    def send(self, queue, f, *marks):
        queue.wait(*marks)
        self.n += 16
        f(queue.engine).then_inc(self.sem, 16)
        return (self.sem, self.n)


class Ring:

    def __init__(self, bufs):
        self.bufs, self.free, self.at = bufs, [None] * len(bufs), 0

    def take(self):
        i = self.at % len(self.bufs)
        self.at += 1
        return i, self.bufs[i], self.free[i]


def build(nc, A, out):
    with ExitStack() as ctx:
        def sb(name, shape, dt=F32):
            return ctx.enter_context(nc.sbuf_tensor(name, shape, dt))

        def sem(name):
            return ctx.enter_context(nc.semaphore(name))

        def chan(name):
            return Chan(sem(name))

        def dram(name, shape):
            return nc.dram_tensor(name, shape, F32, kind="Internal").ap()

        PE, DVE, ACTQ, POOL, SP = (
            Queue(e, sem(n)) for e, n in ((nc.tensor, "s_pe"), (nc.vector, "s_dve"), (nc.scalar, "s_act"),
                                          (nc.gpsimd, "s_pool"), (nc.sync, "s_sp")))

        xT = sb("xT", [P, 4, N])
        Y = sb("Y", [P, 12800])
        Yt = Y[:, :].rearrange("p (t d) -> p t d", t=NT)
        WA = sb("WA", [P, 3, 4, 512])
        G = sb("G", [P, 16, 512])
        Sc = sb("Sc", [P, ET * H])
        same = sb("same", [P, CH + 1], U8)
        stage = sb("stage", [P, 4, 512])
        work = sb("work", [P, 3, 512])
        rowsb = sb("rowsb", [P, 5, 512])
        ordE = sb("ordE", [P, ET])
        fvE = sb("fvE", [P, ET])
        srcE = sb("srcE", [P, ET], U32)
        dstE = sb("dstE", [P, ET], U32)
        segE = sb("segE", [P, ET], U32)
        ident = sb("ident", [P, P])
        iota = sb("iota", [P, P])
        onehot = sb("onehot", [P, 4, P])
        zero = work[:, 2, :]
        ones = sb("ones", [P, 1])
        vec = sb("vec", [P, 58])
        dB = sb("dB", [TP, TB])
        iotaT = sb("iotaT", [TP, TB])
        st = sb("st", [P, 4 * 7 * 6])
        mv = sb("mv", [P, NT, 2])
        rs = sb("rs", [P, NT])
        small = sb("small", [P, 64])
        rows1 = rowsb[0:1, 1:5, :].rearrange("a s (q p) -> a (s q) p", p=P)
        bgr = WA[:, 0].rearrange("p k o -> p (k o)")[:, 1200:1208]
        router = WA[:, 0].rearrange("p k o -> p (k o)")[:, 0:1200].rearrange("p (s e) -> p s e", s=6)
        PS = [ctx.enter_context(nc.psum_tensor(f"ps{i}", [P, 512], F32)) for i in range(8)]

        Kd = [dram(f"Kd{l}", [N, D]) for l in range(2)]
        Qd = [dram(f"Qd{l}", [AGG_B, D]) for l in range(2)]
        Vd = [dram(f"Vd{l}", [N, D]) for l in range(2)]
        aggd = [dram(f"aggd{l}", [AGG_ROWS, D]) for l in range(2)]
        mixd = dram("mixd", [N, D])

        dense = Ring([PS[i] for i in range(4)])
        turn = Ring([PS[4], PS[5]])
        edge = Ring([PS[6], PS[7]])
        stg = Ring([stage[:, i, :] for i in range(4)])
        stg_ch = [chan(f"c_stg{i}") for i in range(4)]

        def load(ch, dst, src, *marks):
            return ch.send(SP, lambda e: e.dma_start(dst, src), *marks)

        z0 = DVE.do(lambda e: e.memset(zero, 0.0))
        on0 = DVE.do(lambda e: e.memset(ones[:, :], 1.0))
        xpad = DVE.do(lambda e: e.memset(Yt[:, NT - 1, :], 0.0))
        m0 = POOL.do(lambda e: e.memset(ident[:, :], 0.0))
        idm = POOL.do(lambda e: e.affine_select(out=ident[:, :], in_=ident[:, :], compare_op=ALU.not_equal, fill=1.0,
                                                base=0, pattern=[[-1, P]], channel_multiplier=1), m0)
        iom = POOL.do(lambda e: e.iota(iota[:, :], pattern=[[1, P]], base=0, channel_multiplier=0,
                                       allow_small_or_imprecise_dtypes=True))
        iotm = POOL.do(lambda e: e.iota(iotaT[:, :], pattern=[[TP, TB]], base=AGG_B, channel_multiplier=1,
                                        allow_small_or_imprecise_dtypes=True))

        xc = [chan(f"c_x{g}") for g in range(5)]
        xld = []
        for g in range(4):
            src = A["x"][0:3072, :].rearrange("(t p) d -> p t d", p=P)[:, 6 * g:6 * g + 6, :]
            xld.append(load(xc[g], Yt[:, 6 * g:6 * g + 6, :], src))
        load(xc[4], Yt[0:48, 24, :], A["x"][3072:3120, :], xpad)
        xld.append(load(xc[4], Yt[48:53, 24, :], A["x"][3120:3125, :], xpad))
        xtile = [xld[min(t // 6, 4)] for t in range(NT)]

        c_pre = [chan(f"c_pre{i}") for i in range(3)]
        pre = Sc[:, 0:6 * 512].rearrange("p (s b e) -> p s b e", s=6, b=TB)
        tm = lambda ap: ap.rearrange("(b p e) -> p b e", b=TB, p=TP)
        ld_d = load(c_pre[0], pre[0:TP, 0].bitcast(I32), tm(A["dst"][1:1 + EP]))
        ld_p = load(c_pre[1], pre[0:TP, 1].bitcast(I32), tm(A["dst"][0:EP]))
        ld_s = load(c_pre[2], pre[0:TP, 2].bitcast(I32), tm(A["src"][0:EP]))

        c_vec, c_wa, c_g, c_row = chan("c_vec"), chan("c_wa"), chan("c_g"), chan("c_row")
        ldv = load(c_vec, vec[:, :], A["vec"])
        kpo = lambda ap: ap.rearrange("(k p) o -> p k o", p=P)

        def load_qkv(l, dst, *marks):
            for i, w in enumerate(("WqT", "WkT", "WvT")):
                m = load(c_wa, dst[:, i], kpo(A[w][l]), *marks)
            return m

        def load_row(i, src, *marks):
            return load(c_row, rowsb[:, i, :], src.partition_broadcast(P), *marks)

        wqkv = load_qkv(0, WA)
        load_row(0, A["gbq"][0])
        for i, b in enumerate(("mbq", "mbk", "mbv", "mbp")):
            rowm = load_row(1 + i, A[b])
        for i, w in enumerate(("MqT", "MkT", "MvT", "MpT")):
            wmix = load(c_g, G[:, 4 * i:4 * i + 4, :], kpo(A[w]))
        c_zero = chan("c_zero")
        for l in range(2):
            load(c_zero, aggd[l][0:3584, :].rearrange("(t p) d -> p t d", p=P),
                 zero.unsqueeze(1).to_broadcast([P, 28, 512]), z0)
            load(c_zero, aggd[l][3584:3616, :], zero[0:32, :], z0)
            zeroed = load(c_zero, Qd[l][N:AGG_B, :], zero[0:AGG_B - N, :], z0)

        def ln_stats(tiles, ready):
            a, b = tiles[0], tiles[-1] + 1
            for t in tiles:
                m = DVE.do(lambda e, t=t: e.bn_stats(out=st[:, 6 * (t % 25):6 * (t % 25) + 6], in_=Yt[:, t, :]), ready(t))
            for t in tiles:
                m2 = DVE.do(lambda e, t=t: e.bn_aggr(out=mv[:, t, :], in_=st[:, 6 * (t % 25):6 * (t % 25) + 6]), m)
            m = DVE.do(lambda e: e.tensor_scalar(rs[:, a:b], mv[:, a:b, 1], EPS, None, ALU.add), m2)
            m = ACTQ.do(lambda e: e.activation(rs[:, a:b], rs[:, a:b], ACT.Sqrt), m)
            return DVE.do(lambda e: e.reciprocal(rs[:, a:b], rs[:, a:b]), m)

        def to_features(t, src, ready, dst_free):
            r = ROWS[t]
            i, bank, free = turn.take()
            for k in range(4):
                f = lambda e, k=k: e.transpose(bank[:, k * P:k * P + r], src[0:r, k * P:(k + 1) * P], ident[0:r, 0:r])
                if k < 3:
                    PE.quiet(f, free, ready, idm)
                else:
                    m = PE.do(f)
            bk = bank[:, :].rearrange("p (k n) -> p k n", k=4)
            turn.free[i] = ACTQ.do(lambda e: e.activation(xT[:, :, P * t:P * t + r], bk[:, :, 0:r], ACT.Copy), m, dst_free)
            return turn.free[i], m

        groups = [list(range(6 * g, min(6 * g + 6, NT))) for g in range(5)]
        xT_ready = [None] * NT
        for tiles in groups:
            m = ln_stats(tiles, lambda t: [xtile[t], xpad])
            for t in tiles:
                mn = DVE.do(lambda e, t=t: e.tensor_scalar(Yt[:, t, :], Yt[:, t, :], mv[:, t, 0:1], rs[:, t:t + 1],
                                                           ALU.subtract, ALU.mult), m)
                xT_ready[t], y_read = to_features(t, Yt[:, t, :], mn, None)

        pf = pre
        d_i, p_i, s_i = pf[0:TP, 0].bitcast(I32), pf[0:TP, 1].bitcast(I32), pf[0:TP, 2].bitcast(I32)
        sm_t, nf_t, or_t, df_t = pf[0:TP, 3], pf[0:TP, 4], pf[0:TP, 5], pf[0:TP, 0]
        w0 = work[0:TP, 0, :].rearrange("p (b e) -> p b e", b=TB)
        w1 = work[0:TP, 1, :].rearrange("p (b e) -> p b e", b=TB)
        m = DVE.do(lambda e: e.tensor_tensor(sm_t, d_i, p_i, ALU.is_equal), ld_d, ld_p)
        m2 = DVE.do(lambda e: e.tensor_copy(w0, d_i))
        DVE.do(lambda e: e.tensor_copy(w1, s_i), ld_s)
        m = DVE.do(lambda e: e.tensor_scalar(nf_t, sm_t, -1.0, 1.0, ALU.mult, ALU.add), m)
        m = DVE.do(lambda e: e.memset(nf_t[:, :, 0], 0.0), m)
        for b in range(TB):
            mo = DVE.do(lambda e, b=b: e.tensor_tensor_scan(or_t[:, b, :], nf_t[:, b, :], nf_t[:, b, :], 0.0,
                                                            ALU.add, ALU.max), m)
        mb = DVE.do(lambda e: e.tensor_copy(dB[:, :], w0[:, :, 0]), m2)
        m = DVE.do(lambda e: e.memset(nf_t[:, :, 0], 1.0), mo)
        m2 = DVE.do(lambda e: e.tensor_copy(df_t, w0), mb)
        c0 = small[0:TP, 0:4]
        m3 = DVE.do(lambda e: e.tensor_tensor(c0, iotaT[:, :], dB[:, :], ALU.subtract), mb, iotm)
        m3 = DVE.do(lambda e: e.tensor_tensor(c0, c0, sm_t[:, :, 0], ALU.mult), m3)
        m3 = DVE.do(lambda e: e.tensor_tensor(df_t[:, :, 0], dB[:, :], c0, ALU.add), m3, m2)
        fv_t = pf[0:TP, 1]
        m3 = DVE.do(lambda e: e.scalar_tensor_tensor(out=fv_t, in0=df_t, scalar=FAR, in1=nf_t,
                                                     op0=ALU.subtract, op1=ALU.mult), m3, m)
        pre_done = []
        for srct, dstt in ((or_t, ordE), (fv_t, fvE), (w1, srcE), (w0, dstE)):
            i, bank, free = turn.take()
            for b in range(TB):
                f = lambda e, b=b, srct=srct, bank=bank: e.transpose(bank[:, b * TP:(b + 1) * TP], srct[:, b, :],
                                                                     ident[0:TP, 0:TP])
                if b < 3:
                    PE.quiet(f, free, m3, idm)
                else:
                    mp = PE.do(f)
            turn.free[i] = ACTQ.do(lambda e, bank=bank, dstt=dstt: e.activation(dstt[:, :], bank[:, 0:ET], ACT.Copy), mp)
            pre_done.append(turn.free[i])
        idx_ready = pre_done[-1]
        pre_read = mp

        def rows_product(t, w, ready, src=None, s0=None):
            r = ROWS[t]
            i, bank, free = dense.take()
            for k in range(4):
                lhs = xT[:, k, P * t:P * t + r] if src is None else src[:, k, s0:s0 + r]
                f = lambda e, k=k, lhs=lhs: e.matmul(bank[0:r, :], lhs, w[:, k, :], start=(k == 0), stop=(k == 3))
                if k < 3:
                    PE.quiet(f, free, ready)
                else:
                    m = PE.do(f)
            return i, bank, m

        def qkv(l, W, wready, xready, rowm, brow):
            bs = DVE.do(lambda e: e.tensor_scalar(rowsb[:, brow, :], rowsb[:, brow, :], 0.125, None, ALU.mult), rowm)
            for t in range(NT):
                r = ROWS[t]
                for w, table in ((0, Qd[l]), (1, Kd[l]), (2, Vd[l])):
                    i, bank, m = rows_product(t, W[:, w], [wready, xready(t)])
                    s, buf, _ = stg.take()
                    gone = stg_ch[s].mark()
                    if w == 0:
                        m = DVE.do(lambda e, bank=bank, buf=buf, r=r: e.scalar_tensor_tensor(
                            out=buf[0:r, :], in0=bank[0:r, :], scalar=0.125, in1=rowsb[0:r, brow, :],
                            op0=ALU.mult, op1=ALU.add), m, gone, bs, stg.free[s])
                    else:
                        m = ACTQ.do(lambda e, bank=bank, buf=buf, r=r: e.activation(buf[0:r, :], bank[0:r, :], ACT.Copy),
                                    m, gone, stg.free[s])
                    dense.free[i] = m
                    stg.free[s] = load(stg_ch[s], table[P * t:P * t + r, :], buf[0:r, :], m)
            return [c.mark() for c in stg_ch], (PE.sem, PE.n)

        kv_ready, x_read = qkv(0, WA, wqkv, lambda t: xT_ready[t], rowm, 0)

        def mix(xready, wready, free_y, free_sc):
            qT = Y[:, 0:4 * N].rearrange("p (k n) -> p k n", k=4)
            mt = Sc[:, 0:6 * 512].rearrange("p (s d) -> p s d", s=6)
            h8 = lambda ap: ap.rearrange("p (h d) -> p h d", h=H)
            Wm = G[:, :, :].rearrange("p (w k) o -> p w k o", w=4)
            ctxb, ksb = PS[6], PS[7]
            used = [free_sc, free_sc]
            pe_used = [None, None]
            for t in range(NT):
                r, b = ROWS[t], 3 * (t % 2)
                bufs = [mt[0:r, b + w, :] for w in range(3)]
                mm = []
                for w in range(3):
                    i, bank, m = rows_product(t, Wm[:, w], [wready, xready(t)])
                    m = DVE.do(lambda e, bw=bufs[w], w=w, bank=bank, r=r: e.tensor_tensor(
                            bw, bank[0:r, :], rowsb[0:r, 1 + w, :], ALU.add), m, used[t % 2], rowm)
                    dense.free[i] = m
                    mm.append(m)
                st8 = [small[0:r, 8 * w:8 * w + 8] for w in range(4)]
                for w in range(2):
                    mm[w] = DVE.do(lambda e, w=w, bw=bufs[w], s=st8[w]: e.tensor_reduce(s, h8(bw), AXX, ALU.max), mm[w])
                for w in range(2):
                    mm[w] = DVE.do(lambda e, w=w, bw=bufs[w], s=st8[w], r=r: e.tensor_tensor(
                        h8(bw), h8(bw), s.unsqueeze(2).to_broadcast([r, H, DH]), ALU.subtract), mm[w])
                for w in range(2):
                    mm[w] = ACTQ.do(lambda e, bw=bufs[w]: e.activation(bw, bw, ACT.Exp), mm[w])
                for w in range(2):
                    mm[w] = DVE.do(lambda e, bw=bufs[w], s=st8[2 + w]: e.tensor_reduce(s, h8(bw), AXX, ALU.add), mm[w])
                for w in range(2):
                    mm[w] = DVE.do(lambda e, s=st8[2 + w]: e.reciprocal(s, s), mm[w])
                for w in range(2):
                    mm[w] = DVE.do(lambda e, bw=bufs[w], s=st8[2 + w], r=r: e.tensor_tensor(
                        h8(bw), h8(bw), s.unsqueeze(2).to_broadcast([r, H, DH]), ALU.mult), mm[w])
                i, bank, free = turn.take()
                for k in range(4):
                    f = lambda e, k=k, bank=bank, bw=bufs[0], r=r: e.transpose(bank[:, k * P:k * P + r],
                                                                               bw[:, k * P:(k + 1) * P], ident[0:r, 0:r])
                    if k < 3:
                        PE.quiet(f, free, mm[0])
                    else:
                        m = PE.do(f)
                bk = bank[:, :].rearrange("p (k n) -> p k n", k=4)
                turn.free[i] = ACTQ.do(lambda e, t=t, r=r, bk=bk: e.activation(qT[:, :, P * t:P * t + r], bk[:, :, 0:r],
                                                                               ACT.Copy), m, free_y)
                q_ready = turn.free[i]
                for p in range(4):
                    PE.quiet(lambda e, p=p, t=t, r=r, bw=bufs: e.matmul(
                        ctxb[:, p * P:(p + 1) * P], bw[1][:, p * P:(p + 1) * P], bw[2][:, p * P:(p + 1) * P],
                        start=(t == 0 and p == 0), stop=(t == NT - 1 and p == 3), skip_group_check=True), mm[1], mm[2])
                for p in range(4):
                    f = lambda e, p=p, t=t, r=r, bw=bufs: e.matmul(
                        ksb[:, p:p + 1], bw[1][:, p * P:(p + 1) * P], ones[0:r, :],
                        start=(t == 0 and p == 0), stop=(t == NT - 1 and p == 3), skip_group_check=True)
                    if p < 3:
                        PE.quiet(f, on0)
                    else:
                        used[t % 2] = PE.do(f)
            ctx_done = used[(NT - 1) % 2]
            ctxBD, ksBD = stage[:, 0, :], stage[:, 1, :]
            gone = [c.mark() for c in stg_ch]
            m = DVE.do(lambda e: e.memset(stage[:, 0:2, :], 0.0), gone)
            for h in range(H):
                a, c = 64 * (h % 2), P * (h // 2) + 64 * (h % 2)
                DVE.do(lambda e, a=a, c=c: e.tensor_copy(ctxBD[a:a + 64, c:c + 64], ctxb[a:a + 64, c:c + 64]), ctx_done, m)
                bd = DVE.do(lambda e, a=a, c=c, h=h: e.tensor_copy(
                    ksBD[a:a + 64, c:c + 64], ksb[a:a + 64, h // 2:h // 2 + 1].to_broadcast([64, 64])))
            edge.free = [bd, bd]
            oc_free = [x_read, x_read]
            tmp = Ring([mt[:, s, :] for s in range(6)])
            tmp.free = [ctx_done] * 6
            mst = Ring([stage[:, 2 + s, :] for s in range(2)])
            for c, (c0, cn) in enumerate(CHUNKS):
                oc = WA[:, c % 2]
                for p in range(4):
                    i1, b1, f1 = dense.take()
                    m1 = PE.do(lambda e, p=p, b1=b1, c0=c0, cn=cn: e.matmul(
                        b1[:, 0:cn], ksBD[:, p * P:(p + 1) * P], qT[:, p, c0:c0 + cn], start=True, stop=True), f1, bd, q_ready)
                    i2, b2, f2 = dense.take()
                    m2 = PE.do(lambda e, p=p, b2=b2, c0=c0, cn=cn: e.matmul(
                        b2[:, 0:cn], ctxBD[:, p * P:(p + 1) * P], qT[:, p, c0:c0 + cn], start=True, stop=True), f2)
                    i3, tb, f3 = tmp.take()
                    m1 = DVE.do(lambda e, tb=tb, b1=b1, cn=cn: e.reciprocal(tb[:, 0:cn], b1[:, 0:cn]), m1, f3)
                    dense.free[i1] = m1
                    m2 = DVE.do(lambda e, tb=tb, b2=b2, cn=cn: e.tensor_tensor(tb[:, 0:cn], b2[:, 0:cn], tb[:, 0:cn],
                                                                               ALU.mult), m1, m2)
                    dense.free[i2] = m2
                    mo = DVE.do(lambda e, p=p, tb=tb, oc=oc, c0=c0, cn=cn: e.tensor_tensor(
                        oc[:, p, 0:cn], tb[:, 0:cn], qT[:, p, c0:c0 + cn], ALU.add), m2, oc_free[c % 2])
                    tmp.free[i3] = mo
                for t in range(4 * c, min(4 * c + 4, NT)):
                    r = ROWS[t]
                    i, bank, m = rows_product(t, Wm[:, 3], [mo, wready], src=oc, s0=P * t - c0)
                    s, buf, _ = mst.take()
                    m2 = DVE.do(lambda e, bank=bank, buf=buf, r=r: e.tensor_tensor(
                        buf[0:r, :], bank[0:r, :], rowsb[0:r, 4, :], ALU.add), m, stg_ch[2 + s].mark())
                    dense.free[i] = m2
                    load(stg_ch[2 + s], mixd[P * t:P * t + r, :], buf[0:r, :], m2)
                oc_free[c % 2] = m
            stg.free = [m, m, m2, m2]
            return m, m2, [stg_ch[2].mark(), stg_ch[3].mark()]

        mix_pe, mix_dve, mix_ready = mix(lambda t: xT_ready[t], wmix, y_read, pre_read)

        dI = Y[:, 0:CH + 2].bitcast(I32)
        c_scan = chan("c_scan")
        for h in range(H):
            src = A["dst"][0:CH + 2]
            src = bass.AP(src.tensor, src.offset, [[CH, NCH], [1, CH + 2]])
            ms = load(c_scan, dI[h * NCH:(h + 1) * NCH, :], src, mix_pe, mix_dve)
        sm_ready = DVE.do(lambda e: e.tensor_tensor(same[:, :], dI[:, 0:CH + 1], dI[:, 1:CH + 2], ALU.is_equal), ms)
        smin = small[:, 32:34]
        DVE.do(lambda e: e.tensor_reduce(smin[:, 0:1], same[:, 0:CH], AXX, ALU.min), sm_ready)
        m = DVE.do(lambda e: e.tensor_reduce(smin[:, 1:2], same[:, 1:CH + 1], AXX, ALU.min))
        hc = lambda row: rows1[0:1, row, :].rearrange("a (h c) -> a h c", h=H)
        mz = DVE.do(lambda e: e.memset(rows1[:, 0:2, :], 0.0), mix_dve)
        mz = DVE.do(lambda e: e.memset(rows1[:, 4:6, :], -BIG))
        mz = DVE.do(lambda e: e.memset(rows1[:, 6:8, :], 0.0))
        for d in range(2):
            i, bank, free = turn.take()
            mp = PE.do(lambda e, d=d, bank=bank: e.transpose(bank[0:1, 0:P], smin[:, d:d + 1], ident[:, :]), free, m)
            bh = bank[0:1, 0:P].rearrange("a (h c) -> a h c", h=H)
            if d == 0:
                m1 = DVE.do(lambda e, bh=bh: e.tensor_copy(hc(0)[:, :, 1:NCH], bh[:, :, 0:NCH - 1]), mp, mz)
            else:
                m1 = DVE.do(lambda e, bh=bh: e.tensor_copy(hc(1)[:, :, 0:NCH - 1], bh[:, :, 1:NCH]), mp, mz)
            turn.free[i] = m1
        links = DVE.do(lambda e: e.tensor_scalar(rows1[:, 2:4, :], rows1[:, 0:2, :], 1.0, BIG, ALU.subtract, ALU.mult), m1)

        SA, SB, SC_ = (Y[:, i * CH:(i + 1) * CH] for i in range(3))
        pen = Y[:, 3 * CH:3 * CH + (CH + 2) // 2].bitcast(BF16)[:, 0:CH + 1]
        Sc3 = Sc[:, :].rearrange("p (j h c) -> p j h c", j=NJ, h=H)
        g_ch = [chan(f"c_g{i}") for i in range(16)]
        g_free = [None] * 16
        sct_ch = [chan(f"c_sct{i}") for i in range(4)]
        order = [c * NJ + j for j in range(NJ) for c in range(NCH)]

        def gather(slot, table, idx, i, *marks):
            return g_ch[slot].send(POOL, lambda e: e.indirect_dma_start(
                out=G[:, slot, :], out_offset=None, in_=table[:, :],
                in_offset=bass.IndirectOffsetOnAxis(ap=idx[:, i:i + 1], axis=0)), *marks)

        def seg_scan(data, res, kind, back, m):
            ops = (ALU.add, ALU.max) if kind == 0 else (ALU.mult, ALU.add)
            init = -BIG if kind == 0 else 0.0
            gate = pen if kind == 0 else same
            if back:
                g, x, o = gate[:, CH:0:-1], data[:, ::-1], res[:, ::-1]
                last = res[:, 0:1]
            else:
                g, x, o = gate[:, 0:CH], data, res
                last = res[:, CH - 1:CH]
            m = DVE.do(lambda e: e.tensor_tensor_scan(o, g, x, init, *ops), m)
            i, bank, free = turn.take()
            mp = PE.do(lambda e: e.transpose(bank[0:1, 0:P], last, ident[:, :]), m, free)
            bh = bank[0:1, 0:P].rearrange("a (h c) -> a h c", h=H)
            hand, link, car = 4 + 2 * kind + back, (2 if kind == 0 else 0) + back, 8 + 2 * kind + back
            if back:
                m = DVE.do(lambda e: e.tensor_copy(hc(hand)[:, :, 0:NCH - 1], bh[:, :, 1:NCH]), mp, links)
                m1 = DVE.do(lambda e: e.tensor_tensor_scan(rows1[:, car, ::-1], rows1[:, link, ::-1],
                                                           rows1[:, hand, ::-1], init, *ops), m)
            else:
                m = DVE.do(lambda e: e.tensor_copy(hc(hand)[:, :, 1:NCH], bh[:, :, 0:NCH - 1]), mp, links)
                m1 = DVE.do(lambda e: e.tensor_tensor_scan(rows1[:, car, :], rows1[:, link, :], rows1[:, hand, :],
                                                           init, *ops), m)
            turn.free[i] = m
            i, bank2, free = turn.take()
            mp = PE.do(lambda e: e.transpose(bank2[:, 0:1], rows1[0:1, car, :], ident[0:1, 0:1]), m1, free)
            cc = small[:, 40 + 2 * kind + back:41 + 2 * kind + back]
            m = DVE.do(lambda e: e.tensor_copy(cc, bank2[:, 0:1]), mp)
            turn.free[i] = m
            return DVE.do(lambda e: e.tensor_tensor_scan(o, g, x, cc, *ops), m)

        wk = Ring([work[:, s, :] for s in range(3)])
        wk.free = [pre_read, pre_read, zeroed]
        oh = Ring([onehot[:, s, :] for s in range(4)])

        def attend(l, tables, g_start, y_start):
            ready = {}

            def fetch(n):
                if n >= ET:
                    return
                s, i = 2 * (n % 8), order[n]
                ready[n] = [gather(s, Kd[l], srcE, i, tables, idx_ready, g_start, g_free[s]),
                            gather(s + 1, Qd[l], dstE, i, g_free[s + 1])]

            for n in range(6):
                fetch(n)
            a_done = None
            for n in range(ET):
                fetch(n + 6)
                s, j, c = 2 * (n % 8), n // NCH, n % NCH
                i, buf, free = wk.take()
                m = DVE.do(lambda e, s=s, buf=buf: e.tensor_tensor(buf, G[:, s, :], G[:, s + 1, :], ALU.mult),
                           ready.pop(n), free)
                g_free[s] = g_free[s + 1] = m
                m = DVE.do(lambda e, j=j, c=c, buf=buf: e.tensor_reduce(
                    Sc3[:, j, :, c], buf.rearrange("p (h d) -> p h d", h=H), AXX, ALU.add), m, mix_pe)
                wk.free[i] = m
                if c == NCH - 1:
                    i, bank, free = turn.take()
                    mp = PE.do(lambda e, j=j, bank=bank: e.transpose(bank[:, 0:P], Sc[:, j * P:(j + 1) * P], ident[:, :]),
                               m, free)
                    a_done = turn.free[i] = ACTQ.do(lambda e, j=j, bank=bank: e.activation(
                        SA[:, j * P:(j + 1) * P], bank[:, 0:P], ACT.Copy), mp, y_start)
            vready = {}

            def fetch_v(n):
                if n < ET:
                    vready[n] = gather(n % 16, Vd[l], srcE, order[n], g_free[n % 16])

            for n in range(14):
                fetch_v(n)
            m = DVE.do(lambda e: e.tensor_scalar(pen, same[:, :], 1.0, BIG, ALU.subtract, ALU.mult), sm_ready, y_start)
            m = seg_scan(SA, SB, 0, 0, [m, a_done])
            m = seg_scan(SB, SC_, 0, 1, m)
            m = DVE.do(lambda e: e.tensor_tensor(SA, SA, SC_, ALU.subtract), m)
            m = ACTQ.do(lambda e: e.activation(SA, SA, ACT.Exp), m)
            m = seg_scan(SA, SB, 1, 0, m)
            m = DVE.do(lambda e: e.scalar_tensor_tensor(out=SB, in0=same[:, 1:CH + 1], scalar=1.0, in1=SB,
                                                        op0=ALU.subtract, op1=ALU.mult), m)
            m = seg_scan(SB, SC_, 1, 1, m)
            m = DVE.do(lambda e: e.tensor_scalar(SC_, SC_, -1.0, 1e-16, ALU.mult, ALU.add), m)
            m = DVE.do(lambda e: e.reciprocal(SC_, SC_), m)
            w_ready = DVE.do(lambda e: e.tensor_tensor(SA, SA, SC_, ALU.mult), m)
            last_scatter = [None] * 4
            pend = []
            for n in range(ET):
                j, c, e_i, s = n // NCH, n % NCH, order[n], n % 16
                if c == 0:
                    i, bank, free = turn.take()
                    mp = PE.do(lambda e, j=j, bank=bank: e.transpose(bank[:, 0:P], SA[:, j * P:(j + 1) * P], ident[:, :]),
                               w_ready, free)
                    turn.free[i] = wt = ACTQ.do(lambda e, j=j, bank=bank: e.activation(
                        Sc[:, j * P:(j + 1) * P], bank[:, 0:P], ACT.Copy), mp)
                    y_done = mp
                i, buf, free = wk.take()
                mw = DVE.do(lambda e, s=s, j=j, c=c, buf=buf: e.tensor_tensor(
                    buf.rearrange("p (h d) -> p h d", h=H), G[:, s, :].rearrange("p (h d) -> p h d", h=H),
                    Sc3[:, j, :, c:c + 1].to_broadcast([P, H, DH]), ALU.mult), vready.pop(n), free, wt)
                g_free[s] = mw
                io, ohb, ofree = oh.take()
                mo = DVE.do(lambda e, e_i=e_i, ohb=ohb: e.tensor_scalar(ohb, iota[:, :], ordE[:, e_i:e_i + 1], None,
                                                                        ALU.is_equal), ofree, iom, pre_done[0])
                ib, bank, free = edge.take()
                mp = PE.do(lambda e, ohb=ohb, buf=buf, bank=bank: e.matmul(bank[:, :], ohb, buf, start=True, stop=True),
                           mw, mo, free)
                wk.free[i] = oh.free[io] = mp
                if l == 0:
                    it, tb, free = turn.take()
                    mp2 = PE.do(lambda e, ohb=ohb, tb=tb, e_i=e_i: e.matmul(tb[:, 0:1], ohb, fvE[:, e_i:e_i + 1],
                                                                           start=True, stop=True), free, pre_done[1])
                    oh.free[io] = mp2
                    turn.free[it] = mseg = ACTQ.do(lambda e, tb=tb, e_i=e_i: e.activation(
                        segE[:, e_i:e_i + 1], tb[:, 0:1], ACT.Copy, bias=FAR), mp2)
                    seg_marks[e_i] = mseg
                k, sbuf, sfree = stg.take()
                me = ACTQ.do(lambda e, sbuf=sbuf, bank=bank: e.activation(sbuf, bank[:, :], ACT.Copy), mp, stg_ch[k].mark(),
                             sfree)
                edge.free[ib] = me
                fetch_v(n + 14)
                pend.append((k, sbuf, e_i, me))
                if len(pend) > 2 or n == ET - 1:
                    while pend and (len(pend) > 2 or n == ET - 1):
                        k, sbuf, e_i, me = pend.pop(0)
                        stg.free[k] = sct_ch[k].send(POOL, lambda e, sbuf=sbuf, e_i=e_i: e.indirect_dma_start(
                            out=aggd[l][:, :], out_offset=bass.IndirectOffsetOnAxis(ap=segE[:, e_i:e_i + 1], axis=0),
                            in_=sbuf, in_offset=None, bounds_check=AGG_ROWS - 1, oob_is_err=False),
                            me, seg_marks[e_i], zeroed)
            return [c.mark() for c in sct_ch], y_done, mp

        st4 = st[:, :].rearrange("p (f c s) -> p f c s", f=4, c=7)

        def norm_coeffs(l, cg, cb, m):
            for f in range(4):
                m2 = DVE.do(lambda e, f=f: e.bn_aggr(out=mv[:, f, :], in_=st4[:, f, :, :]), m)
            sc, off = small[:, 0:4], small[:, 4:8]
            m = DVE.do(lambda e: e.tensor_scalar(sc, mv[:, 0:4, 1], EPS, None, ALU.add), m2)
            m = ACTQ.do(lambda e: e.activation(sc, sc, ACT.Sqrt), m)
            m = DVE.do(lambda e: e.reciprocal(sc, sc), m)
            m = DVE.do(lambda e: e.tensor_tensor(sc, sc, vec[:, cg + 4 * l:cg + 4 * l + 4], ALU.mult), m, ldv)
            m = DVE.do(lambda e: e.tensor_tensor(off, mv[:, 0:4, 0], sc, ALU.mult), m)
            return DVE.do(lambda e: e.tensor_tensor(off, vec[:, cb + 4 * l:cb + 4 * l + 4], off, ALU.subtract), m)

        def normalise(c, m):
            c0, cn = CHUNKS[c]
            for f in range(4):
                m2 = DVE.do(lambda e, f=f: e.tensor_scalar(xT[:, f, c0:c0 + cn], xT[:, f, c0:c0 + cn], small[:, f:f + 1],
                                                           small[:, 4 + f:5 + f], ALU.mult, ALU.add), m)
            return m2

        c_agg = [chan(f"c_agg{i}") for i in range(5)]

        def finish_layer(l, agg_ready, pv_done, x_free, Wo, W1, W2, wready):
            aggT = [G[:, 0:4, :], G[:, 4:8, :]]
            Bt = G[0:TP, 8:12, :]
            rows = Ring([G[:, 12 + s, :] for s in range(4)])
            bm = load(c_agg[4], Bt, aggd[l][AGG_B:AGG_ROWS, :].rearrange("(b p) d -> p b d", p=TP), agg_ready, pv_done)
            t_free = [None, None]
            got = {}

            def fetch(t):
                if t < NT:
                    s, buf, free = rows.take()
                    got[t] = (s, buf, load(c_agg[s], buf[0:ROWS[t], :], aggd[l][P * t:P * t + ROWS[t], :],
                                           agg_ready, pv_done, free))

            for t in range(3):
                fetch(t)
            for c, (c0, cn) in enumerate(CHUNKS):
                dst = aggT[c % 2]
                for t in range(4 * c, min(4 * c + 4, NT)):
                    fetch(t + 3)
                    r = ROWS[t]
                    s, row, ml = got.pop(t)
                    hot = []
                    for b in range(TB):
                        io, ohb, ofree = oh.take()
                        mo = DVE.do(lambda e, b=b, ohb=ohb, t=t: e.tensor_scalar(
                            ohb[0:TP, :], iota[0:TP, :], float(P * t), dB[:, b:b + 1], ALU.add, ALU.is_equal), ofree)
                        hot.append((io, ohb))
                    it, bank, free = turn.take()
                    for f in range(4):
                        PE.quiet(lambda e, f=f, bank=bank, row=row, r=r: e.matmul(
                            bank[:, f * P:f * P + r], row[0:r, f * P:(f + 1) * P], ident[0:r, 0:r], start=True, stop=False),
                            free, ml, bm)
                        for b in range(TB):
                            g = lambda e, f=f, b=b, bank=bank, ohb=hot[b][1], r=r: e.matmul(
                                bank[:, f * P:f * P + r], Bt[:, b, f * P:(f + 1) * P], ohb[0:TP, 0:r],
                                start=False, stop=(b == TB - 1))
                            if f == 3 and b == TB - 1:
                                mp = PE.do(g)
                            else:
                                PE.quiet(g, mo)
                    for io, _ in hot:
                        oh.free[io] = mp
                    rows.free[s] = mp
                    o0 = P * t - c0
                    bk = bank[:, :].rearrange("p (k n) -> p k n", k=4)
                    turn.free[it] = mt = ACTQ.do(lambda e, bk=bk, dst=dst, o0=o0, r=r: e.activation(
                        dst[:, :, o0:o0 + r], bk[:, :, 0:r], ACT.Copy), mp, t_free[c % 2])
                for f in range(4):
                    i, bank, free = dense.take()
                    for k in range(4):
                        g = lambda e, k=k, f=f, bank=bank, dst=dst, cn=cn: e.matmul(
                            bank[:, 0:cn], Wo[:, k, f * P:(f + 1) * P], dst[:, k, 0:cn], start=(k == 0), stop=(k == 3))
                        if k < 3:
                            PE.quiet(g, free, mt, wready)
                        else:
                            mp = PE.do(g)
                    m = DVE.do(lambda e, f=f, bank=bank, c0=c0, cn=cn: e.scalar_tensor_tensor(
                        out=xT[:, f, c0:c0 + cn], in0=bank[:, 0:cn], scalar=vec[:, C_BO + 4 * l + f:C_BO + 4 * l + f + 1],
                        in1=xT[:, f, c0:c0 + cn], op0=ALU.add, op1=ALU.add), mp, x_free, ldv)
                    dense.free[i] = m
                    m = DVE.do(lambda e, f=f, c=c, c0=c0, cn=cn: e.bn_stats(out=st4[:, f, c, :], in_=xT[:, f, c0:c0 + cn]), m)
                t_free[c % 2] = mp
            co = norm_coeffs(l, C_G1, C_E1, m)
            g_done = mp
            nx = {0: normalise(0, co)}
            for c, (c0, cn) in enumerate(CHUNKS):
                if c + 1 < len(CHUNKS):
                    nx[c + 1] = normalise(c + 1, co)
                i, bank, free = dense.take()
                for k in range(4):
                    g = lambda e, k=k, bank=bank, c0=c0, cn=cn: e.matmul(
                        bank[:, 0:cn], W1[:, k, :], xT[:, k, c0:c0 + cn], start=(k == 0), stop=(k == 3))
                    if k < 3:
                        PE.quiet(g, free, nx[c])
                    else:
                        mp = PE.do(g)
                iw, hb, hfree = wk.take()
                mh = ACTQ.do(lambda e, bank=bank, hb=hb, cn=cn: e.activation(
                    hb[:, 0:cn], bank[:, 0:cn], ACT.Relu, bias=vec[:, C_B1 + l:C_B1 + l + 1]), mp, hfree)
                dense.free[i] = mh
                for f in range(4):
                    i, bank, free = dense.take()
                    mp = PE.do(lambda e, f=f, bank=bank, hb=hb, cn=cn: e.matmul(
                        bank[:, 0:cn], W2[:, f * P:(f + 1) * P], hb[:, 0:cn], start=True, stop=True), free, mh)
                    m = DVE.do(lambda e, f=f, bank=bank, c0=c0, cn=cn: e.scalar_tensor_tensor(
                        out=xT[:, f, c0:c0 + cn], in0=bank[:, 0:cn], scalar=vec[:, C_B2 + 4 * l + f:C_B2 + 4 * l + f + 1],
                        in1=xT[:, f, c0:c0 + cn], op0=ALU.add, op1=ALU.add), mp)
                    dense.free[i] = m
                    m = DVE.do(lambda e, f=f, c=c, c0=c0, cn=cn: e.bn_stats(out=st4[:, f, c, :], in_=xT[:, f, c0:c0 + cn]), m)
                wk.free[iw] = mp
            co = norm_coeffs(l, C_G2, C_E2, m)
            marks = [normalise(c, co) for c in range(len(CHUNKS))]
            return (lambda t: marks[t // 4]), g_done

        def load_layer(l, m):
            load(c_wa, WA[:, 0], kpo(A["WoT"][l]), m)
            load(c_wa, WA[:, 1].rearrange("p k (a o) -> p (k a) o", o=P)[:, 0:4, :], kpo(A["W1T"][l]), m)
            mk = load(c_wa, WA[:, 2, 0, :], A["W2T"][l], m)
            return WA[:, 0], WA[:, 1].rearrange("p k (a o) -> p (k a) o", o=P)[:, 0:4, :], WA[:, 2, 0, :], mk

        seg_marks = {}
        Wl = load_layer(0, mix_pe)
        agg_ready, y_done, pv = attend(0, kv_ready + [zeroed], mix_pe, [sm_ready, mix_pe, mix_dve])
        Y3 = Y[:, 0:3 * 2048].rearrange("p (w k o) -> p w k o", w=3, k=4)
        wqkv1 = load_qkv(1, Y3, y_done)
        row1 = load_row(0, A["gbq"][1], (DVE.sem, DVE.n))
        x_ready, _ = finish_layer(0, agg_ready, pv, [x_read, mix_pe], *Wl)
        kv_ready, x_read1 = qkv(1, Y3, wqkv1, x_ready, row1, 0)
        Wl = load_layer(1, x_read1)
        agg_ready, y_done, pv = attend(1, kv_ready + [zeroed], (PE.sem, PE.n), x_read1)
        for i in range(8):
            g_free[i] = None
        x_ready, g_done = finish_layer(1, agg_ready, pv, x_read1, *Wl)

        rl = [load_row(1, A["ln_g"], mix_dve), load_row(2, A["ln_b"], mix_dve)]
        Wm1 = G[:, 0:8, :].rearrange("p a b -> p (a b)").rearrange("p (k e f) -> p k e f", k=4, e=8)
        Wm2 = G[:, 8:16, :]
        for k in range(4):
            load(c_g, Wm1[:, k], A["EW1"][:, k * P:(k + 1) * P, :].rearrange("e p f -> p e f"), g_done)
        wmoe = load(c_g, Wm2, A["EW2"].rearrange("e f o -> f e o"), g_done)
        c_moe = chan("c_moe")
        wg = router[:, 0, 0:32].rearrange("p (k e) -> p k e", k=4)
        load(c_moe, wg, A["Wg"].rearrange("(k p) e -> p k e", p=P), g_done)
        load(c_moe, bgr, A["bg"].partition_broadcast(P), g_done)
        b2row = work[0:8, 0, :]
        rmoe = load(c_moe, b2row, A["Eb2"], (PE.sem, PE.n))

        tail = DVE.do(lambda e: e.memset(Yt[:, NT - 1, :], 0.0), x_read1, y_done)
        ymark = []
        for t in range(NT):
            r = ROWS[t]
            i, bank, free = turn.take()
            for k in range(4):
                f = lambda e, k=k, t=t, r=r, bank=bank: e.transpose(bank[0:r, k * P:(k + 1) * P], xT[:, k, P * t:P * t + r],
                                                                    ident[:, :])
                if k < 3:
                    PE.quiet(f, free, x_ready(t))
                else:
                    mp = PE.do(f)
            turn.free[i] = ACTQ.do(lambda e, t=t, r=r, bank=bank: e.activation(Yt[0:r, t, :], bank[0:r, :], ACT.Copy),
                                   mp, tail, y_done)
            ymark.append(turn.free[i])
        xT_free = mp
        xin = Ring([stage[:, s, :] for s in range(2)])
        min_ = Ring([stage[:, 2 + s, :] for s in range(2)])
        got = {}

        def fetch_res(t):
            if t < NT:
                r = ROWS[t]
                a, xb, xf = xin.take()
                b, mb_, mf = min_.take()
                got[t] = (a, xb, b, mb_, load(stg_ch[a], xb[0:r, :], A["x"][P * t:P * t + r, :], xf, agg_ready),
                          load(stg_ch[2 + b], mb_[0:r, :], mixd[P * t:P * t + r, :], mf, mix_ready, agg_ready))

        fetch_res(0)
        fetch_res(1)
        x2 = [None] * NT
        for tiles in groups:
            m = ln_stats(tiles, lambda t: ymark[t])
            for t in tiles:
                r = ROWS[t]
                a, xb, b, mb_, la, lb = got.pop(t)
                m1 = POOL.do(lambda e, xb=xb, mb_=mb_, r=r: e.tensor_tensor(xb[0:r, :], xb[0:r, :], mb_[0:r, :], ALU.add),
                             la, lb)
                min_.free[b] = m1
                m1 = POOL.do(lambda e, xb=xb, r=r: e.tensor_tensor(xb[0:r, :], xb[0:r, :], rowsb[0:r, 2, :], ALU.add), m1, rl)
                m2 = DVE.do(lambda e, t=t, r=r: e.scalar_tensor_tensor(
                    out=Yt[0:r, t, :], in0=Yt[0:r, t, :], scalar=mv[0:r, t, 0:1], in1=rowsb[0:r, 1, :],
                    op0=ALU.subtract, op1=ALU.mult), m, rl)
                x2[t] = DVE.do(lambda e, t=t, r=r, xb=xb: e.scalar_tensor_tensor(
                    out=Yt[0:r, t, :], in0=Yt[0:r, t, :], scalar=rs[0:r, t:t + 1], in1=xb[0:r, :],
                    op0=ALU.mult, op1=ALU.add), m2, m1)
                xin.free[a] = x2[t]
                fetch_res(t + 2)
        wk.free = [(PE.sem, PE.n)] * 3
        fx = Ring([work[:, 1 + s, :] for s in range(2)])
        fx.free = [(PE.sem, PE.n)] * 2
        xf_ready = [None] * NT
        for tiles in groups:
            m = ln_stats(tiles, lambda t: x2[t])
            for t in tiles:
                i, buf, free = fx.take()
                mn = DVE.do(lambda e, t=t, buf=buf: e.tensor_scalar(buf, Yt[:, t, :], mv[:, t, 0:1], rs[:, t:t + 1],
                                                                    ALU.subtract, ALU.mult), m, free)
                xf_ready[t], fx.free[i] = to_features(t, buf, mn, xT_free)

        lgb = PS[6]
        mz = DVE.do(lambda e: e.memset(lgb[:, 0:200], 0.0), edge.free)
        for t in range(NT):
            r = ROWS[t]
            for k in range(4):
                f = lambda e, k=k, t=t, r=r: e.matmul(lgb[0:r, 8 * t:8 * t + 8], xT[:, k, P * t:P * t + r], wg[:, k, :],
                                                      start=(k == 0), stop=(k == 3))
                if k < 3:
                    PE.quiet(f, xf_ready[t], rmoe, mz)
                else:
                    mp = PE.do(f)
        pr, ta, tb_, tc, comb = (router[:, 1 + s, :].rearrange("p (t e) -> p t e", t=NT) for s in range(5))
        one = small[:, 0:NT]
        wide = lambda: one.unsqueeze(2).to_broadcast([P, NT, 8])
        lg3 = lgb[:, 0:200].rearrange("p (t e) -> p t e", t=NT)

        def tt(o, a, b, op, *marks):
            return DVE.do(lambda e: e.tensor_tensor(o, a, b, op), *marks)

        def red(a, op, *marks):
            return DVE.do(lambda e: e.tensor_reduce(one, a, AXX, op), *marks)

        m = tt(pr, lg3, bgr.unsqueeze(1).to_broadcast([P, NT, 8]), ALU.add, mp)
        m = red(pr, ALU.max, m)
        m = tt(pr, pr, wide(), ALU.subtract, m)
        m = ACTQ.do(lambda e: e.activation(pr, pr, ACT.Exp), m)
        m = red(pr, ALU.add, m)
        m = DVE.do(lambda e: e.reciprocal(one, one), m)
        m = tt(pr, pr, wide(), ALU.mult, m)
        kx = POOL.do(lambda e: e.iota(tc, pattern=[[0, NT], [-1, 8]], base=8, channel_multiplier=0,
                                      allow_small_or_imprecise_dtypes=True))
        m = DVE.do(lambda e: e.tensor_copy(ta, pr), m)
        for turn_no in range(2):
            m = red(ta, ALU.max, m)
            m = tt(tb_, ta, wide(), ALU.is_equal, m)
            m = tt(tb_, tb_, tc, ALU.mult, m, kx)
            m = red(tb_, ALU.max, m)
            m = tt(tb_, tc, wide(), ALU.is_equal, m)
            if turn_no == 0:
                m = DVE.do(lambda e: e.tensor_copy(comb, tb_), m)
                m = DVE.do(lambda e: e.scalar_tensor_tensor(out=ta, in0=tb_, scalar=-4.0, in1=ta, op0=ALU.mult, op1=ALU.add), m)
        m = tt(comb, comb, tb_, ALU.add, m)
        cm = tt(comb, comb, pr, ALU.mult, m)

        cT = Sc[0:8, 0:N]
        for t in range(NT):
            r = ROWS[t]
            i, bank, free = turn.take()
            mp = PE.do(lambda e, t=t, r=r, bank=bank: e.transpose(bank[0:8, 0:r], comb[0:r, t, :], ident[0:r, 0:r]), free, cm)
            turn.free[i] = mc = ACTQ.do(lambda e, t=t, r=r, bank=bank: e.activation(cT[:, P * t:P * t + r], bank[0:8, 0:r],
                                                                                    ACT.Copy), mp, pv)
        hid = Ring([WA[:, 2, s, :] for s in range(4)])
        hid.free = [(PE.sem, PE.n)] * 4
        c_out = [chan(f"c_out{i}") for i in range(4)]
        acc = list(x2)
        for c, (c0, cn) in enumerate(CHUNKS):
            tiles = range(4 * c, min(4 * c + 4, NT))
            for t in tiles:
                r = ROWS[t]
                i, bank, free = dense.take()
                mp = PE.do(lambda e, t=t, r=r, bank=bank: e.matmul(bank[0:r, :], cT[:, P * t:P * t + r], b2row,
                                                                   start=True, stop=True), free, mc, rmoe)
                acc[t] = dense.free[i] = DVE.do(lambda e, t=t, r=r, bank=bank: e.tensor_tensor(
                    Yt[0:r, t, :], bank[0:r, :], Yt[0:r, t, :], ALU.add), mp, acc[t])
            for x in range(8):
                i, bank, free = dense.take()
                for k in range(4):
                    f = lambda e, k=k, x=x, bank=bank, c0=c0, cn=cn: e.matmul(
                        bank[:, 0:cn], Wm1[:, k, x, :], xT[:, k, c0:c0 + cn], start=(k == 0), stop=(k == 3))
                    if k < 3:
                        PE.quiet(f, free, wmoe, [xf_ready[t] for t in tiles])
                    else:
                        mp = PE.do(f)
                ih, hb, hfree = hid.take()
                mh = dense.free[i] = ACTQ.do(lambda e, x=x, bank=bank, hb=hb, cn=cn: e.activation(
                    hb[:, 0:cn], bank[:, 0:cn], ACT.Gelu_apprx_tanh, bias=vec[:, C_MB1 + x:C_MB1 + x + 1]), mp, hfree)
                for t in tiles:
                    r, o0 = ROWS[t], P * t - c0
                    i, bank, free = dense.take()
                    mp = PE.do(lambda e, x=x, r=r, o0=o0, bank=bank, hb=hb: e.matmul(
                        bank[0:r, :], hb[:, o0:o0 + r], Wm2[:, x, :], start=True, stop=True), free, mh)
                    acc[t] = dense.free[i] = DVE.do(lambda e, t=t, x=x, r=r, bank=bank: e.scalar_tensor_tensor(
                        out=Yt[0:r, t, :], in0=bank[0:r, :], scalar=comb[0:r, t, x:x + 1], in1=Yt[0:r, t, :],
                        op0=ALU.mult, op1=ALU.add), mp, acc[t])
                hid.free[ih] = mp
            for t in tiles:
                r = ROWS[t]
                load(c_out[t % 4], out[P * t:P * t + r, :], Yt[0:r, t, :], acc[t])
        SP.wait(*[c.mark() for c in c_out])
        SP.wait(*[c.mark() for c in stg_ch])


def kernel(**inputs):
    import numpy as np
    import concourse.bacc as bacc
    from concourse.bass_utils import run_bass_kernel_spmd

    a = {k: np.asarray(v) for k, v in inputs.items()}
    t = lambda w: np.ascontiguousarray(np.swapaxes(w, -1, -2))
    cols = lambda v: np.concatenate([x.reshape(4, P).T for x in v], axis=1)
    it = a["dst"].dtype
    arrays = {
        "x": a["x"],
        "src": np.concatenate([a["src"], np.zeros(EP - NE, a["src"].dtype)]),
        "dst": np.concatenate([np.full(1, -1, it), a["dst"], np.full(EP - NE, N, it), np.full(1, N + 1, it)]),
        "WqT": t(a["L0_gnn_Wq"]), "WkT": t(a["L0_gnn_Wk"]), "WvT": t(a["L0_gnn_Wv"]), "WoT": t(a["L0_gnn_Wo"]),
        "W1T": t(a["L0_gnn_W1"]), "W2T": t(a["L0_gnn_W2"]), "gbq": a["L0_gnn_bq"],
        "MqT": t(a["L0_mix_Wq"]), "MkT": t(a["L0_mix_Wk"]), "MvT": t(a["L0_mix_Wv"]), "MpT": t(a["L0_mix_Wp"]),
        "mbq": a["L0_mix_bq"], "mbk": a["L0_mix_bk"], "mbv": a["L0_mix_bv"], "mbp": a["L0_mix_bp"],
        "ln_g": a["L0_gnn_ln_g"], "ln_b": a["L0_gnn_ln_b"],
        "Wg": a["L0_ffn_Wg"], "bg": a["L0_ffn_bg"], "EW1": a["L0_ffn_W1"], "EW2": a["L0_ffn_W2"], "Eb2": a["L0_ffn_b2"],
        "vec": np.concatenate([cols(a["L0_gnn_" + n]) for n in ("bo", "b2", "g1", "beta1", "g2", "beta2")]
                              + [a["L0_gnn_b1"].T, a["L0_ffn_b1"].T], axis=1),
    }
    nc = bacc.Bacc("TRN2", target_bir_lowering=False, num_devices=1)
    feed, A = {}, {}
    for name, v in arrays.items():
        v = np.ascontiguousarray(v)
        feed["in_" + name] = v
        A[name] = nc.dram_tensor("in_" + name, v.shape, mybir.dt.from_np(v.dtype), kind="ExternalInput").ap()
    out = nc.dram_tensor("out", (N, D), F32, kind="ExternalOutput").ap()
    build(nc, A, out)
    r = run_bass_kernel_spmd(nc, [feed], core_ids=[0])
    return r.results[0]["out"]
```

```python
from contextlib import ExitStack

import concourse.bass as bass
from concourse import mybir

P = 128
N, D, H, DH = 3125, 512, 8, 64
NT = 25
ROWS = [min(P, N - P * t) for t in range(NT)]
CHUNKS = [(c, min(512, N - c)) for c in range(0, N, 512)]
NE = 53125
ET = 416
EP = ET * P
NCH = 8
NJ = ET // NCH
CH = NJ * P
SEQ = 2 * NJ
HC = H * NCH
TB, TP = 4, 104
AGG_F = 3200
AGG_L = AGG_F + ET
AGG_ROWS = AGG_L + ET
KV, LAG, AHEAD = 14, 10, 3
FAR = 8192.0
BIG = 1.0e30
EPS = 1e-5

F32 = mybir.dt.float32
I32 = mybir.dt.int32
U32 = mybir.dt.uint32
ALU = mybir.AluOpType
ACT = mybir.ActivationFunctionType
AXX = mybir.AxisListType.X

C_BO, C_B2, C_G1, C_E1, C_G2, C_E2, C_B1, C_MB1 = 0, 8, 16, 24, 32, 40, 48, 50


class Queue:

    def __init__(self, engine, sem):
        self.engine, self.sem, self.n, self.seen = engine, sem, 0, {}

    def wait(self, *marks):
        for m in marks:
            if m is None:
                continue
            if isinstance(m, list):
                self.wait(*m)
                continue
            sem, v = m
            if self.seen.get(id(sem), 0) < v:
                self.seen[id(sem)] = v
                self.engine.wait_ge(sem, v)

    def do(self, f, *marks):
        self.wait(*marks)
        self.n += 1
        f(self.engine).then_inc(self.sem, 1)
        return (self.sem, self.n)

    def quiet(self, f, *marks):
        self.wait(*marks)
        f(self.engine)


class Chan:

    def __init__(self, sem):
        self.sem, self.n = sem, 0

    def mark(self):
        return (self.sem, self.n) if self.n else None

    def send(self, queue, f, *marks):
        queue.wait(*marks)
        self.n += 16
        f(queue.engine).then_inc(self.sem, 16)
        return (self.sem, self.n)


class Ring:

    def __init__(self, bufs):
        self.bufs, self.free, self.at = bufs, [None] * len(bufs), 0

    def take(self):
        i = self.at % len(self.bufs)
        self.at += 1
        return i, self.bufs[i], self.free[i]


def build(nc, A, out):
    with ExitStack() as ctx:
        def sb(name, shape, dt=F32):
            return ctx.enter_context(nc.sbuf_tensor(name, shape, dt))

        def sem(name):
            return ctx.enter_context(nc.semaphore(name))

        def chan(name):
            return Chan(sem(name))

        def dram(name, shape):
            return nc.dram_tensor(name, shape, F32, kind="Internal").ap()

        PE, DVE, ACTQ, POOL, SP = (
            Queue(e, sem(n)) for e, n in ((nc.tensor, "s_pe"), (nc.vector, "s_dve"), (nc.scalar, "s_act"),
                                          (nc.gpsimd, "s_pool"), (nc.sync, "s_sp")))

        xT = sb("xT", [P, 4, N])
        Y = sb("Y", [P, 12800])
        Yt = Y[:, :].rearrange("p (t d) -> p t d", t=NT)
        WA = sb("WA", [P, 3, 4, 512])
        G = sb("G", [P, 16, 512])
        mt = sb("mt", [P, 3072])
        stage = sb("stage", [P, 4, 512])
        work = sb("work", [P, 3, 512])
        rowsb = sb("rowsb", [P, 4, 512])
        ordE = sb("ordE", [P, ET])
        fvE = sb("fvE", [P, ET])
        nfE = sb("nfE", [P, ET])
        srcE = sb("srcE", [P, ET], U32)
        dstE = sb("dstE", [P, ET], U32)
        segE = sb("segE", [P, ET], U32)
        ident = sb("ident", [P, P])
        iota = sb("iota", [P, P])
        onehot = sb("onehot", [P, 3, P])
        zero = work[:, 2, :]
        ones = sb("ones", [P, 1])
        vec = sb("vec", [P, 58])
        bnd = sb("bnd", [TP, 7, TB])
        runrow = sb("runrow", [TP, TB], U32)
        dnx = sb("dnx", [TP, TB, 2], I32)
        scores = sb("scores", [P, 3, HC])
        firsts = sb("firsts", [P, HC])
        pen = sb("pen", [HC, P + 1])
        same = sb("same", [HC, P + 1])
        fixm = sb("fixm", [HC, NJ, 2])
        fixl = sb("fixl", [HC, NJ, 2])
        link = sb("link", [HC, SEQ + 1])
        linkp = sb("linkp", [HC, SEQ + 1])
        maskC = sb("maskC", [HC, NCH])
        selH = sb("selH", [HC, H])
        iotaT = sb("iotaT", [TP, TB])
        st = sb("st", [P, 4 * 7 * 6])
        mv = sb("mv", [P, NT, 2])
        rs = sb("rs", [P, NT])
        small = sb("small", [P, 64])
        rows1 = rowsb[0:1, 1:3, :].rearrange("a s (q p) -> a (s q) p", p=HC)
        sA, sB, sC = (Y[0:HC, 12288 + P * i:12288 + P * (i + 1)] for i in range(3))
        wts = Y[:, 12672:12800].rearrange("p (s q) -> p s q", s=2)
        kvs = [Y[:, 1024 * i:1024 * (i + 1)] for i in range(12)] + [
            G[:, 6 + 2 * i:8 + 2 * i, :].rearrange("p a b -> p (a b)") for i in range(2)]
        bgr = WA[:, 0].rearrange("p k o -> p (k o)")[:, 1200:1208]
        router = WA[:, 0].rearrange("p k o -> p (k o)")[:, 0:1200].rearrange("p (s e) -> p s e", s=6)
        PS = [ctx.enter_context(nc.psum_tensor(f"ps{i}", [P, 512], F32)) for i in range(8)]

        KVd = [dram(f"KVd{l}", [N, 2 * D]) for l in range(2)]
        Qd = [dram(f"Qd{l}", [AGG_F, D]) for l in range(2)]
        aggd = [dram(f"aggd{l}", [AGG_ROWS, D]) for l in range(2)]
        mixd = dram("mixd", [N, D])

        dense = Ring([PS[i] for i in range(4)])
        turn = Ring([PS[4], PS[5]])
        edge = Ring([PS[6], PS[7]])
        stg = Ring([stage[:, i, :] for i in range(4)])
        stg_ch = [chan(f"c_stg{i}") for i in range(4)]

        def load(ch, dst, src, *marks):
            return ch.send(SP, lambda e: e.dma_start(dst, src), *marks)

        z0 = DVE.do(lambda e: e.memset(zero, 0.0))
        on0 = DVE.do(lambda e: e.memset(ones[:, :], 1.0))
        xpad = DVE.do(lambda e: e.memset(Yt[:, NT - 1, :], 0.0))
        m0 = POOL.do(lambda e: e.memset(ident[:, :], 0.0))
        idm = POOL.do(lambda e: e.affine_select(out=ident[:, :], in_=ident[:, :], compare_op=ALU.not_equal, fill=1.0,
                                                base=0, pattern=[[-1, P]], channel_multiplier=1), m0)
        iom = POOL.do(lambda e: e.iota(iota[:, :], pattern=[[1, P]], base=0, channel_multiplier=0,
                                       allow_small_or_imprecise_dtypes=True))
        iotm = POOL.do(lambda e: e.iota(iotaT[:, :], pattern=[[TP, TB]], base=AGG_F, channel_multiplier=1,
                                        allow_small_or_imprecise_dtypes=True))

        xc = [chan(f"c_x{g}") for g in range(5)]
        xld = []
        for g in range(4):
            src = A["x"][0:3072, :].rearrange("(t p) d -> p t d", p=P)[:, 6 * g:6 * g + 6, :]
            xld.append(load(xc[g], Yt[:, 6 * g:6 * g + 6, :], src))
        load(xc[4], Yt[0:48, 24, :], A["x"][3072:3120, :], xpad)
        xld.append(load(xc[4], Yt[48:53, 24, :], A["x"][3120:3125, :], xpad))
        xtile = [xld[min(t // 6, 4)] for t in range(NT)]

        c_pre = [chan(f"c_pre{i}") for i in range(3)]
        pre = mt[:, :].rearrange("p (s b e) -> p s b e", s=6, b=TB)
        tm = lambda ap: ap.rearrange("(b p e) -> p b e", b=TB, p=TP)
        ld_d = load(c_pre[0], pre[0:TP, 0].bitcast(I32), tm(A["dst"][1:1 + EP]))
        ld_p = load(c_pre[1], pre[0:TP, 1].bitcast(I32), tm(A["dst"][0:EP]))
        ld_s = load(c_pre[2], pre[0:TP, 2].bitcast(I32), tm(A["src"][0:EP]))
        c_nx = chan("c_nx")
        nxt = A["dst"][P:P + 2]
        ld_n = load(c_nx, dnx[:, :, :], bass.AP(nxt.tensor, nxt.offset, [[P, TP], [P * TP, TB], [1, 2]]))
        dI = G[:, 0:16, :].rearrange("p a b -> p (a b)").bitcast(I32)
        c_scan = chan("c_scan")
        for h in range(H):
            src = A["dst"][0:CH + 2]
            src = bass.AP(src.tensor, src.offset, [[CH, NCH], [1, CH + 2]])
            ld_q = load(c_scan, dI[h * NCH:(h + 1) * NCH, 0:CH + 2], src)

        c_vec, c_wa, c_g, c_row = chan("c_vec"), chan("c_wa"), chan("c_g"), chan("c_row")
        ldv = load(c_vec, vec[:, :], A["vec"])
        kpo = lambda ap: ap.rearrange("(k p) o -> p k o", p=P)

        def load_qkv(l, dst, *marks):
            for i, w in enumerate(("WqT", "WkT", "WvT")):
                m = load(c_wa, dst[:, i], kpo(A[w][l]), *marks)
            return m

        def load_row(i, src, *marks):
            return load(c_row, rowsb[:, i, :], src.partition_broadcast(P), *marks)

        wqkv = load_qkv(0, WA)
        rowm = load_row(0, A["gbq"][0])
        c_zero = chan("c_zero")
        for l in range(2):
            load(c_zero, aggd[l][0:3968, :].rearrange("(t p) d -> p t d", p=P),
                 zero.unsqueeze(1).to_broadcast([P, 31, 512]), z0)
            load(c_zero, aggd[l][3968:AGG_ROWS, :], zero[0:AGG_ROWS - 3968, :], z0)
            zeroed = load(c_zero, Qd[l][N:AGG_F, :], zero[0:AGG_F - N, :], z0)

        def ln_stats(tiles, ready):
            a, b = tiles[0], tiles[-1] + 1
            for t in tiles:
                m = DVE.do(lambda e, t=t: e.bn_stats(out=st[:, 6 * (t % 25):6 * (t % 25) + 6], in_=Yt[:, t, :]), ready(t))
            for t in tiles:
                m2 = DVE.do(lambda e, t=t: e.bn_aggr(out=mv[:, t, :], in_=st[:, 6 * (t % 25):6 * (t % 25) + 6]), m)
            m = DVE.do(lambda e: e.tensor_scalar(rs[:, a:b], mv[:, a:b, 1], EPS, None, ALU.add), m2)
            m = ACTQ.do(lambda e: e.activation(rs[:, a:b], rs[:, a:b], ACT.Sqrt), m)
            return DVE.do(lambda e: e.reciprocal(rs[:, a:b], rs[:, a:b]), m)

        def to_features(t, src, ready, dst_free):
            r = ROWS[t]
            i, bank, free = turn.take()
            for k in range(4):
                f = lambda e, k=k: e.transpose(bank[:, k * P:k * P + r], src[0:r, k * P:(k + 1) * P], ident[0:r, 0:r])
                if k < 3:
                    PE.quiet(f, free, ready, idm)
                else:
                    m = PE.do(f)
            bk = bank[:, :].rearrange("p (k n) -> p k n", k=4)
            turn.free[i] = ACTQ.do(lambda e: e.activation(xT[:, :, P * t:P * t + r], bk[:, :, 0:r], ACT.Copy), m, dst_free)
            return turn.free[i], m

        groups = [list(range(6 * g, min(6 * g + 6, NT))) for g in range(5)]
        xT_ready = [None] * NT
        for tiles in groups:
            m = ln_stats(tiles, lambda t: [xtile[t], xpad])
            for t in tiles:
                mn = DVE.do(lambda e, t=t: e.tensor_scalar(Yt[:, t, :], Yt[:, t, :], mv[:, t, 0:1], rs[:, t:t + 1],
                                                           ALU.subtract, ALU.mult), m)
                xT_ready[t], y_read = to_features(t, Yt[:, t, :], mn, None)

        pf = pre
        d_i, p_i, s_i = pf[0:TP, 0].bitcast(I32), pf[0:TP, 1].bitcast(I32), pf[0:TP, 2].bitcast(I32)
        sm_t, nf_t, or_t, df_t = pf[0:TP, 3], pf[0:TP, 4], pf[0:TP, 5], pf[0:TP, 0]
        w0 = work[0:TP, 0, :].rearrange("p (b e) -> p b e", b=TB)
        w1 = work[0:TP, 1, :].rearrange("p (b e) -> p b e", b=TB)
        m = DVE.do(lambda e: e.tensor_tensor(sm_t, d_i, p_i, ALU.is_equal), ld_d, ld_p)
        m2 = DVE.do(lambda e: e.tensor_copy(w0, d_i))
        DVE.do(lambda e: e.tensor_copy(w1, s_i), ld_s)
        m = DVE.do(lambda e: e.tensor_scalar(nf_t, sm_t, -1.0, 1.0, ALU.mult, ALU.add), m)
        m = DVE.do(lambda e: e.memset(nf_t[:, :, 0], 0.0), m)
        for b in range(TB):
            mo = DVE.do(lambda e, b=b: e.tensor_tensor_scan(or_t[:, b, :], nf_t[:, b, :], nf_t[:, b, :], 0.0,
                                                            ALU.add, ALU.max), m)
        mnf = DVE.do(lambda e: e.memset(nf_t[:, :, 0], 1.0), mo)
        nodeF, nodeL, goes, toL, start, t0, t1 = (bnd[:, i, :] for i in range(7))
        came = sm_t[:, :, 0]
        DVE.do(lambda e: e.tensor_copy(nodeF, w0[:, :, 0]), m2)
        mb = DVE.do(lambda e: e.tensor_copy(nodeL, w0[:, :, P - 1]))
        mg = DVE.do(lambda e: e.tensor_tensor(goes, dnx[:, :, 0], dnx[:, :, 1], ALU.is_equal), ld_n)
        m3 = DVE.do(lambda e: e.scalar_tensor_tensor(out=toL, in0=iotaT[:, :], scalar=float(ET), in1=nodeL,
                                                     op0=ALU.add, op1=ALU.subtract), mb, iotm)
        m3 = DVE.do(lambda e: e.tensor_tensor(toL, toL, goes, ALU.mult), m3, mg)
        for b in range(TB):
            m4 = DVE.do(lambda e, b=b: e.tensor_scalar(df_t[:, b, :], w0[:, b, :], nodeL[:, b:b + 1], toL[:, b:b + 1],
                                                       ALU.is_equal, ALU.mult), m3)
        m4 = DVE.do(lambda e: e.tensor_tensor(df_t, df_t, w0, ALU.add), m4)
        m3 = DVE.do(lambda e: e.tensor_tensor(t0, iotaT[:, :], df_t[:, :, 0], ALU.subtract), m4)
        m3 = DVE.do(lambda e: e.tensor_tensor(t0, t0, came, ALU.mult), m3)
        m3 = DVE.do(lambda e: e.tensor_tensor(df_t[:, :, 0], df_t[:, :, 0], t0, ALU.add), m3)
        fv_t = pf[0:TP, 1]
        m3 = DVE.do(lambda e: e.scalar_tensor_tensor(out=fv_t, in0=df_t, scalar=FAR, in1=nf_t,
                                                     op0=ALU.subtract, op1=ALU.mult), m3, mnf)
        m5 = DVE.do(lambda e: e.tensor_tensor(t1, nodeF, nodeL, ALU.is_equal), mb)
        m5 = DVE.do(lambda e: e.tensor_tensor(t1, t1, came, ALU.mult), m5)
        m5 = DVE.do(lambda e: e.tensor_tensor(t1, t1, goes, ALU.mult), m5, mg)
        m5 = DVE.do(lambda e: e.tensor_tensor(t1, goes, t1, ALU.subtract), m5)
        m6 = DVE.do(lambda e: e.scalar_tensor_tensor(out=start, in0=nodeL, scalar=5.0, in1=t1, op0=ALU.add, op1=ALU.mult), m5)
        start_m = DVE.do(lambda e: e.tensor_scalar(start, start, -5.0, None, ALU.add), m6)
        m6 = DVE.do(lambda e: e.scalar_tensor_tensor(out=t0, in0=nodeL, scalar=FAR, in1=t1, op0=ALU.subtract, op1=ALU.mult),
                    m5, m3)
        runrow_m = DVE.do(lambda e: e.tensor_scalar(runrow[:, :], t0, FAR, None, ALU.add), m6)
        DVE.do(lambda e: e.tensor_tensor(link[:, 0:SEQ + 1:2], dI[0:HC, 0:CH + 1:P], dI[0:HC, 1:CH + 2:P], ALU.is_equal), ld_q)
        link_m = DVE.do(lambda e: e.tensor_tensor(link[:, 1:SEQ:2], dI[0:HC, 1:CH + 1:P], dI[0:HC, P:CH + 1:P], ALU.is_equal))
        linkp_m = DVE.do(lambda e: e.tensor_scalar(linkp[:, :], link[:, :], 1.0, BIG, ALU.subtract, ALU.mult), link_m)
        idr = ident[0:HC, 0:HC]
        DVE.do(lambda e: e.tensor_reduce(maskC[:, :], idr.rearrange("p (h c) -> p c h", h=H), AXX, ALU.add), idm)
        mask_m = DVE.do(lambda e: e.tensor_reduce(selH[:, :], idr.rearrange("p (h c) -> p h c", h=H), AXX, ALU.add))
        DVE.do(lambda e: e.memset(pen[:, P:P + 1], 0.0))
        gate_m = DVE.do(lambda e: e.memset(same[:, P:P + 1], 0.0))
        pre_done = []
        for srct, dstt in ((or_t, ordE), (fv_t, fvE), (nf_t, nfE), (w1, srcE), (w0, dstE)):
            i, bank, free = turn.take()
            for b in range(TB):
                f = lambda e, b=b, srct=srct, bank=bank: e.transpose(bank[:, b * TP:(b + 1) * TP], srct[:, b, :],
                                                                     ident[0:TP, 0:TP])
                if b < 3:
                    PE.quiet(f, free, m3, idm)
                else:
                    mp = PE.do(f)
            turn.free[i] = ACTQ.do(lambda e, bank=bank, dstt=dstt: e.activation(dstt[:, :], bank[:, 0:ET], ACT.Copy), mp)
            pre_done.append(turn.free[i])
        idx_ready = pre_done[-1]
        pre_read = mp

        def rows_product(t, w, ready, src=None, s0=None):
            r = ROWS[t]
            i, bank, free = dense.take()
            for k in range(4):
                lhs = xT[:, k, P * t:P * t + r] if src is None else src[:, k, s0:s0 + r]
                f = lambda e, k=k, lhs=lhs: e.matmul(bank[0:r, :], lhs, w[:, k, :], start=(k == 0), stop=(k == 3))
                if k < 3:
                    PE.quiet(f, free, ready)
                else:
                    m = PE.do(f)
            return i, bank, m

        def qkv(l, W, wready, xready, rowm, brow):
            bs = DVE.do(lambda e: e.tensor_scalar(rowsb[:, brow, :], rowsb[:, brow, :], 0.125, None, ALU.mult), rowm)
            for t in range(NT):
                r = ROWS[t]
                for w, table in ((0, Qd[l]), (1, KVd[l][:, 0:D]), (2, KVd[l][:, D:2 * D])):
                    i, bank, m = rows_product(t, W[:, w], [wready, xready(t)])
                    s, buf, _ = stg.take()
                    gone = stg_ch[s].mark()
                    if w == 0:
                        m = DVE.do(lambda e, bank=bank, buf=buf, r=r: e.scalar_tensor_tensor(
                            out=buf[0:r, :], in0=bank[0:r, :], scalar=0.125, in1=rowsb[0:r, brow, :],
                            op0=ALU.mult, op1=ALU.add), m, gone, bs, stg.free[s])
                    else:
                        m = ACTQ.do(lambda e, bank=bank, buf=buf, r=r: e.activation(buf[0:r, :], bank[0:r, :], ACT.Copy),
                                    m, gone, stg.free[s])
                    dense.free[i] = m
                    stg.free[s] = load(stg_ch[s], table[P * t:P * t + r, :], buf[0:r, :], m)
            return [c.mark() for c in stg_ch], (PE.sem, PE.n)

        kv_ready, x_read = qkv(0, WA, wqkv, lambda t: xT_ready[t], rowm, 0)

        h8 = lambda ap: ap.rearrange("p (h d) -> p h d", h=H)
        mix_end = {}

        def mix(xready, wa_free, mt_free):
            rows = [load_row(i, A[b], (DVE.sem, DVE.n)) for i, b in enumerate(("mbq", "mbk", "mbv", "mbp"))][-1]
            for i, w in enumerate(("MkT", "MvT", "MqT")):
                load(c_wa, WA[:, i], kpo(A[w]), wa_free)
            wm = [c_wa.mark(), load(c_g, G[:, 12:16, :], kpo(A["MpT"]), link_m)]
            prod = Ring([PS[0], PS[1]])
            prod.free = [dense.free[0], dense.free[1]]
            acc = [PS[2], PS[3]]
            acc_free = [dense.free[2], dense.free[3]]
            kb = [mt[:, 512 * i:512 * (i + 1)] for i in range(2)]
            vb = [mt[:, 1024 + 516 * i:1024 + 516 * (i + 1)].rearrange("p (k n) -> p k n", k=4) for i in range(2)]
            BD = mt[:, 2064:2584].rearrange("p (k n) -> p k n", k=4)
            qT, oT = (G[:, 10 + i, :].rearrange("p (k n) -> p k n", k=4) for i in range(2))
            for i in range(2):
                one_m = DVE.do(lambda e, i=i: e.memset(vb[i][:, :, P], 1.0), mt_free)
            bd0 = DVE.do(lambda e: e.memset(BD, 0.0), mt_free)
            yield

            plan = {}

            def at(step, f, *args):
                plan.setdefault(step, []).append((f, args))

            S = [dict() for _ in range(2 * NT)]

            def product(x, t, w, k, src=None):
                r = ROWS[t]
                if k == 0:
                    x["i"], x["bank"], x["free"] = prod.take()
                lhs = xT[:, k, P * t:P * t + r] if src is None else src[:, k, 0:r]
                f = lambda e: e.matmul(x["bank"][0:r, :], lhs, w[:, k, :], start=(k == 0), stop=(k == 3))
                if k < 3:
                    PE.quiet(f, x["free"], wm, xready(t), x.get("src"))
                else:
                    x["m"] = PE.do(f)

            def soft_a(x, y, t, buf, row, free):
                r = ROWS[t]
                s = small[0:r, 8:16]
                b = buf[0:r, :]
                m = DVE.do(lambda e: e.tensor_tensor(b, x["bank"][0:r, :], rowsb[0:r, row, :], ALU.add), x["m"], free(), rows)
                prod.free[x["i"]] = m
                m = DVE.do(lambda e: e.tensor_reduce(s, h8(b), AXX, ALU.max), m)
                m = DVE.do(lambda e: e.tensor_tensor(h8(b), h8(b), s.unsqueeze(2).to_broadcast([r, H, DH]), ALU.subtract), m)
                y["exp"] = ACTQ.do(lambda e: e.activation(b, b, ACT.Exp), m)

            def soft_b(y, t, buf):
                r = ROWS[t]
                s = small[0:r, 16:24]
                b = buf[0:r, :]
                m = DVE.do(lambda e: e.tensor_reduce(s, h8(b), AXX, ALU.add), y["exp"])
                m = DVE.do(lambda e: e.reciprocal(s, s), m)
                y["soft"] = DVE.do(lambda e: e.tensor_tensor(h8(b), h8(b), s.unsqueeze(2).to_broadcast([r, H, DH]),
                                                             ALU.mult), m)

            used = [None, None]

            def add_v(y, xv, t):
                r, u = ROWS[t], t % 2
                y["v"] = prod.free[xv["i"]] = DVE.do(lambda e: e.tensor_tensor(
                    vb[u][0:r, :, 0:P], xv["bank"][0:r, :].rearrange("p (k n) -> p k n", k=4),
                    rowsb[0:r, 2, :].rearrange("p (k n) -> p k n", k=4), ALU.add), xv["m"], used[u], one_m)

            def context(y, t, k):
                r, u = ROWS[t], t % 2
                used[u] = PE.do(lambda e: e.matmul(
                    acc[k // 2][:, 129 * (k % 2):129 * (k % 2) + 129], kb[u][0:r, k * P:(k + 1) * P], vb[u][0:r, k, :],
                    start=(t == 0 and k % 2 == 0), stop=(t == NT - 1 and k % 2 == 1), skip_group_check=True),
                    y["soft"], y["v"], acc_free)

            for t in range(NT):
                xk, xv, y = {}, {}, S[t]
                for k in range(4):
                    at(8 * t + k, product, xk, t, WA[:, 0], k)
                    at(8 * t + 4 + k, product, xv, t, WA[:, 1], k)
                    at(8 * t + 10 + k // 2, context, y, t, k)
                at(8 * t + 5, soft_a, xk, y, t, kb[t % 2], 1, lambda t=t: used[t % 2])
                at(8 * t + 6, soft_b, y, t, kb[t % 2])
                at(8 * t + 9, add_v, y, xv, t)

            z = {"q": None, "o": None, "qT": None, "oT": None}

            def block_diagonal():
                z["kv"] = z["q"] = z["o"] = used[(NT - 1) % 2]
                for h in range(H):
                    a, k = 64 * (h % 2), h // 2
                    bank, c = acc[k // 2], 129 * (k % 2)
                    DVE.do(lambda e, a=a, k=k, bank=bank, c=c: e.tensor_copy(
                        BD[a:a + 64, k, a:a + 64], bank[a:a + 64, c + a:c + a + 64]), z["kv"], bd0)
                    z["bd"] = z["o2"] = DVE.do(lambda e, a=a, k=k, bank=bank, c=c, h=h: e.tensor_copy(
                        BD[a:a + 64, k, P + h % 2:P + h % 2 + 1], bank[a:a + 64, c + P:c + P + 1]))

            at(8 * NT + 4, block_diagonal)
            qb, ob = kb[0], kb[1]
            outb = [mt[:, 1024:1536], mt[:, 1536:2048]]
            sch = [chan("c_mix0"), chan("c_mix1")]

            def features(t, buf, dst, ready, free):
                r = ROWS[t]
                i, bank, fr = turn.take()
                for k in range(4):
                    f = lambda e, k=k: e.transpose(bank[:, k * P:k * P + r], buf[0:r, k * P:(k + 1) * P], ident[0:r, 0:r])
                    if k < 3:
                        PE.quiet(f, fr, ready)
                    else:
                        m = PE.do(f)
                bk = bank[:, :].rearrange("p (k n) -> p k n", k=4)
                turn.free[i] = ACTQ.do(lambda e: e.activation(dst[:, :, 0:r], bk[:, :, 0:r], ACT.Copy), m, free, link_m)
                return m, turn.free[i]

            def q_features(y, t):
                _, y["qT"] = features(t, qb, qT, y["soft"], z["qT"])

            def q_context(y, t):
                r = ROWS[t]
                for k in range(4):
                    f = lambda e, k=k: e.matmul(acc[k // 2][0:r, 130 * (k % 2):130 * (k % 2) + 130], qT[:, k, 0:r],
                                                BD[:, k, :], start=(k % 2 == 0), stop=(k % 2 == 1), skip_group_check=True)
                    if k < 3:
                        PE.quiet(f, y["qT"], z["bd"], z["o2"])
                    else:
                        y["c"] = z["qT"] = PE.do(f)

            def normal(y, t):
                r = ROWS[t]
                di = small[0:r, 24:32]
                mm = []
                for g in range(2):
                    v = acc[g][0:r, 0:260].rearrange("p (k n) -> p k n", k=2)
                    d2 = di[:, 4 * g:4 * g + 4].rearrange("p (k j) -> p k j", k=2)
                    mm.append(DVE.do(lambda e, v=v, d2=d2: e.reciprocal(d2, v[:, :, P:P + 2]), y["c"]))
                for g in range(2):
                    v = acc[g][0:r, 0:260].rearrange("p (k n) -> p k n", k=2)
                    for k in range(2):
                        o2 = 4 * g + 2 * k
                        m = DVE.do(lambda e, v=v, g=g, k=k, o2=o2: e.tensor_tensor(
                            ob[0:r, 256 * g + P * k:256 * g + P * k + P].rearrange("p (j d) -> p j d", j=2),
                            v[:, k, 0:P].rearrange("p (j d) -> p j d", j=2),
                            di[:, o2:o2 + 2].unsqueeze(2).to_broadcast([r, 2, DH]), ALU.mult), mm[g], z["o"])
                z["o2"] = m
                y["out"] = DVE.do(lambda e: e.tensor_tensor(ob[0:r, :], ob[0:r, :], qb[0:r, :], ALU.add), m)
                z["q"] = [y["out"], y["c"]]

            def o_features(y, xp, t):
                z["o"], xp["src"] = features(t, ob, oT, y["out"], z["oT"])

            def store(xp, t):
                r, u = ROWS[t], t % 2
                z["oT"] = xp["m"]
                m = prod.free[xp["i"]] = DVE.do(lambda e: e.tensor_tensor(
                    outb[u][0:r, :], xp["bank"][0:r, :], rowsb[0:r, 3, :], ALU.add), xp["m"], sch[u].mark(), z["kv"])
                load(sch[u], mixd[P * t:P * t + r, :], outb[u][0:r, :], m)

            for t in range(NT):
                xq, xp, y, b = {}, {}, S[NT + t], 8 * (NT + t)
                for k in range(4):
                    at(b + k, product, xq, t, WA[:, 2], k)
                    at(b + 12 + k, product, xp, t, G[:, 12:16, :], k, oT)
                at(b + 5, soft_a, xq, y, t, qb, 0, lambda: z["q"])
                at(b + 6, soft_b, y, t, qb)
                at(b + 8, q_features, y, t)
                at(b + 9, q_context, y, t)
                at(b + 10, normal, y, t)
                at(b + 11, o_features, y, xp, t)
                at(b + 17, store, xp, t)
            for step in range(max(plan) + 1):
                for f, args in plan.get(step, ()):
                    f(*args)
                yield
            mix_end["done"] = [(PE.sem, PE.n), (DVE.sem, DVE.n), (ACTQ.sem, ACTQ.n)]
            mix_end["stores"] = [c.mark() for c in sch]

        kv_ch = [chan(f"c_kv{i}") for i in range(KV)]
        q_ch = [chan(f"c_q{i}") for i in range(6)]
        sct_ch = [chan(f"c_sct{i}") for i in range(4)]
        order = [c * NJ + j for j in range(NJ) for c in range(NCH)]
        nfb = nfE[:, :].rearrange("p (c j) -> p j c", c=NCH)
        wk = Ring([work[:, s, :] for s in range(3)])
        wk.free = [pre_read, pre_read, zeroed]
        oh = Ring([onehot[:, s, :] for s in range(3)])
        seg_marks = {}

        def attend(l, tables, start, side):
            kv_free, q_free = [None] * KV, [None] * 6
            ready, batch, pend = {}, {}, []
            sc_free, w_free, fix_m = [None] * 3, [None] * 2, None

            def fetch(n):
                if n < ET:
                    a, b, i = n % KV, n % 6, order[n]
                    ready[n] = [kv_ch[a].send(POOL, lambda e: e.indirect_dma_start(
                        out=kvs[a], out_offset=None, in_=KVd[l][:, :],
                        in_offset=bass.IndirectOffsetOnAxis(ap=srcE[:, i:i + 1], axis=0)),
                        tables, idx_ready, start, kv_free[a]),
                        q_ch[b].send(POOL, lambda e: e.indirect_dma_start(
                            out=G[:, b, :], out_offset=None, in_=Qd[l][:, :],
                            in_offset=bass.IndirectOffsetOnAxis(ap=dstE[:, i:i + 1], axis=0)), q_free[b])]

            for n in range(AHEAD):
                fetch(n)
            sub_free, same_free, rep_free = None, None, None
            for n in range(ET + LAG):
                if n < ET:
                    fetch(n + AHEAD)
                    a, b, j, c = n % KV, n % 6, n // NCH, n % NCH
                    i, buf, free = wk.take()
                    m = DVE.do(lambda e, a=a, b=b, buf=buf: e.tensor_tensor(buf, kvs[a][:, 0:D], G[:, b, :], ALU.mult),
                               ready.pop(n), free)
                    q_free[b] = m
                    sj = scores[:, j % 3, :]
                    m = DVE.do(lambda e, c=c, buf=buf, sj=sj: e.tensor_reduce(
                        sj.rearrange("p (h c) -> p h c", h=H)[:, :, c], h8(buf), AXX, ALU.add), m, sc_free[j % 3])
                    wk.free[i] = m
                    if c == NCH - 1:
                        mn = ACTQ.do(lambda e, j=j: e.activation(
                            firsts[:, :].rearrange("p (h c) -> p h c", h=H),
                            nfb[:, j, :].unsqueeze(1).to_broadcast([P, H, NCH]), ACT.Copy), idx_ready, rep_free)
                        i, bank, free = turn.take()
                        PE.quiet(lambda e, bank=bank, sj=sj: e.transpose(bank[0:HC, 0:P], sj, ident[:, :]), m, free)
                        mp = rep_free = PE.do(lambda e, bank=bank: e.transpose(bank[0:HC, P:2 * P], firsts[:, :], ident[:, :]), mn)
                        sc_free[j % 3] = mp
                        mt1 = ACTQ.do(lambda e, bank=bank: e.activation(sA, bank[0:HC, 0:P], ACT.Copy), mp, sub_free, start)
                        mt2 = ACTQ.do(lambda e, bank=bank: e.activation(pen[:, 0:P], bank[0:HC, P:2 * P], ACT.Copy,
                                                                        scale=-BIG), same_free)
                        turn.free[i] = mt2 = ACTQ.do(lambda e, bank=bank: e.activation(
                            same[:, 0:P], bank[0:HC, P:2 * P], ACT.Copy, scale=-1.0, bias=1.0), same_free)
                        batch["t"] = (j, [mt1, mt2])
                r = n % NCH
                if r == 0 and "t" in batch:
                    j, m = batch.pop("t")
                    m = DVE.do(lambda e: e.tensor_tensor_scan(sB, pen[:, 0:P], sA, -BIG, ALU.add, ALU.max), m, fix_m, gate_m)
                    m = DVE.do(lambda e: e.tensor_tensor_scan(sC[:, ::-1], pen[:, P:0:-1], sB[:, ::-1], -BIG,
                                                              ALU.add, ALU.max), m)
                    mx = ACTQ.do(lambda e, j=j: e.activation(fixm[:, j, :], sC[:, 0:P:P - 1], ACT.Copy), m)
                    m = DVE.do(lambda e: e.tensor_tensor(sA, sA, sC, ALU.subtract), m)
                    m = ACTQ.do(lambda e: e.activation(sA, sA, ACT.Exp), m)
                    batch["x"] = (j, m, mx)
                if r == 1 and "x" in batch:
                    j, m, mx = batch.pop("x")
                    m = DVE.do(lambda e: e.tensor_tensor_scan(sB, same[:, 0:P], sA, 0.0, ALU.mult, ALU.add), m)
                    m = DVE.do(lambda e: e.scalar_tensor_tensor(out=sB, in0=same[:, 1:P + 1], scalar=1.0, in1=sB,
                                                                op0=ALU.subtract, op1=ALU.mult), m)
                    m = DVE.do(lambda e: e.tensor_tensor_scan(sC[:, ::-1], same[:, P:0:-1], sB[:, ::-1], 0.0,
                                                              ALU.mult, ALU.add), m, mx)
                    same_free = m
                    m = DVE.do(lambda e: e.tensor_scalar(sC, sC, -1.0, 1e-16, ALU.mult, ALU.add), m)
                    fix_m = ACTQ.do(lambda e, j=j: e.activation(fixl[:, j, :], sC[:, 0:P:P - 1], ACT.Copy), m)
                    m = DVE.do(lambda e: e.reciprocal(sB, sC), m)
                    m = DVE.do(lambda e: e.tensor_tensor(sA, sA, sB, ALU.mult), m)
                    i, bank, free = turn.take()
                    mp = sub_free = PE.do(lambda e, bank=bank: e.transpose(bank[:, 0:HC], sA, ident[0:HC, 0:HC]), m, free)
                    wj = wts[:, j % 2, :]
                    turn.free[i] = mw_ready = ACTQ.do(lambda e, bank=bank, wj=wj: e.activation(wj, bank[:, 0:HC], ACT.Copy),
                                                      mp, w_free[j % 2])
                if n >= LAG:
                    v = n - LAG
                    a, j, c, e_i = v % KV, v // NCH, v % NCH, order[v]
                    wj = wts[:, j % 2, :].rearrange("p (h c) -> p h c", h=H)[:, :, c:c + 1]
                    i, buf, free = wk.take()
                    mw = DVE.do(lambda e, a=a, wj=wj, buf=buf: e.tensor_tensor(
                        h8(buf), h8(kvs[a][:, D:2 * D]), wj.to_broadcast([P, H, DH]), ALU.mult), free, mw_ready)
                    kv_free[a] = w_free[j % 2] = mw
                    io, ohb, ofree = oh.take()
                    mo = DVE.do(lambda e, e_i=e_i, ohb=ohb: e.tensor_scalar(ohb, iota[:, :], ordE[:, e_i:e_i + 1], None,
                                                                            ALU.is_equal), ofree, iom, idx_ready)
                    ib, bank, free = edge.take()
                    mp = PE.do(lambda e, ohb=ohb, buf=buf, bank=bank: e.matmul(bank[:, :], ohb, buf, start=True, stop=True),
                               mw, mo, free)
                    wk.free[i] = oh.free[io] = mp
                    if l == 0:
                        it, tb, free = turn.take()
                        mp2 = PE.do(lambda e, ohb=ohb, tb=tb, e_i=e_i: e.matmul(tb[:, 0:1], ohb, fvE[:, e_i:e_i + 1],
                                                                               start=True, stop=True), free)
                        oh.free[io] = mp2
                        turn.free[it] = seg_marks[e_i] = ACTQ.do(lambda e, tb=tb, e_i=e_i: e.activation(
                            segE[:, e_i:e_i + 1], tb[:, 0:1], ACT.Copy, bias=FAR), mp2)
                    k, sbuf, sfree = stg.take()
                    me = edge.free[ib] = ACTQ.do(lambda e, sbuf=sbuf, bank=bank: e.activation(sbuf, bank[:, :], ACT.Copy), mp,
                                                 stg_ch[k].mark(), sfree)
                    pend.append((k, sbuf, e_i, me))
                    while pend and (len(pend) > 2 or v == ET - 1):
                        k, sbuf, e_i, me = pend.pop(0)
                        stg.free[k] = sct_ch[k].send(POOL, lambda e, sbuf=sbuf, e_i=e_i: e.indirect_dma_start(
                            out=aggd[l][:, :], out_offset=bass.IndirectOffsetOnAxis(ap=segE[:, e_i:e_i + 1], axis=0),
                            in_=sbuf, in_offset=None, bounds_check=AGG_ROWS - 1, oob_is_err=False),
                            me, seg_marks[e_i], zeroed)
                if side is not None:
                    next(side, None)
            return [mw, mp], fix_m

        hc = lambda row: rows1[0:1, row, :].rearrange("a (h c) -> a h c", h=H)
        links = []
        snB = fvE
        c_join = [chan("c_joinF"), chan("c_joinL")]

        def shared_setup(free):
            smin = small[0:HC, 32:34]
            DVE.do(lambda e: e.tensor_reduce(smin[:, 0:1], link[:, 0:SEQ], AXX, ALU.min), linkp_m)
            m = DVE.do(lambda e: e.tensor_reduce(smin[:, 1:2], link[:, 1:SEQ + 1], AXX, ALU.min))
            DVE.do(lambda e: e.memset(rows1[:, 0:2, :], 0.0), free)
            DVE.do(lambda e: e.memset(rows1[:, 4:6, :], -BIG))
            DVE.do(lambda e: e.memset(rows1[:, 12:14, :], 1.0))
            mz = DVE.do(lambda e: e.memset(rows1[:, 6:8, :], 0.0))
            for d in range(2):
                i, bank, fr = turn.take()
                mp = PE.do(lambda e, d=d, bank=bank: e.transpose(bank[0:1, 0:HC], smin[:, d:d + 1], ident[0:HC, 0:HC]), fr, m)
                bh = bank[0:1, 0:HC].rearrange("a (h c) -> a h c", h=H)
                if d == 0:
                    m1 = DVE.do(lambda e, bh=bh: e.tensor_copy(hc(0)[:, :, 1:NCH], bh[:, :, 0:NCH - 1]), mp, mz)
                else:
                    m1 = DVE.do(lambda e, bh=bh: e.tensor_copy(hc(1)[:, :, 0:NCH - 1], bh[:, :, 1:NCH]), mp, mz)
                turn.free[i] = m1
            links.append(DVE.do(lambda e: e.tensor_scalar(rows1[:, 2:4, :], rows1[:, 0:2, :], 1.0, BIG,
                                                          ALU.subtract, ALU.mult), m1))
            i, bank, fr = turn.take()
            for b in range(TB):
                mp = PE.do(lambda e, b=b, bank=bank: e.transpose(bank[0:1, b * TP:(b + 1) * TP], start[:, b:b + 1],
                                                                 ident[0:TP, 0:TP]), fr, start_m)
            row = rowsb[0:1, 3, 0:ET]
            m = turn.free[i] = DVE.do(lambda e, bank=bank: e.tensor_copy(row, bank[0:1, 0:ET]), mp, free)
            i, bank, fr = turn.take()
            o1 = rows1[0:1, 12:14, :].rearrange("a s p -> a (s p)")[:, 0:TP]
            mp = PE.do(lambda e, bank=bank: e.matmul(bank[0:TP, 0:ET], o1, row, start=True, stop=True), fr, m)
            m = turn.free[i] = DVE.do(lambda e, bank=bank: e.tensor_copy(snB[0:TP, :], bank[0:TP, 0:ET]), mp, free)
            links.append(m)

        def seg_scan(data, res, kind, back, m):
            ops = (ALU.add, ALU.max) if kind == 0 else (ALU.mult, ALU.add)
            init = -BIG if kind == 0 else 0.0
            gate = linkp if kind == 0 else link
            if back:
                g, x, o = gate[:, SEQ:0:-1], data[:, ::-1], res[:, ::-1]
                last = res[:, 0:1]
            else:
                g, x, o = gate[:, 0:SEQ], data, res
                last = res[:, SEQ - 1:SEQ]
            m = DVE.do(lambda e: e.tensor_tensor_scan(o, g, x, init, *ops), m)
            i, bank, free = turn.take()
            mp = PE.do(lambda e: e.transpose(bank[0:1, 0:HC], last, ident[0:HC, 0:HC]), m, free)
            bh = bank[0:1, 0:HC].rearrange("a (h c) -> a h c", h=H)
            hand, lk, car = 4 + 2 * kind + back, (2 if kind == 0 else 0) + back, 8 + 2 * kind + back
            if back:
                m = DVE.do(lambda e: e.tensor_copy(hc(hand)[:, :, 0:NCH - 1], bh[:, :, 1:NCH]), mp, links)
                m1 = DVE.do(lambda e: e.tensor_tensor_scan(rows1[:, car, ::-1], rows1[:, lk, ::-1],
                                                           rows1[:, hand, ::-1], init, *ops), m)
            else:
                m = DVE.do(lambda e: e.tensor_copy(hc(hand)[:, :, 1:NCH], bh[:, :, 0:NCH - 1]), mp, links)
                m1 = DVE.do(lambda e: e.tensor_tensor_scan(rows1[:, car, :], rows1[:, lk, :], rows1[:, hand, :],
                                                           init, *ops), m)
            turn.free[i] = m
            i, bank2, free = turn.take()
            mp = PE.do(lambda e: e.transpose(bank2[0:HC, 0:1], rows1[0:1, car, :], ident[0:1, 0:1]), m1, free)
            cc = small[0:HC, 40 + 2 * kind + back:41 + 2 * kind + back]
            m = DVE.do(lambda e: e.tensor_copy(cc, bank2[0:HC, 0:1]), mp)
            turn.free[i] = m
            return DVE.do(lambda e: e.tensor_tensor_scan(o, g, x, cc, *ops), m)

        def join(l, fix_m, edges):
            stored = [c.mark() for c in sct_ch]
            part = [G[0:TP, 4 * i:4 * i + 4, :] for i in range(2)]
            base = (AGG_F, AGG_L)
            pl = [load(c_join[i], part[i], aggd[l][base[i]:base[i] + ET, :].rearrange("(b p) d -> p b d", p=TP),
                       stored, edges) for i in range(2)]
            if l == 0:
                shared_setup([edges, mix_end["done"]])
            flat = lambda ap: ap.rearrange("p j k -> p (j k)")
            X, Z, W_ = (ap[:, 0:SEQ] for ap in (sA, sB, sC))
            m = seg_scan(flat(fixm[:, :, :]), X, 0, 0, [fix_m, edges])
            m = seg_scan(X, Z, 0, 1, m)
            m = DVE.do(lambda e: e.tensor_tensor(X, flat(fixm[:, :, :]), Z, ALU.subtract), m)
            m = ACTQ.do(lambda e: e.activation(X, X, ACT.Exp), m)
            X3 = X.rearrange("p (j k) -> p j k", k=2)
            m = DVE.do(lambda e: e.tensor_tensor(X, X, flat(fixl[:, :, :]), ALU.mult), m)
            Z3 = Z.rearrange("p (j k) -> p j k", k=2)
            m2 = DVE.do(lambda e: e.tensor_copy(Z, X), m)
            m2 = DVE.do(lambda e: e.tensor_tensor(Z3[:, :, 1], X3[:, :, 1], link[:, 1:SEQ:2], ALU.mult), m2)
            m2 = DVE.do(lambda e: e.tensor_tensor(Z3[:, :, 1], X3[:, :, 1], Z3[:, :, 1], ALU.subtract), m2)
            m = seg_scan(Z, W_, 1, 0, m2)
            m = DVE.do(lambda e: e.scalar_tensor_tensor(out=W_, in0=link[:, 1:SEQ + 1], scalar=1.0, in1=W_,
                                                        op0=ALU.subtract, op1=ALU.mult), m)
            m = seg_scan(W_, Z, 1, 1, m)
            m = DVE.do(lambda e: e.tensor_scalar(Z, Z, -1.0, 1e-16, ALU.mult, ALU.add), m)
            m = DVE.do(lambda e: e.reciprocal(Z, Z), m)
            m = DVE.do(lambda e: e.tensor_tensor(X, X, Z, ALU.mult), m)
            fac = small[0:TP, 0:64 - 0].rearrange("p (k b h) -> p k b h", k=2, b=TB)
            i, bank, free = turn.take()
            for k in range(2):
                for b in range(TB):
                    iw, hb, hfree = wk.take()
                    lhs = hb[0:HC, 0:TP]
                    m2 = DVE.do(lambda e, k=k, b=b, lhs=lhs: e.tensor_tensor(
                        lhs.rearrange("p (c j) -> p c j", c=2), X3[:, :, k].unsqueeze(1).to_broadcast([HC, 2, NJ]),
                        maskC[:, 2 * b:2 * b + 2].unsqueeze(2).to_broadcast([HC, 2, NJ]), ALU.mult), m, mask_m, hfree)
                    o = (k * TB + b) * H
                    mp = wk.free[iw] = PE.do(lambda e, lhs=lhs, o=o, bank=bank: e.matmul(
                        bank[0:TP, o:o + H], lhs, selH[:, :], start=True, stop=True), m2, free)
            mf = turn.free[i] = DVE.do(lambda e, bank=bank: e.tensor_copy(small[0:TP, 0:64], bank[0:TP, 0:64]), mp)
            banks = [dense.take() for _ in range(TB)]
            for k in range(2):
                for b in range(TB):
                    mr = DVE.do(lambda e, k=k, b=b: e.tensor_tensor(
                        h8(part[k][:, b, :]), h8(part[k][:, b, :]),
                        fac[:, k, b, :].unsqueeze(2).to_broadcast([TP, H, DH]), ALU.mult), mf, pl[k])
                    iw, hb, hfree = wk.take()
                    node = (nodeF, nodeL)[k]
                    ms = DVE.do(lambda e, hb=hb, node=node, b=b: e.tensor_scalar(
                        hb[0:TP, 0:ET], snB[0:TP, :], node[:, b:b + 1], None, ALU.is_equal), hfree, links)
                    for q in range(TB):
                        _, bank, free = banks[q]
                        mp = PE.do(lambda e, k=k, b=b, q=q, bank=bank, hb=hb: e.matmul(
                            bank[0:TP, :], hb[0:TP, q * TP:(q + 1) * TP], part[k][:, b, :],
                            start=(k == 0 and b == 0), stop=(k == 1 and b == TB - 1)), ms, mr, free)
                    wk.free[iw] = mp
            for q in range(TB):
                i, bank, _ = banks[q]
                k, sbuf, sfree = stg.take()
                me = dense.free[i] = ACTQ.do(lambda e, sbuf=sbuf, bank=bank: e.activation(sbuf[0:TP, :], bank[0:TP, :],
                                                                                          ACT.Copy), mp, sfree)
                stg.free[k] = sct_ch[k].send(POOL, lambda e, sbuf=sbuf, q=q: e.indirect_dma_start(
                    out=aggd[l][:, :], out_offset=bass.IndirectOffsetOnAxis(ap=runrow[:, q:q + 1], axis=0),
                    in_=sbuf[0:TP, :], in_offset=None, bounds_check=AGG_ROWS - 1, oob_is_err=False), me, runrow_m, stored)
            return [c.mark() for c in sct_ch], [mp, edges]

        st4 = st[:, :].rearrange("p (f c s) -> p f c s", f=4, c=7)

        def norm_coeffs(l, cg, cb, m):
            for f in range(4):
                m2 = DVE.do(lambda e, f=f: e.bn_aggr(out=mv[:, f, :], in_=st4[:, f, :, :]), m)
            sc, off = small[:, 0:4], small[:, 4:8]
            m = DVE.do(lambda e: e.tensor_scalar(sc, mv[:, 0:4, 1], EPS, None, ALU.add), m2)
            m = ACTQ.do(lambda e: e.activation(sc, sc, ACT.Sqrt), m)
            m = DVE.do(lambda e: e.reciprocal(sc, sc), m)
            m = DVE.do(lambda e: e.tensor_tensor(sc, sc, vec[:, cg + 4 * l:cg + 4 * l + 4], ALU.mult), m, ldv)
            m = DVE.do(lambda e: e.tensor_tensor(off, mv[:, 0:4, 0], sc, ALU.mult), m)
            return DVE.do(lambda e: e.tensor_tensor(off, vec[:, cb + 4 * l:cb + 4 * l + 4], off, ALU.subtract), m)

        def normalise(c, m):
            c0, cn = CHUNKS[c]
            for f in range(4):
                m2 = DVE.do(lambda e, f=f: e.tensor_scalar(xT[:, f, c0:c0 + cn], xT[:, f, c0:c0 + cn], small[:, f:f + 1],
                                                           small[:, 4 + f:5 + f], ALU.mult, ALU.add), m)
            return m2

        c_agg = [chan(f"c_agg{i}") for i in range(5)]

        def finish_layer(l, agg_ready, g_free, x_free, Wo, W1, W2, wready):
            aggT = [G[:, 0:4, :], G[:, 4:8, :]]
            rows = Ring([G[:, 8 + s, :] for s in range(4)])
            t_free = [None, None]
            got = {}

            def fetch(t):
                if t < NT:
                    s, buf, free = rows.take()
                    got[t] = (s, buf, load(c_agg[s], buf[0:ROWS[t], :], aggd[l][P * t:P * t + ROWS[t], :],
                                           agg_ready, g_free, free))

            for t in range(3):
                fetch(t)
            for c, (c0, cn) in enumerate(CHUNKS):
                dst = aggT[c % 2]
                for t in range(4 * c, min(4 * c + 4, NT)):
                    fetch(t + 3)
                    r = ROWS[t]
                    s, row, ml = got.pop(t)
                    it, bank, free = turn.take()
                    for f in range(4):
                        g = lambda e, f=f, bank=bank, row=row, r=r: e.transpose(
                            bank[:, f * P:f * P + r], row[0:r, f * P:(f + 1) * P], ident[0:r, 0:r])
                        if f < 3:
                            PE.quiet(g, free, ml)
                        else:
                            mp = PE.do(g)
                    rows.free[s] = mp
                    o0 = P * t - c0
                    bk = bank[:, :].rearrange("p (k n) -> p k n", k=4)
                    turn.free[it] = mt_ = ACTQ.do(lambda e, bk=bk, dst=dst, o0=o0, r=r: e.activation(
                        dst[:, :, o0:o0 + r], bk[:, :, 0:r], ACT.Copy), mp, t_free[c % 2], g_free)
                for f in range(4):
                    i, bank, free = dense.take()
                    for k in range(4):
                        g = lambda e, k=k, f=f, bank=bank, dst=dst, cn=cn: e.matmul(
                            bank[:, 0:cn], Wo[:, k, f * P:(f + 1) * P], dst[:, k, 0:cn], start=(k == 0), stop=(k == 3))
                        if k < 3:
                            PE.quiet(g, free, mt_, wready)
                        else:
                            mp = PE.do(g)
                    m = DVE.do(lambda e, f=f, bank=bank, c0=c0, cn=cn: e.scalar_tensor_tensor(
                        out=xT[:, f, c0:c0 + cn], in0=bank[:, 0:cn], scalar=vec[:, C_BO + 4 * l + f:C_BO + 4 * l + f + 1],
                        in1=xT[:, f, c0:c0 + cn], op0=ALU.add, op1=ALU.add), mp, x_free, ldv)
                    dense.free[i] = m
                    m = DVE.do(lambda e, f=f, c=c, c0=c0, cn=cn: e.bn_stats(out=st4[:, f, c, :], in_=xT[:, f, c0:c0 + cn]), m)
                t_free[c % 2] = mp
            co = norm_coeffs(l, C_G1, C_E1, m)
            g_done = mp
            nx = {0: normalise(0, co)}
            for c, (c0, cn) in enumerate(CHUNKS):
                if c + 1 < len(CHUNKS):
                    nx[c + 1] = normalise(c + 1, co)
                i, bank, free = dense.take()
                for k in range(4):
                    g = lambda e, k=k, bank=bank, c0=c0, cn=cn: e.matmul(
                        bank[:, 0:cn], W1[:, k, :], xT[:, k, c0:c0 + cn], start=(k == 0), stop=(k == 3))
                    if k < 3:
                        PE.quiet(g, free, nx[c])
                    else:
                        mp = PE.do(g)
                iw, hb, hfree = wk.take()
                mh = ACTQ.do(lambda e, bank=bank, hb=hb, cn=cn: e.activation(
                    hb[:, 0:cn], bank[:, 0:cn], ACT.Relu, bias=vec[:, C_B1 + l:C_B1 + l + 1]), mp, hfree)
                dense.free[i] = mh
                for f in range(4):
                    i, bank, free = dense.take()
                    mp = PE.do(lambda e, f=f, bank=bank, hb=hb, cn=cn: e.matmul(
                        bank[:, 0:cn], W2[:, f * P:(f + 1) * P], hb[:, 0:cn], start=True, stop=True), free, mh)
                    m = DVE.do(lambda e, f=f, bank=bank, c0=c0, cn=cn: e.scalar_tensor_tensor(
                        out=xT[:, f, c0:c0 + cn], in0=bank[:, 0:cn], scalar=vec[:, C_B2 + 4 * l + f:C_B2 + 4 * l + f + 1],
                        in1=xT[:, f, c0:c0 + cn], op0=ALU.add, op1=ALU.add), mp)
                    dense.free[i] = m
                    m = DVE.do(lambda e, f=f, c=c, c0=c0, cn=cn: e.bn_stats(out=st4[:, f, c, :], in_=xT[:, f, c0:c0 + cn]), m)
                wk.free[iw] = mp
            co = norm_coeffs(l, C_G2, C_E2, m)
            marks = [normalise(c, co) for c in range(len(CHUNKS))]
            return (lambda t: marks[t // 4]), g_done

        def load_layer(l, m):
            load(c_wa, WA[:, 0], kpo(A["WoT"][l]), m)
            load(c_wa, WA[:, 1].rearrange("p k (a o) -> p (k a) o", o=P)[:, 0:4, :], kpo(A["W1T"][l]), m)
            mk = load(c_wa, WA[:, 2, 0, :], A["W2T"][l], m)
            return WA[:, 0], WA[:, 1].rearrange("p k (a o) -> p (k a) o", o=P)[:, 0:4, :], WA[:, 2, 0, :], mk

        side = mix(lambda t: xT_ready[t], x_read, pre_read)
        edges, mark0 = attend(0, kv_ready + [zeroed], [link_m, x_read], side)
        for _ in side:
            pass
        mix_done, mix_ready = mix_end["done"], mix_end["stores"]
        dense.free = [mix_done] * 4
        Wl = load_layer(0, mix_done)
        Y3 = Y[:, 0:3 * 2048].rearrange("p (w k o) -> p w k o", w=3, k=4)
        wqkv1 = load_qkv(1, Y3, edges)
        agg_ready, g_ok = join(0, mark0, edges)
        row1 = load_row(0, A["gbq"][1], mix_done)
        x_ready, g_ok = finish_layer(0, agg_ready, g_ok, [x_read, mix_done], *Wl)
        kv_ready, x_read1 = qkv(1, Y3, wqkv1, x_ready, row1, 0)
        Wl = load_layer(1, x_read1)
        edges, mark0 = attend(1, kv_ready + [zeroed], [g_ok, x_read1], None)
        agg_ready, g_ok = join(1, mark0, edges)
        y_done = edges
        x_ready, g_done = finish_layer(1, agg_ready, g_ok, x_read1, *Wl)
        pv = [(PE.sem, PE.n), (DVE.sem, DVE.n)]

        rl = [load_row(1, A["ln_g"], agg_ready), load_row(2, A["ln_b"], agg_ready)][-1]
        Wm1 = G[:, 0:8, :].rearrange("p a b -> p (a b)").rearrange("p (k e f) -> p k e f", k=4, e=8)
        Wm2 = G[:, 8:16, :]
        for k in range(4):
            load(c_g, Wm1[:, k], A["EW1"][:, k * P:(k + 1) * P, :].rearrange("e p f -> p e f"), g_done)
        wmoe = load(c_g, Wm2, A["EW2"].rearrange("e f o -> f e o"), g_done)
        c_moe = chan("c_moe")
        wg = router[:, 0, 0:32].rearrange("p (k e) -> p k e", k=4)
        load(c_moe, wg, A["Wg"].rearrange("(k p) e -> p k e", p=P), g_done)
        load(c_moe, bgr, A["bg"].partition_broadcast(P), g_done)
        b2row = work[0:8, 0, :]
        rmoe = load(c_moe, b2row, A["Eb2"], (PE.sem, PE.n))

        tail = DVE.do(lambda e: e.memset(Yt[:, NT - 1, :], 0.0), x_read1, y_done)
        ymark = []
        for t in range(NT):
            r = ROWS[t]
            i, bank, free = turn.take()
            for k in range(4):
                f = lambda e, k=k, t=t, r=r, bank=bank: e.transpose(bank[0:r, k * P:(k + 1) * P], xT[:, k, P * t:P * t + r],
                                                                    ident[:, :])
                if k < 3:
                    PE.quiet(f, free, x_ready(t))
                else:
                    mp = PE.do(f)
            turn.free[i] = ACTQ.do(lambda e, t=t, r=r, bank=bank: e.activation(Yt[0:r, t, :], bank[0:r, :], ACT.Copy),
                                   mp, tail, y_done)
            ymark.append(turn.free[i])
        xT_free = mp
        xin = Ring([stage[:, s, :] for s in range(2)])
        min_ = Ring([stage[:, 2 + s, :] for s in range(2)])
        got = {}

        def fetch_res(t):
            if t < NT:
                r = ROWS[t]
                a, xb, xf = xin.take()
                b, mb_, mf = min_.take()
                got[t] = (a, xb, b, mb_, load(stg_ch[a], xb[0:r, :], A["x"][P * t:P * t + r, :], xf, agg_ready),
                          load(stg_ch[2 + b], mb_[0:r, :], mixd[P * t:P * t + r, :], mf, mix_ready, agg_ready))

        fetch_res(0)
        fetch_res(1)
        x2 = [None] * NT
        for tiles in groups:
            m = ln_stats(tiles, lambda t: ymark[t])
            for t in tiles:
                r = ROWS[t]
                a, xb, b, mb_, la, lb = got.pop(t)
                m1 = POOL.do(lambda e, xb=xb, mb_=mb_, r=r: e.tensor_tensor(xb[0:r, :], xb[0:r, :], mb_[0:r, :], ALU.add),
                             la, lb)
                min_.free[b] = m1
                m1 = POOL.do(lambda e, xb=xb, r=r: e.tensor_tensor(xb[0:r, :], xb[0:r, :], rowsb[0:r, 2, :], ALU.add), m1, rl)
                m2 = DVE.do(lambda e, t=t, r=r: e.scalar_tensor_tensor(
                    out=Yt[0:r, t, :], in0=Yt[0:r, t, :], scalar=mv[0:r, t, 0:1], in1=rowsb[0:r, 1, :],
                    op0=ALU.subtract, op1=ALU.mult), m, rl)
                x2[t] = DVE.do(lambda e, t=t, r=r, xb=xb: e.scalar_tensor_tensor(
                    out=Yt[0:r, t, :], in0=Yt[0:r, t, :], scalar=rs[0:r, t:t + 1], in1=xb[0:r, :],
                    op0=ALU.mult, op1=ALU.add), m2, m1)
                xin.free[a] = x2[t]
                fetch_res(t + 2)
        wk.free = [(PE.sem, PE.n)] * 3
        fx = Ring([work[:, 1 + s, :] for s in range(2)])
        fx.free = [(PE.sem, PE.n)] * 2
        xf_ready = [None] * NT
        for tiles in groups:
            m = ln_stats(tiles, lambda t: x2[t])
            for t in tiles:
                i, buf, free = fx.take()
                mn = DVE.do(lambda e, t=t, buf=buf: e.tensor_scalar(buf, Yt[:, t, :], mv[:, t, 0:1], rs[:, t:t + 1],
                                                                    ALU.subtract, ALU.mult), m, free)
                xf_ready[t], fx.free[i] = to_features(t, buf, mn, xT_free)

        lgb = PS[6]
        mz = DVE.do(lambda e: e.memset(lgb[:, 0:200], 0.0), edge.free)
        for t in range(NT):
            r = ROWS[t]
            for k in range(4):
                f = lambda e, k=k, t=t, r=r: e.matmul(lgb[0:r, 8 * t:8 * t + 8], xT[:, k, P * t:P * t + r], wg[:, k, :],
                                                      start=(k == 0), stop=(k == 3))
                if k < 3:
                    PE.quiet(f, xf_ready[t], rmoe, mz)
                else:
                    mp = PE.do(f)
        pr, ta, tb_, tc, comb = (router[:, 1 + s, :].rearrange("p (t e) -> p t e", t=NT) for s in range(5))
        one = small[:, 0:NT]
        wide = lambda: one.unsqueeze(2).to_broadcast([P, NT, 8])
        lg3 = lgb[:, 0:200].rearrange("p (t e) -> p t e", t=NT)

        def tt(o, a, b, op, *marks):
            return DVE.do(lambda e: e.tensor_tensor(o, a, b, op), *marks)

        def red(a, op, *marks):
            return DVE.do(lambda e: e.tensor_reduce(one, a, AXX, op), *marks)

        m = tt(pr, lg3, bgr.unsqueeze(1).to_broadcast([P, NT, 8]), ALU.add, mp)
        m = red(pr, ALU.max, m)
        m = tt(pr, pr, wide(), ALU.subtract, m)
        m = ACTQ.do(lambda e: e.activation(pr, pr, ACT.Exp), m)
        m = red(pr, ALU.add, m)
        m = DVE.do(lambda e: e.reciprocal(one, one), m)
        m = tt(pr, pr, wide(), ALU.mult, m)
        kx = POOL.do(lambda e: e.iota(tc, pattern=[[0, NT], [-1, 8]], base=8, channel_multiplier=0,
                                      allow_small_or_imprecise_dtypes=True))
        m = DVE.do(lambda e: e.tensor_copy(ta, pr), m)
        for turn_no in range(2):
            m = red(ta, ALU.max, m)
            m = tt(tb_, ta, wide(), ALU.is_equal, m)
            m = tt(tb_, tb_, tc, ALU.mult, m, kx)
            m = red(tb_, ALU.max, m)
            m = tt(tb_, tc, wide(), ALU.is_equal, m)
            if turn_no == 0:
                m = DVE.do(lambda e: e.tensor_copy(comb, tb_), m)
                m = DVE.do(lambda e: e.scalar_tensor_tensor(out=ta, in0=tb_, scalar=-4.0, in1=ta, op0=ALU.mult, op1=ALU.add), m)
        m = tt(comb, comb, tb_, ALU.add, m)
        cm = tt(comb, comb, pr, ALU.mult, m)

        cT = WA[0:8].rearrange("p w k o -> p (w k o)")[:, 2048:2048 + N]
        for t in range(NT):
            r = ROWS[t]
            i, bank, free = turn.take()
            mp = PE.do(lambda e, t=t, r=r, bank=bank: e.transpose(bank[0:8, 0:r], comb[0:r, t, :], ident[0:r, 0:r]), free, cm)
            turn.free[i] = mc = ACTQ.do(lambda e, t=t, r=r, bank=bank: e.activation(cT[:, P * t:P * t + r], bank[0:8, 0:r],
                                                                                    ACT.Copy), mp, pv)
        hid = Ring([mt[:, 512 * s:512 * (s + 1)] for s in range(4)])
        hid.free = [(PE.sem, PE.n)] * 4
        c_out = [chan(f"c_out{i}") for i in range(4)]
        acc = list(x2)
        for c, (c0, cn) in enumerate(CHUNKS):
            tiles = range(4 * c, min(4 * c + 4, NT))
            for t in tiles:
                r = ROWS[t]
                i, bank, free = dense.take()
                mp = PE.do(lambda e, t=t, r=r, bank=bank: e.matmul(bank[0:r, :], cT[:, P * t:P * t + r], b2row,
                                                                   start=True, stop=True), free, mc, rmoe)
                acc[t] = dense.free[i] = DVE.do(lambda e, t=t, r=r, bank=bank: e.tensor_tensor(
                    Yt[0:r, t, :], bank[0:r, :], Yt[0:r, t, :], ALU.add), mp, acc[t])
            for x in range(8):
                i, bank, free = dense.take()
                for k in range(4):
                    f = lambda e, k=k, x=x, bank=bank, c0=c0, cn=cn: e.matmul(
                        bank[:, 0:cn], Wm1[:, k, x, :], xT[:, k, c0:c0 + cn], start=(k == 0), stop=(k == 3))
                    if k < 3:
                        PE.quiet(f, free, wmoe, [xf_ready[t] for t in tiles])
                    else:
                        mp = PE.do(f)
                ih, hb, hfree = hid.take()
                mh = dense.free[i] = ACTQ.do(lambda e, x=x, bank=bank, hb=hb, cn=cn: e.activation(
                    hb[:, 0:cn], bank[:, 0:cn], ACT.Gelu_apprx_tanh, bias=vec[:, C_MB1 + x:C_MB1 + x + 1]), mp, hfree)
                for t in tiles:
                    r, o0 = ROWS[t], P * t - c0
                    i, bank, free = dense.take()
                    mp = PE.do(lambda e, x=x, r=r, o0=o0, bank=bank, hb=hb: e.matmul(
                        bank[0:r, :], hb[:, o0:o0 + r], Wm2[:, x, :], start=True, stop=True), free, mh)
                    acc[t] = dense.free[i] = DVE.do(lambda e, t=t, x=x, r=r, bank=bank: e.scalar_tensor_tensor(
                        out=Yt[0:r, t, :], in0=bank[0:r, :], scalar=comb[0:r, t, x:x + 1], in1=Yt[0:r, t, :],
                        op0=ALU.mult, op1=ALU.add), mp, acc[t])
                hid.free[ih] = mp
            for t in tiles:
                r = ROWS[t]
                load(c_out[t % 4], out[P * t:P * t + r, :], Yt[0:r, t, :], acc[t])
        SP.wait(*[c.mark() for c in c_out])
        SP.wait(*[c.mark() for c in stg_ch])


def kernel(**inputs):
    import numpy as np
    import concourse.bacc as bacc
    from concourse.bass_utils import run_bass_kernel_spmd

    a = {k: np.asarray(v) for k, v in inputs.items()}
    t = lambda w: np.ascontiguousarray(np.swapaxes(w, -1, -2))
    cols = lambda v: np.concatenate([x.reshape(4, P).T for x in v], axis=1)
    it = a["dst"].dtype
    arrays = {
        "x": a["x"],
        "src": np.concatenate([a["src"], np.zeros(EP - NE, a["src"].dtype)]),
        "dst": np.concatenate([np.full(1, -1, it), a["dst"], np.full(EP - NE, N, it), np.full(1, N + 1, it)]),
        "WqT": t(a["L0_gnn_Wq"]), "WkT": t(a["L0_gnn_Wk"]), "WvT": t(a["L0_gnn_Wv"]), "WoT": t(a["L0_gnn_Wo"]),
        "W1T": t(a["L0_gnn_W1"]), "W2T": t(a["L0_gnn_W2"]), "gbq": a["L0_gnn_bq"],
        "MqT": t(a["L0_mix_Wq"]), "MkT": t(a["L0_mix_Wk"]), "MvT": t(a["L0_mix_Wv"]), "MpT": t(a["L0_mix_Wp"]),
        "mbq": a["L0_mix_bq"], "mbk": a["L0_mix_bk"], "mbv": a["L0_mix_bv"], "mbp": a["L0_mix_bp"],
        "ln_g": a["L0_gnn_ln_g"], "ln_b": a["L0_gnn_ln_b"],
        "Wg": a["L0_ffn_Wg"], "bg": a["L0_ffn_bg"], "EW1": a["L0_ffn_W1"], "EW2": a["L0_ffn_W2"], "Eb2": a["L0_ffn_b2"],
        "vec": np.concatenate([cols(a["L0_gnn_" + n]) for n in ("bo", "b2", "g1", "beta1", "g2", "beta2")]
                              + [a["L0_gnn_b1"].T, a["L0_ffn_b1"].T], axis=1),
    }
    nc = bacc.Bacc("TRN2", target_bir_lowering=False, num_devices=1)
    feed, A = {}, {}
    for name, v in arrays.items():
        v = np.ascontiguousarray(v)
        feed["in_" + name] = v
        A[name] = nc.dram_tensor("in_" + name, v.shape, mybir.dt.from_np(v.dtype), kind="ExternalInput").ap()
    out = nc.dram_tensor("out", (N, D), F32, kind="ExternalOutput").ap()
    build(nc, A, out)
    r = run_bass_kernel_spmd(nc, [feed], core_ids=[0])
    return r.results[0]["out"]
```

```python
from contextlib import ExitStack

import concourse.bass as bass
from concourse import mybir

P = 128
N, D, H, DH = 3125, 512, 8, 64
NT = 25
ROWS = [min(P, N - P * t) for t in range(NT)]
CHUNKS = [(c, min(512, N - c)) for c in range(0, N, 512)]
NE = 53125
ET = 416
EP = ET * P
NCH = 8
NJ = ET // NCH
CH = NJ * P
SEQ = 2 * NJ
HC = H * NCH
TB, TP = 4, 104
AGG_F = 3200
AGG_L = AGG_F + ET
AGG_ROWS = AGG_L + ET
KV, LAG, AHEAD = 14, 10, 3
PACK, CAP = 4, 32
FAR = 8192.0
BIG = 1.0e30
EPS = 1e-5

F32 = mybir.dt.float32
F32R = mybir.dt.float32r
I32 = mybir.dt.int32
U32 = mybir.dt.uint32
ALU = mybir.AluOpType
ACT = mybir.ActivationFunctionType
AXX = mybir.AxisListType.X

C_BO, C_B2, C_G1, C_E1, C_G2, C_E2, C_B1, C_MB1 = 0, 8, 16, 24, 32, 40, 48, 50


class Queue:

    def __init__(self, engine, sem):
        self.engine, self.sem, self.n, self.seen = engine, sem, 0, {}

    def wait(self, *marks):
        for m in marks:
            if m is None:
                continue
            if isinstance(m, list):
                self.wait(*m)
                continue
            sem, v = m
            if self.seen.get(id(sem), 0) < v:
                self.seen[id(sem)] = v
                self.engine.wait_ge(sem, v)

    def do(self, f, *marks):
        self.wait(*marks)
        self.n += 1
        f(self.engine).then_inc(self.sem, 1)
        return (self.sem, self.n)

    def quiet(self, f, *marks):
        self.wait(*marks)
        f(self.engine)


class Chan:

    def __init__(self, sem):
        self.sem, self.n = sem, 0

    def mark(self):
        return (self.sem, self.n) if self.n else None

    def send(self, queue, f, *marks):
        queue.wait(*marks)
        self.n += 16
        f(queue.engine).then_inc(self.sem, 16)
        return (self.sem, self.n)


class Ring:

    def __init__(self, bufs):
        self.bufs, self.free, self.at = bufs, [None] * len(bufs), 0

    def take(self):
        i = self.at % len(self.bufs)
        self.at += 1
        return i, self.bufs[i], self.free[i]


def build(nc, A, out):
    with ExitStack() as ctx:
        def sb(name, shape, dt=F32):
            return ctx.enter_context(nc.sbuf_tensor(name, shape, dt))

        def sem(name):
            return ctx.enter_context(nc.semaphore(name))

        def chan(name):
            return Chan(sem(name))

        def dram(name, shape):
            return nc.dram_tensor(name, shape, F32, kind="Internal").ap()

        PE, DVE, ACTQ, POOL, SP = (
            Queue(e, sem(n)) for e, n in ((nc.tensor, "s_pe"), (nc.vector, "s_dve"), (nc.scalar, "s_act"),
                                          (nc.gpsimd, "s_pool"), (nc.sync, "s_sp")))

        xT = sb("xT", [P, 4, N])
        mt = sb("mt", [P, 3072])
        stage = sb("stage", [P, 4, 512])
        work = sb("work", [P, 3, 512])
        rowsb = sb("rowsb", [P, 4, 512])
        ordE = sb("ordE", [P, ET])
        fvE = sb("fvE", [P, ET])
        nfE = sb("nfE", [P, ET])
        srcE = sb("srcE", [P, ET], U32)
        dstE = sb("dstE", [P, ET], U32)
        segE = sb("segE", [P, ET // PACK], U32)
        segS = sb("segS", [P, 2], U32)
        ident = sb("ident", [P, P])
        iota = sb("iota", [P, P])
        onehot = sb("onehot", [P, 10, P])
        zero = work[:, 2, :]
        ones = sb("ones", [P, 1])
        vec = sb("vec", [P, 58])
        bnd = sb("bnd", [TP, 7, TB])
        crowd = sb("crowd", [TP, 4])
        flag = sb("flag", [1, 1], I32)
        runrow = sb("runrow", [TP, TB], U32)
        dnx = sb("dnx", [TP, TB, 2], I32)
        scores = sb("scores", [P, 2, HC])
        firsts = sb("firsts", [P, HC])
        same = sb("same", [HC, P + 1])
        fixm = sb("fixm", [HC, NJ, 2])
        fixl = sb("fixl", [HC, NJ, 2])
        link = sb("link", [HC, SEQ + 1])
        maskC = sb("maskC", [HC, NCH])
        selH = sb("selH", [HC, H])
        iotaT = sb("iotaT", [TP, TB])
        st = sb("st", [P, 4 * 7 * 6])
        mv = sb("mv", [P, NT, 2])
        rs = sb("rs", [P, NT])
        small = sb("small", [P, 64])
        linkp = mt[0:HC, 512:512 + SEQ + 1]
        ends = rowsb[0:HC, 3, 0:2 * NJ + 2].bitcast(I32).rearrange("p (j k) -> p j k", k=2)
        pen = st[0:HC, 0:P + 1]
        rows1 = rowsb[0:1, 1:3, :].rearrange("a s (q p) -> a (s q) p", p=HC)
        area = ctx.enter_context(ExitStack())
        tensor = lambda name, shape, dt=F32: area.enter_context(nc.sbuf_tensor(name, shape, dt))
        Wh0 = tensor("Wh0", [P, 3, 4, 512], F32R)
        Y = tensor("Y0", [P, 12800])
        Wl0 = tensor("Wl0", [P, 3, 4, 512], F32R)
        xs0 = tensor("xs0", [P, 2, 2, 4, P], F32R)
        Yt = Y[:, :].rearrange("p (t d) -> p t d", t=NT)

        def views(Y, G):
            kvs = [Y[:, 1024 * i:1024 * (i + 1)] for i in range(12)] + [
                G[:, 6 + 2 * i:8 + 2 * i, :].rearrange("p a b -> p (a b)") for i in range(2)]
            scan = [Y[0:HC, 12288 + P * i:12288 + P * (i + 1)] for i in range(3)]
            return (Y[:, :].rearrange("p (t d) -> p t d", t=NT), kvs, *scan,
                    Y[:, 12672:12800].rearrange("p (s q) -> p s q", s=2))

        PS = [ctx.enter_context(nc.psum_tensor(f"ps{i}", [P, 512], F32)) for i in range(8)]

        KVd = [dram(f"KVd{l}", [N, 2 * D]) for l in range(2)]
        Qd = [dram(f"Qd{l}", [AGG_F, D]) for l in range(2)]
        aggd = [dram(f"aggd{l}", [AGG_ROWS, D]) for l in range(2)]
        mixd = dram("mixd", [N, D])
        Wd = [dram(f"Wd{l}", [NJ, P, HC]) for l in range(2)]

        dense = Ring([PS[i] for i in range(4)])
        turn = Ring([PS[4], PS[5]])
        edge = Ring([PS[6], PS[7]])
        stg = Ring([stage[:, i, :] for i in range(4)])
        stg_ch = [chan(f"c_stg{i}") for i in range(4)]

        def load(ch, dst, src, *marks):
            return ch.send(SP, lambda e: e.dma_start(dst, src), *marks)

        z0 = DVE.do(lambda e: e.memset(zero, 0.0))
        on0 = DVE.do(lambda e: e.memset(ones[:, :], 1.0))
        xpad = DVE.do(lambda e: e.memset(Yt[:, NT - 1, :], 0.0))
        m0 = POOL.do(lambda e: e.memset(ident[:, :], 0.0))
        idm = POOL.do(lambda e: e.affine_select(out=ident[:, :], in_=ident[:, :], compare_op=ALU.not_equal, fill=1.0,
                                                base=0, pattern=[[-1, P]], channel_multiplier=1), m0)
        iom = POOL.do(lambda e: e.iota(iota[:, :], pattern=[[1, P]], base=0, channel_multiplier=0,
                                       allow_small_or_imprecise_dtypes=True))
        iotm = POOL.do(lambda e: e.iota(iotaT[:, :], pattern=[[TP, TB]], base=AGG_F, channel_multiplier=1,
                                        allow_small_or_imprecise_dtypes=True))

        off_p = crowd[:, 0:1]
        offm = POOL.do(lambda e: e.iota(off_p, pattern=[[0, 1]], base=0, channel_multiplier=1,
                                        allow_small_or_imprecise_dtypes=True))

        xc = [chan(f"c_x{g}") for g in range(5)]
        xld = []
        for g in range(4):
            src = A["x"][0:3072, :].rearrange("(t p) d -> p t d", p=P)[:, 6 * g:6 * g + 6, :]
            xld.append(load(xc[g], Yt[:, 6 * g:6 * g + 6, :], src))
        load(xc[4], Yt[0:48, 24, :], A["x"][3072:3120, :], xpad)
        xld.append(load(xc[4], Yt[48:53, 24, :], A["x"][3120:3125, :], xpad))
        xtile = [xld[min(t // 6, 4)] for t in range(NT)]

        c_pre = [chan(f"c_pre{i}") for i in range(3)]
        pre = mt[:, :].rearrange("p (s b e) -> p s b e", s=6, b=TB)
        tm = lambda ap: ap.rearrange("(b p e) -> p b e", b=TB, p=TP)
        ld_d = load(c_pre[0], pre[0:TP, 0].bitcast(I32), tm(A["dst"][1:1 + EP]))
        ld_p = load(c_pre[1], pre[0:TP, 1].bitcast(I32), tm(A["dst"][0:EP]))
        ld_s = load(c_pre[2], pre[0:TP, 2].bitcast(I32), tm(A["src"][0:EP]))
        c_nx = chan("c_nx")
        nxt = A["dst"][P:P + 2]
        ld_n = load(c_nx, dnx[:, :, :], bass.AP(nxt.tensor, nxt.offset, [[P, TP], [P * TP, TB], [1, 2]]))
        c_scan = chan("c_scan")
        for h in range(H):
            src = A["dst"][0:CH + 2]
            src = bass.AP(src.tensor, src.offset, [[CH, NCH], [P, NJ + 1], [1, 2]])
            ld_q = load(c_scan, ends[h * NCH:(h + 1) * NCH, :, :], src)

        c_vec, c_wa, c_g, c_row = chan("c_vec"), chan("c_wa"), chan("c_g"), chan("c_row")
        ldv = load(c_vec, vec[:, :], A["vec"])
        kpo = lambda ap: ap.rearrange("(k p) o -> p k o", p=P)

        def load_qkv(l, dst, *marks):
            for i, w in enumerate(("WqT", "WkT", "WvT")):
                m = load(c_wa, dst[:, i], kpo(A[w][l]), *marks)
            return m

        def load_row(i, src, *marks):
            return load(c_row, rowsb[:, i, :], src.partition_broadcast(P), *marks)

        rowm = load_row(0, A["gbq"][0])
        def ln_stats(tiles, ready):
            a, b = tiles[0], tiles[-1] + 1
            for t in tiles:
                m = DVE.do(lambda e, t=t: e.bn_stats(out=st[:, 6 * (t % 25):6 * (t % 25) + 6], in_=Yt[:, t, :]), ready(t))
            for t in tiles:
                m2 = DVE.do(lambda e, t=t: e.bn_aggr(out=mv[:, t, :], in_=st[:, 6 * (t % 25):6 * (t % 25) + 6]), m)
            m = DVE.do(lambda e: e.tensor_scalar(rs[:, a:b], mv[:, a:b, 1], EPS, None, ALU.add), m2)
            m = ACTQ.do(lambda e: e.activation(rs[:, a:b], rs[:, a:b], ACT.Sqrt), m)
            return DVE.do(lambda e: e.reciprocal(rs[:, a:b], rs[:, a:b]), m)

        def to_features(t, src, ready, dst_free):
            r = ROWS[t]
            i, bank, free = turn.take()
            for k in range(4):
                f = lambda e, k=k: e.transpose(bank[:, k * P:k * P + r], src[0:r, k * P:(k + 1) * P], ident[0:r, 0:r])
                if k < 3:
                    PE.quiet(f, free, ready, idm)
                else:
                    m = PE.do(f)
            bk = bank[:, :].rearrange("p (k n) -> p k n", k=4)
            turn.free[i] = ACTQ.do(lambda e: e.activation(xT[:, :, P * t:P * t + r], bk[:, :, 0:r], ACT.Copy), m, dst_free)
            return turn.free[i], m

        def split(raw, hi, lo, *marks):
            m = ACTQ.do(lambda e: e.activation(hi, raw, ACT.Copy), *marks)
            return DVE.do(lambda e: e.tensor_tensor(lo, raw, hi.bitcast(F32), ALU.subtract), m)

        raw_free = [None] * 4

        def fetch_raw(n):
            w, k = n // 4, n % 4
            return load(stg_ch[n % 4], stage[:, n % 4, :], A[("WqT", "WkT", "WvT")[w]][0, k * P:(k + 1) * P, :], raw_free[n % 4])

        raw_in = [fetch_raw(n) for n in range(4)]
        groups = [list(range(6 * g, min(6 * g + 6, NT))) for g in range(5)]
        xT_ready = [None] * NT
        for tiles in groups:
            m = ln_stats(tiles, lambda t: [xtile[t], xpad])
            for t in tiles:
                mn = DVE.do(lambda e, t=t: e.tensor_scalar(Yt[:, t, :], Yt[:, t, :], mv[:, t, 0:1], rs[:, t:t + 1],
                                                           ALU.subtract, ALU.mult), m)
                xT_ready[t], y_read = to_features(t, Yt[:, t, :], mn, None)
            if tiles[0] == 6:
                for n in range(12):
                    w, k = n // 4, n % 4
                    raw_free[k] = w_ready = split(stage[:, k, :], Wh0[:, w, k, :], Wl0[:, w, k, :], raw_in[k])
                    if n < 8:
                        raw_in[k] = fetch_raw(n + 4)
        stg.free = list(raw_free)
        c_zero = chan("c_zero")
        for l in range(2):
            load(c_zero, aggd[l][0:3968, :].rearrange("(t p) d -> p t d", p=P),
                 zero.unsqueeze(1).to_broadcast([P, 31, 512]), z0)
            load(c_zero, aggd[l][3968:AGG_ROWS, :], zero[0:AGG_ROWS - 3968, :], z0)
            zeroed = load(c_zero, Qd[l][N:AGG_F, :], zero[0:AGG_F - N, :], z0)


        pf = pre
        d_i, p_i, s_i = pf[0:TP, 0].bitcast(I32), pf[0:TP, 1].bitcast(I32), pf[0:TP, 2].bitcast(I32)
        sm_t, nf_t, or_t, df_t = pf[0:TP, 3], pf[0:TP, 4], pf[0:TP, 5], pf[0:TP, 0]
        w0 = work[0:TP, 0, :].rearrange("p (b e) -> p b e", b=TB)
        w1 = work[0:TP, 1, :].rearrange("p (b e) -> p b e", b=TB)
        m = DVE.do(lambda e: e.tensor_tensor(sm_t, d_i, p_i, ALU.is_equal), ld_d, ld_p)
        m2 = DVE.do(lambda e: e.tensor_copy(w0, d_i))
        ws = DVE.do(lambda e: e.tensor_copy(w1, s_i), ld_s)
        m = DVE.do(lambda e: e.tensor_scalar(nf_t, sm_t, -1.0, 1.0, ALU.mult, ALU.add), m)
        m = DVE.do(lambda e: e.memset(nf_t[:, :, 0], 0.0), m)
        for b in range(TB):
            mo = DVE.do(lambda e, b=b: e.tensor_tensor_scan(or_t[:, b, :], nf_t[:, b, :], nf_t[:, b, :], 0.0,
                                                            ALU.add, ALU.max), m)
        mnf = DVE.do(lambda e: e.memset(nf_t[:, :, 0], 1.0), mo)
        nodeF, nodeL, goes, toL, start, t0, t1 = (bnd[:, i, :] for i in range(7))
        came = sm_t[:, :, 0]
        DVE.do(lambda e: e.tensor_copy(nodeF, w0[:, :, 0]), m2)
        mb = DVE.do(lambda e: e.tensor_copy(nodeL, w0[:, :, P - 1]))
        mg = DVE.do(lambda e: e.tensor_tensor(goes, dnx[:, :, 0], dnx[:, :, 1], ALU.is_equal), ld_n)
        m3 = DVE.do(lambda e: e.scalar_tensor_tensor(out=toL, in0=iotaT[:, :], scalar=float(ET), in1=nodeL,
                                                     op0=ALU.add, op1=ALU.subtract), mb, iotm)
        m3 = DVE.do(lambda e: e.tensor_tensor(toL, toL, goes, ALU.mult), m3, mg)
        for b in range(TB):
            m4 = DVE.do(lambda e, b=b: e.tensor_scalar(df_t[:, b, :], w0[:, b, :], nodeL[:, b:b + 1], toL[:, b:b + 1],
                                                       ALU.is_equal, ALU.mult), m3)
        m4 = DVE.do(lambda e: e.tensor_tensor(df_t, df_t, w0, ALU.add), m4)
        m3 = DVE.do(lambda e: e.tensor_tensor(t0, iotaT[:, :], df_t[:, :, 0], ALU.subtract), m4)
        m3 = DVE.do(lambda e: e.tensor_tensor(t0, t0, came, ALU.mult), m3)
        m3 = DVE.do(lambda e: e.tensor_tensor(df_t[:, :, 0], df_t[:, :, 0], t0, ALU.add), m3)
        fv_t = pf[0:TP, 1]
        m3 = DVE.do(lambda e: e.scalar_tensor_tensor(out=fv_t, in0=df_t, scalar=FAR, in1=nf_t,
                                                     op0=ALU.subtract, op1=ALU.mult), m3, mnf)
        m5 = DVE.do(lambda e: e.tensor_tensor(t1, nodeF, nodeL, ALU.is_equal), mb)
        m5 = DVE.do(lambda e: e.tensor_tensor(t1, t1, came, ALU.mult), m5)
        m5 = DVE.do(lambda e: e.tensor_tensor(t1, t1, goes, ALU.mult), m5, mg)
        m5 = DVE.do(lambda e: e.tensor_tensor(t1, goes, t1, ALU.subtract), m5)
        m6 = DVE.do(lambda e: e.scalar_tensor_tensor(out=start, in0=nodeL, scalar=5.0, in1=t1, op0=ALU.add, op1=ALU.mult), m5)
        start_m = DVE.do(lambda e: e.tensor_scalar(start, start, -5.0, None, ALU.add), m6)
        m6 = DVE.do(lambda e: e.scalar_tensor_tensor(out=t0, in0=nodeL, scalar=FAR, in1=t1, op0=ALU.subtract, op1=ALU.mult),
                    m5, m3)
        runrow_m = DVE.do(lambda e: e.tensor_scalar(runrow[:, :], t0, FAR, None, ALU.add), m6)
        DVE.do(lambda e: e.tensor_tensor(link[:, 0:SEQ + 1:2], ends[:, :, 0], ends[:, :, 1], ALU.is_equal), ld_q)
        link_m = DVE.do(lambda e: e.tensor_tensor(link[:, 1:SEQ:2], ends[:, 0:NJ, 1], ends[:, 1:NJ + 1, 0], ALU.is_equal))
        idr = ident[0:HC, 0:HC]
        DVE.do(lambda e: e.tensor_reduce(maskC[:, :], idr.rearrange("p (h c) -> p c h", h=H), AXX, ALU.add), idm)
        mask_m = DVE.do(lambda e: e.tensor_reduce(selH[:, :], idr.rearrange("p (h c) -> p h c", h=H), AXX, ALU.add))
        gate_m = DVE.do(lambda e: e.memset(same[:, P:P + 1], 0.0))
        m7 = DVE.do(lambda e: e.tensor_scalar(off_p, off_p, float(NJ), float(CAP), ALU.is_ge, ALU.mult), offm)
        m8 = DVE.do(lambda e: e.tensor_reduce(crowd[:, 1:2], or_t, mybir.AxisListType.XY, ALU.max), mo)
        w2 = pf[0:TP, 2]
        m9 = DVE.do(lambda e: e.tensor_scalar(w2, or_t, float(CAP), 1000.0, ALU.is_ge, ALU.mult), mo, ws)
        m9 = DVE.do(lambda e: e.tensor_tensor(or_t, or_t, w2, ALU.add), m8, m9)
        for b in range(TB):
            m3 = DVE.do(lambda e, b=b: e.tensor_scalar(or_t[:, b, :], or_t[:, b, :], off_p, float(2 * CAP * (b % 2)),
                                                       ALU.add, ALU.add), m9, m7, m3)
        i, bank, free = turn.take()
        mp = PE.do(lambda e, bank=bank: e.transpose(bank[0:1, 0:TP], crowd[:, 1:2], ident[0:TP, 0:TP]), m8, idm, free)
        turn.free[i] = mfl = DVE.do(lambda e, bank=bank: e.tensor_reduce(crowd[0:1, 2:3], bank[0:1, 0:TP], AXX, ALU.max), mp)
        flag_m = DVE.do(lambda e: e.tensor_scalar(flag[:, :], crowd[0:1, 2:3], float(CAP), None, ALU.is_ge), mfl)
        pre_done = []
        for srct, dstt in ((or_t, ordE), (fv_t, fvE), (nf_t, nfE), (w1, srcE), (w0, dstE)):
            i, bank, free = turn.take()
            for b in range(TB):
                f = lambda e, b=b, srct=srct, bank=bank: e.transpose(bank[:, b * TP:(b + 1) * TP], srct[:, b, :],
                                                                     ident[0:TP, 0:TP])
                if b < 3:
                    PE.quiet(f, free, m3, idm)
                else:
                    mp = PE.do(f)
            turn.free[i] = ACTQ.do(lambda e, bank=bank, dstt=dstt: e.activation(dstt[:, :], bank[:, 0:ET], ACT.Copy), mp)
            pre_done.append(turn.free[i])
        idx_ready = pre_done[-1]
        pre_read = mp

        def qkv(l, wready, xready, rowm, brow, parts, free_x=None):
            bs = DVE.do(lambda e: e.tensor_scalar(rowsb[:, brow, :], rowsb[:, brow, :], 0.125, None, ALU.mult), rowm)
            Wh, Wl, xbufs = parts
            xs = Ring(xbufs)
            xs.free = [free_x] * len(xbufs)
            cut = {}

            def cut_x(t):
                if t < NT:
                    i, (xh, xl), free = xs.take()
                    r = ROWS[t]
                    cut[t] = (i, xh, xl, split(xT[:, :, P * t:P * t + r], xh[:, :, 0:r], xl[:, :, 0:r], xready(t), free))

            cut_x(0)
            for t in range(NT):
                r = ROWS[t]
                cut_x(t + 1)
                for w, table in ((0, Qd[l]), (1, KVd[l][:, 0:D]), (2, KVd[l][:, D:2 * D])):
                    ix, xh, xl, xm = cut[t]
                    i, bank, free = dense.take()
                    terms = [(a, b, k) for k in range(4) for a, b in ((xh, Wh), (xh, Wl), (xl, Wh))]
                    for n, (a, b, k) in enumerate(terms):
                        f = lambda e, a=a, b=b, k=k, n=n, bank=bank, r=r, w=w: e.matmul(
                            bank[0:r, :], a[:, k, 0:r], b[:, w, k, :], start=(n == 0), stop=(n == 11))
                        if n < 11:
                            PE.quiet(f, free, wready, xm)
                        else:
                            m = xs.free[ix] = PE.do(f)
                    s, buf, _ = stg.take()
                    gone = stg_ch[s].mark()
                    if w == 0:
                        m = DVE.do(lambda e, bank=bank, buf=buf, r=r: e.scalar_tensor_tensor(
                            out=buf[0:r, :], in0=bank[0:r, :], scalar=0.125, in1=rowsb[0:r, brow, :],
                            op0=ALU.mult, op1=ALU.add), m, gone, bs, stg.free[s])
                    else:
                        m = ACTQ.do(lambda e, bank=bank, buf=buf, r=r: e.activation(buf[0:r, :], bank[0:r, :], ACT.Copy),
                                    m, gone, stg.free[s])
                    dense.free[i] = m
                    stg.free[s] = load(stg_ch[s], table[P * t:P * t + r, :], buf[0:r, :], m)
            return [c.mark() for c in stg_ch], (PE.sem, PE.n)

        parts0 = (Wh0, Wl0, [(xs0[:, u, 0], xs0[:, u, 1]) for u in range(2)])
        kv_ready, x_read = qkv(0, w_ready, lambda t: xT_ready[t], rowm, 0, parts0)
        area.close()
        WA = sb("WA", [P, 3, 4, 512])
        bgr = WA[:, 0].rearrange("p k o -> p (k o)")[:, 1200:1208]
        router = WA[:, 0].rearrange("p k o -> p (k o)")[:, 0:1200].rearrange("p (s e) -> p s e", s=6)
        Y, G = tensor("Y1", [P, 12800]), tensor("G1", [P, 16, 512])
        Yt, kvs, sA, sB, sC, wts = views(Y, G)

        h8 = lambda ap: ap.rearrange("p (h d) -> p h d", h=H)
        mix_end = {}

        def mix(xready, wa_free, mt_free):
            rows = [load_row(i, A[b], (DVE.sem, DVE.n)) for i, b in enumerate(("mbq", "mbk", "mbv", "mbp"))][-1]
            for i, w in enumerate(("MkT", "MvT", "MqT")):
                load(c_wa, WA[:, i], kpo(A[w]), wa_free)
            wm = [c_wa.mark(), load(c_g, G[:, 12:16, :], kpo(A["MpT"]), wa_free)]
            prod = Ring([PS[0], PS[1]])
            prod.free = [dense.free[0], dense.free[1]]
            acc = [PS[2], PS[3]]
            acc_free = [dense.free[2], dense.free[3]]
            kb = [mt[:, 512 * i:512 * (i + 1)] for i in range(2)]
            vb = [mt[:, 1024 + 516 * i:1024 + 516 * (i + 1)].rearrange("p (k n) -> p k n", k=4) for i in range(2)]
            BD = mt[:, 2064:2584].rearrange("p (k n) -> p k n", k=4)
            qT, oT = (G[:, 10 + i, :].rearrange("p (k n) -> p k n", k=4) for i in range(2))
            for i in range(2):
                one_m = DVE.do(lambda e, i=i: e.memset(vb[i][:, :, P], 1.0), mt_free)
            bd0 = DVE.do(lambda e: e.memset(BD, 0.0), mt_free)
            yield

            plan = {}

            def at(step, f, *args):
                plan.setdefault(step, []).append((f, args))

            S = [dict() for _ in range(2 * NT)]

            def product(x, t, w, k, src=None):
                r = ROWS[t]
                if k == 0:
                    x["i"], x["bank"], x["free"] = prod.take()
                lhs = xT[:, k, P * t:P * t + r] if src is None else src[:, k, 0:r]
                f = lambda e: e.matmul(x["bank"][0:r, :], lhs, w[:, k, :], start=(k == 0), stop=(k == 3))
                if k < 3:
                    PE.quiet(f, x["free"], wm, xready(t), x.get("src"))
                else:
                    x["m"] = PE.do(f)

            def soft_a(x, y, t, buf, row, free):
                r = ROWS[t]
                s = small[0:r, 8:16]
                b = buf[0:r, :]
                m = DVE.do(lambda e: e.tensor_tensor(b, x["bank"][0:r, :], rowsb[0:r, row, :], ALU.add), x["m"], free(), rows)
                prod.free[x["i"]] = m
                m = DVE.do(lambda e: e.tensor_reduce(s, h8(b), AXX, ALU.max), m)
                m = DVE.do(lambda e: e.tensor_scalar(s, s, -1.0, None, ALU.mult), m)
                for h in range(H):
                    y["exp"] = ACTQ.do(lambda e, h=h: e.activation(
                        b[:, DH * h:DH * (h + 1)], b[:, DH * h:DH * (h + 1)], ACT.Exp, bias=s[:, h:h + 1],
                        accum_out=small[0:r, 16 + h:17 + h]), m)

            def soft_b(y, t, buf):
                r = ROWS[t]
                s = small[0:r, 16:24]
                b = buf[0:r, :]
                m = DVE.do(lambda e: e.reciprocal(s, s), y["exp"])
                y["soft"] = DVE.do(lambda e: e.tensor_tensor(h8(b), h8(b), s.unsqueeze(2).to_broadcast([r, H, DH]),
                                                             ALU.mult), m)

            used = [None, None]

            def add_v(y, xv, t):
                r, u = ROWS[t], t % 2
                y["v"] = prod.free[xv["i"]] = DVE.do(lambda e: e.tensor_tensor(
                    vb[u][0:r, :, 0:P], xv["bank"][0:r, :].rearrange("p (k n) -> p k n", k=4),
                    rowsb[0:r, 2, :].rearrange("p (k n) -> p k n", k=4), ALU.add), xv["m"], used[u], one_m)

            def context(y, t, k):
                r, u = ROWS[t], t % 2
                used[u] = PE.do(lambda e: e.matmul(
                    acc[k // 2][:, 129 * (k % 2):129 * (k % 2) + 129], kb[u][0:r, k * P:(k + 1) * P], vb[u][0:r, k, :],
                    start=(t == 0 and k % 2 == 0), stop=(t == NT - 1 and k % 2 == 1), skip_group_check=True),
                    y["soft"], y["v"], acc_free)

            for t in range(NT):
                xk, xv, y = {}, {}, S[t]
                for k in range(4):
                    at(8 * t + k, product, xk, t, WA[:, 0], k)
                    at(8 * t + 4 + k, product, xv, t, WA[:, 1], k)
                    at(8 * t + 11 + k // 2, context, y, t, k)
                at(8 * t + 5, soft_a, xk, y, t, kb[t % 2], 1, lambda t=t: used[t % 2])
                at(8 * t + 6, soft_b, y, t, kb[t % 2])
                at(8 * t + 9, add_v, y, xv, t)

            z = {"q": None, "o": None, "qT": None, "oT": None}

            def block_diagonal():
                z["kv"] = z["q"] = z["o"] = used[(NT - 1) % 2]
                for h in range(H):
                    a, k = 64 * (h % 2), h // 2
                    bank, c = acc[k // 2], 129 * (k % 2)
                    DVE.do(lambda e, a=a, k=k, bank=bank, c=c: e.tensor_copy(
                        BD[a:a + 64, k, a:a + 64], bank[a:a + 64, c + a:c + a + 64]), z["kv"], bd0)
                    z["bd"] = z["o2"] = DVE.do(lambda e, a=a, k=k, bank=bank, c=c, h=h: e.tensor_copy(
                        BD[a:a + 64, k, P + h % 2:P + h % 2 + 1], bank[a:a + 64, c + P:c + P + 1]))

            at(8 * NT + 5, block_diagonal)
            qb, ob = kb[0], kb[1]
            outb = [mt[:, 1024:1536], mt[:, 1536:2048]]
            sch = [chan("c_mix0"), chan("c_mix1")]

            def features(t, buf, dst, ready, free):
                r = ROWS[t]
                i, bank, fr = turn.take()
                for k in range(4):
                    f = lambda e, k=k: e.transpose(bank[:, k * P:k * P + r], buf[0:r, k * P:(k + 1) * P], ident[0:r, 0:r])
                    if k < 3:
                        PE.quiet(f, fr, ready)
                    else:
                        m = PE.do(f)
                bk = bank[:, :].rearrange("p (k n) -> p k n", k=4)
                turn.free[i] = ACTQ.do(lambda e: e.activation(dst[:, :, 0:r], bk[:, :, 0:r], ACT.Copy), m, free, link_m)
                return m, turn.free[i]

            def q_features(y, t):
                _, y["qT"] = features(t, qb, qT, y["soft"], z["qT"])

            def q_context(y, t):
                r = ROWS[t]
                for k in range(4):
                    f = lambda e, k=k: e.matmul(acc[k // 2][0:r, 130 * (k % 2):130 * (k % 2) + 130], qT[:, k, 0:r],
                                                BD[:, k, :], start=(k % 2 == 0), stop=(k % 2 == 1), skip_group_check=True)
                    if k < 3:
                        PE.quiet(f, y["qT"], z["bd"], z["o2"])
                    else:
                        y["c"] = z["qT"] = PE.do(f)

            def normal(y, t):
                r = ROWS[t]
                di = small[0:r, 24:32]
                mm = []
                for g in range(2):
                    v = acc[g][0:r, 0:260].rearrange("p (k n) -> p k n", k=2)
                    d2 = di[:, 4 * g:4 * g + 4].rearrange("p (k j) -> p k j", k=2)
                    mm.append(DVE.do(lambda e, v=v, d2=d2: e.reciprocal(d2, v[:, :, P:P + 2]), y["c"]))
                for g in range(2):
                    v = acc[g][0:r, 0:260].rearrange("p (k n) -> p k n", k=2)
                    for k in range(2):
                        o2 = 4 * g + 2 * k
                        m = DVE.do(lambda e, v=v, g=g, k=k, o2=o2: e.tensor_tensor(
                            ob[0:r, 256 * g + P * k:256 * g + P * k + P].rearrange("p (j d) -> p j d", j=2),
                            v[:, k, 0:P].rearrange("p (j d) -> p j d", j=2),
                            di[:, o2:o2 + 2].unsqueeze(2).to_broadcast([r, 2, DH]), ALU.mult), mm[g], z["o"])
                z["o2"] = m
                y["out"] = DVE.do(lambda e: e.tensor_tensor(ob[0:r, :], ob[0:r, :], qb[0:r, :], ALU.add), m)
                z["q"] = [y["out"], y["c"]]

            def o_features(y, xp, t):
                z["o"], xp["src"] = features(t, ob, oT, y["out"], z["oT"])

            def store(xp, t):
                r, u = ROWS[t], t % 2
                z["oT"] = xp["m"]
                m = prod.free[xp["i"]] = DVE.do(lambda e: e.tensor_tensor(
                    outb[u][0:r, :], xp["bank"][0:r, :], rowsb[0:r, 3, :], ALU.add), xp["m"], sch[u].mark(), z["kv"])
                load(sch[u], mixd[P * t:P * t + r, :], outb[u][0:r, :], m)

            for t in range(NT):
                xq, xp, y, b = {}, {}, S[NT + t], 8 * (NT + t)
                for k in range(4):
                    at(b + k, product, xq, t, WA[:, 2], k)
                    at(b + 13 + k, product, xp, t, G[:, 12:16, :], k, oT)
                at(b + 5, soft_a, xq, y, t, qb, 0, lambda: z["q"])
                at(b + 6, soft_b, y, t, qb)
                at(b + 7, q_features, y, t)
                at(b + 9, q_context, y, t)
                at(b + 11, normal, y, t)
                at(b + 12, o_features, y, xp, t)
                at(b + 18, store, xp, t)
            for step in range(max(plan) + 1):
                for f, args in plan.get(step, ()):
                    f(*args)
                yield
            mix_end["done"] = [(PE.sem, PE.n), (DVE.sem, DVE.n), (ACTQ.sem, ACTQ.n)]
            mix_end["stores"] = [c.mark() for c in sch]

        kv_ch = [chan(f"c_kv{i}") for i in range(KV)]
        q_ch = [chan(f"c_q{i}") for i in range(6)]
        sct_ch = [chan(f"c_sct{i}") for i in range(4)]
        order = [c * NJ + j for j in range(NJ) for c in range(NCH)]
        nfb = nfE[:, :].rearrange("p (c j) -> p j c", c=NCH)
        wk = Ring([work[:, s, :] for s in range(3)])
        wk.free = [pre_read, pre_read, zeroed]
        oh = Ring([onehot[:, s, :] for s in range(10)])
        wd_ch = [chan(f"c_wd{i}") for i in range(2)]
        seg_marks = {}

        def attend(l, tables, start, side):
            kv_free, q_free = [None] * KV, [None] * 6
            ready, batch, pend = {}, {}, []
            sc_free, w_free, fix_m = [None] * 2, [None] * 2, None

            def fetch(n):
                if n < ET:
                    a, b, i = n % KV, n % 6, order[n]
                    ready[n] = [kv_ch[a].send(POOL, lambda e: e.indirect_dma_start(
                        out=kvs[a], out_offset=None, in_=KVd[l][:, :],
                        in_offset=bass.IndirectOffsetOnAxis(ap=srcE[:, i:i + 1], axis=0)),
                        tables, idx_ready, start, kv_free[a]),
                        q_ch[b].send(POOL, lambda e: e.indirect_dma_start(
                            out=G[:, b, :], out_offset=None, in_=Qd[l][:, :],
                            in_offset=bass.IndirectOffsetOnAxis(ap=dstE[:, i:i + 1], axis=0)), q_free[b])]

            for n in range(AHEAD):
                fetch(n)
            sub_free, same_free, rep_free, rec_free = None, None, None, None
            hots, maps = {}, []

            def one_hot(v):
                io, ohb, ofree = oh.take()
                key = ordE[:, order[v]:order[v] + 1]
                m = ACTQ.do(lambda e: e.activation(ohb, iota[:, :], ACT.Abs, bias=key, scale=-1.0), ofree, iom, idx_ready)
                hots[v] = (io, ohb, ACTQ.do(lambda e: e.activation(ohb, ohb, ACT.Relu, bias=ones[:, 0:1], scale=-1.0), m, on0))

            for n in range(ET + LAG):
                if n < ET:
                    fetch(n + AHEAD)
                    a, b, j, c = n % KV, n % 6, n // NCH, n % NCH
                    i, buf, free = wk.take()
                    m = DVE.do(lambda e, a=a, b=b, buf=buf: e.tensor_tensor(buf, kvs[a][:, 0:D], G[:, b, :], ALU.mult),
                               ready.pop(n), free)
                    q_free[b] = m
                    sj = scores[:, j % 2, :]
                    late = (m, buf, sj, i)
                r = n % NCH
                if r == 0 and "t" in batch:
                    j, m = batch.pop("t")
                    m = DVE.do(lambda e: e.tensor_tensor_scan(sB, pen[:, 0:P], sA, -BIG, ALU.add, ALU.max), m, fix_m, gate_m)
                    m = DVE.do(lambda e: e.tensor_tensor_scan(sC[:, ::-1], pen[:, P:0:-1], sB[:, ::-1], -BIG,
                                                              ALU.add, ALU.max), m)
                    mx = ACTQ.do(lambda e, j=j: e.activation(fixm[:, j, :], sC[:, 0:P:P - 1], ACT.Copy), m)
                    m = DVE.do(lambda e: e.tensor_tensor(sA, sA, sC, ALU.subtract), m)
                    m = ACTQ.do(lambda e: e.activation(sA, sA, ACT.Exp), m)
                    batch["x"] = (j, m, mx)
                if r == 1 and "x" in batch:
                    j, m, mx = batch.pop("x")
                    m = DVE.do(lambda e: e.tensor_tensor_scan(sB, same[:, 0:P], sA, 0.0, ALU.mult, ALU.add), m)
                    m = DVE.do(lambda e: e.scalar_tensor_tensor(out=sB, in0=same[:, 1:P + 1], scalar=1.0, in1=sB,
                                                                op0=ALU.subtract, op1=ALU.mult), m)
                    m = DVE.do(lambda e: e.tensor_tensor_scan(sC[:, ::-1], same[:, P:0:-1], sB[:, ::-1], 0.0,
                                                              ALU.mult, ALU.add), m, mx)
                    same_free = m
                    fix_m = ACTQ.do(lambda e, j=j: e.activation(fixl[:, j, :], sC[:, 0:P:P - 1], ACT.Copy, scale=-1.0,
                                                                bias=1e-16), m)
                    i, bank, free = turn.take()
                    PE.quiet(lambda e, bank=bank: e.transpose(bank[:, 0:HC], sA, ident[0:HC, 0:HC]), m, free)
                    mp = sub_free = PE.do(lambda e, bank=bank: e.transpose(bank[:, HC:2 * HC], sC, ident[0:HC, 0:HC]))
                    fix_m = [fix_m, mp]
                    wj = wts[:, j % 2, :]
                    m = DVE.do(lambda e, bank=bank: e.tensor_scalar(firsts[:, :], bank[:, HC:2 * HC], -1.0, 1e-16,
                                                                    ALU.mult, ALU.add), mp, rep_free)
                    m = DVE.do(lambda e: e.reciprocal(firsts[:, :], firsts[:, :]), m)
                    turn.free[i] = rec_free = mw_ready = DVE.do(lambda e, bank=bank, wj=wj: e.tensor_tensor(
                        wj, bank[:, 0:HC], firsts[:, :], ALU.mult), m, w_free[j % 2], wd_ch[j % 2].mark())
                    load(wd_ch[j % 2], Wd[l][j], wj, mw_ready)
                if n >= LAG:
                    v = n - LAG
                    a, j, c, e_i = v % KV, v // NCH, v % NCH, order[v]
                    wj = wts[:, j % 2, :].rearrange("p (h c) -> p h c", h=H)[:, :, c:c + 1]
                    i, buf, free = wk.take()
                    mw = DVE.do(lambda e, a=a, wj=wj, buf=buf: e.tensor_tensor(
                        h8(buf), h8(kvs[a][:, D:2 * D]), wj.to_broadcast([P, H, DH]), ALU.mult), free, mw_ready)
                    kv_free[a] = w_free[j % 2] = mw
                    io, ohb, mo = hots.pop(v)
                    q, g = v % PACK, v // PACK
                    if q == 0:
                        ib, ebank, efree = edge.take()
                        hot = []
                    hot.append((ohb, e_i, io))
                    mp = PE.do(lambda e, ohb=ohb, buf=buf, ebank=ebank, q=q: e.matmul(
                        ebank[:, :], ohb, buf, start=(q == 0), stop=(q == PACK - 1)), mw, mo, efree)
                    wk.free[i] = oh.free[io] = mp
                    if q == PACK - 1:
                        if l == 0:
                            maps.append([g, list(hot)])
                        k, sbuf, sfree = stg.take()
                        me = edge.free[ib] = ACTQ.do(lambda e, sbuf=sbuf, ebank=ebank: e.activation(
                            sbuf, ebank[:, :], ACT.Copy), mp, stg_ch[k].mark(), sfree)
                        pend.append((v, k, sbuf, g, me))
                    if maps and (v % PACK < 2 or v == ET - 1):
                        g, hot2 = maps[0]
                        if len(hot2) == PACK:
                            mbank = turn.take()
                        it, tb, free = mbank
                        for _ in range(PACK if v == ET - 1 else 2):
                            q2 = PACK - len(hot2)
                            ohb, e2, io2 = hot2.pop(0)
                            mp2 = oh.free[io2] = PE.do(lambda e, ohb=ohb, tb=tb, e2=e2, q2=q2: e.matmul(
                                tb[:, 0:1], ohb, fvE[:, e2:e2 + 1], start=(q2 == 0), stop=(q2 == PACK - 1)), free)
                        if not hot2:
                            maps.pop(0)
                            turn.free[it] = seg_marks[g] = ACTQ.do(lambda e, tb=tb, g=g: e.activation(
                                segE[:, g:g + 1], tb[:, 0:1], ACT.Copy, bias=FAR), mp2)
                    while pend and (v >= pend[0][0] + 3 or v == ET - 1):
                        _, k, sbuf, g, me = pend.pop(0)
                        stg.free[k] = sct_ch[k].send(POOL, lambda e, sbuf=sbuf, g=g: e.indirect_dma_start(
                            out=aggd[l][:, :], out_offset=bass.IndirectOffsetOnAxis(ap=segE[:, g:g + 1], axis=0),
                            in_=sbuf, in_offset=None, bounds_check=AGG_ROWS - 1, oob_is_err=False),
                            me, seg_marks[g], zeroed)
                if n < ET:
                    m, buf, sj, i = late
                    c, j = n % NCH, n // NCH
                    m = DVE.do(lambda e, c=c, buf=buf, sj=sj: e.tensor_reduce(
                        sj.rearrange("p (h c) -> p h c", h=H)[:, :, c], h8(buf), AXX, ALU.add), m, sc_free[j % 2])
                    wk.free[i] = m
                    if c == NCH - 1:
                        mn = ACTQ.do(lambda e, j=j: e.activation(
                            firsts[:, :].rearrange("p (h c) -> p h c", h=H),
                            nfb[:, j, :].unsqueeze(1).to_broadcast([P, H, NCH]), ACT.Copy), idx_ready, rep_free, rec_free)
                        i, bank, free = turn.take()
                        PE.quiet(lambda e, bank=bank, sj=sj: e.transpose(bank[0:HC, 0:P], sj, ident[:, :]), m, free)
                        mp = rep_free = PE.do(lambda e, bank=bank: e.transpose(bank[0:HC, P:2 * P], firsts[:, :], ident[:, :]), mn)
                        sc_free[j % 2] = mp
                        mt1 = ACTQ.do(lambda e, bank=bank: e.activation(sA, bank[0:HC, 0:P], ACT.Copy), mp, sub_free, start)
                        mt2 = ACTQ.do(lambda e, bank=bank: e.activation(pen[:, 0:P], bank[0:HC, P:2 * P], ACT.Copy,
                                                                        scale=-BIG), same_free)
                        turn.free[i] = mt2 = ACTQ.do(lambda e, bank=bank: e.activation(
                            same[:, 0:P], bank[0:HC, P:2 * P], ACT.Copy, scale=-1.0, bias=1.0), same_free)
                        batch["t"] = (j, [mt1, mt2])
                if LAG - 2 <= n < ET + LAG - 2:
                    one_hot(n - LAG + 2)
                if side is not None:
                    next(side, None)
            return [mw, mp], fix_m

        def crowded(l, edges):
            stored = [c.mark() for c in sct_ch] + [c.mark() for c in wd_ch]
            for q in (PE, DVE, ACTQ, POOL, SP):
                q.wait(flag_m)
            any_ = nc.values_load(flag[0:1, 0:1], min_val=0, max_val=1)
            pe, dve, act, pool, sp = (Queue(q.engine, sem(f"s_crowd{l}{i}"))
                                      for i, q in enumerate((PE, DVE, ACTQ, POOL, SP)))
            cw, cs = chan(f"c_crw{l}"), [chan(f"c_crs{l}{i}") for i in range(2)]
            cg = [chan(f"c_crg{l}{i}") for i in range(2)]
            with nc.If(any_ != 0):
                begin = [edges, stored, (ACTQ.sem, ACTQ.n)]
                m_v, m_pe, m_act = [begin] * 2, [begin] * 2, [begin] * 2
                for v in range(ET):
                    a, j, c, e_i = v % 2, v // NCH, v % NCH, order[v]
                    if c == 0:
                        mw_ = cw.send(sp, lambda e, j=j: e.dma_start(wts[:, 0, :], Wd[l][j]), m_v[1 - a])
                    mg_ = cg[a].send(pool, lambda e, a=a, e_i=e_i: e.indirect_dma_start(
                        out=kvs[a], out_offset=None, in_=KVd[l][:, :],
                        in_offset=bass.IndirectOffsetOnAxis(ap=srcE[:, e_i:e_i + 1], axis=0)), m_v[a])
                    mo = dve.do(lambda e, a=a, c=c, e_i=e_i: e.tensor_scalar(
                        onehot[:, a, :], iota[:, :], 1000.0 + CAP + CAP * (c % PACK), ordE[:, e_i:e_i + 1],
                        ALU.add, ALU.is_equal), m_pe[a])
                    wj = wts[:, 0, :].rearrange("p (h c) -> p h c", h=H)[:, :, c:c + 1]
                    m_v[a] = dve.do(lambda e, a=a, wj=wj: e.tensor_tensor(
                        h8(work[:, a, :]), h8(kvs[a][:, D:2 * D]), wj.to_broadcast([P, H, DH]), ALU.mult),
                        mw_, mg_, m_pe[a])
                    pe.do(lambda e, a=a: e.matmul(PS[6 + a][:, :], onehot[:, a, :], work[:, a, :], start=True, stop=True),
                          mo, m_v[a], m_act[a])
                    m_pe[a] = pe.do(lambda e, a=a, e_i=e_i: e.matmul(
                        PS[4 + a][:, 0:1], onehot[:, a, :], fvE[:, e_i:e_i + 1], start=True, stop=True))
                    act.do(lambda e, a=a: e.activation(stage[:, a, :], PS[6 + a][:, :], ACT.Copy), m_pe[a], cs[a].mark(), begin)
                    m_act[a] = act.do(lambda e, a=a: e.activation(segS[:, a:a + 1], PS[4 + a][:, 0:1], ACT.Copy, bias=FAR))
                    cs[a].send(pool, lambda e, a=a: e.indirect_dma_start(
                        out=aggd[l][:, :], out_offset=bass.IndirectOffsetOnAxis(ap=segS[:, a:a + 1], axis=0),
                        in_=stage[:, a, :], in_offset=None, bounds_check=AGG_ROWS - 1, oob_is_err=False), m_act[a])
                pool.wait(*[c.mark() for c in cs])
            done = POOL.do(lambda e: e.memset(crowd[0:1, 3:4], 0.0))
            for q in (PE, DVE, ACTQ, SP):
                q.wait(done)
            return done

        hc = lambda row: rows1[0:1, row, :].rearrange("a (h c) -> a h c", h=H)
        links = []
        snB = mt[:, 0:ET]
        c_join = [chan("c_joinF"), chan("c_joinL")]

        def shared_setup(free):
            smin = small[0:HC, 32:34]
            links.append(DVE.do(lambda e: e.tensor_scalar(linkp, link[:, :], 1.0, BIG, ALU.subtract, ALU.mult), free, link_m))
            DVE.do(lambda e: e.tensor_reduce(smin[:, 0:1], link[:, 0:SEQ], AXX, ALU.min))
            m = DVE.do(lambda e: e.tensor_reduce(smin[:, 1:2], link[:, 1:SEQ + 1], AXX, ALU.min))
            DVE.do(lambda e: e.memset(rows1[:, 0:2, :], 0.0), free)
            DVE.do(lambda e: e.memset(rows1[:, 4:6, :], -BIG))
            DVE.do(lambda e: e.memset(rows1[:, 12:14, :], 1.0))
            mz = DVE.do(lambda e: e.memset(rows1[:, 6:8, :], 0.0))
            for d in range(2):
                i, bank, fr = turn.take()
                mp = PE.do(lambda e, d=d, bank=bank: e.transpose(bank[0:1, 0:HC], smin[:, d:d + 1], ident[0:HC, 0:HC]), fr, m)
                bh = bank[0:1, 0:HC].rearrange("a (h c) -> a h c", h=H)
                if d == 0:
                    m1 = DVE.do(lambda e, bh=bh: e.tensor_copy(hc(0)[:, :, 1:NCH], bh[:, :, 0:NCH - 1]), mp, mz)
                else:
                    m1 = DVE.do(lambda e, bh=bh: e.tensor_copy(hc(1)[:, :, 0:NCH - 1], bh[:, :, 1:NCH]), mp, mz)
                turn.free[i] = m1
            links.append(DVE.do(lambda e: e.tensor_scalar(rows1[:, 2:4, :], rows1[:, 0:2, :], 1.0, BIG,
                                                          ALU.subtract, ALU.mult), m1))
            i, bank, fr = turn.take()
            for b in range(TB):
                mp = PE.do(lambda e, b=b, bank=bank: e.transpose(bank[0:1, b * TP:(b + 1) * TP], start[:, b:b + 1],
                                                                 ident[0:TP, 0:TP]), fr, start_m)
            row = rowsb[0:1, 3, 0:ET]
            m = turn.free[i] = DVE.do(lambda e, bank=bank: e.tensor_copy(row, bank[0:1, 0:ET]), mp, free)
            i, bank, fr = turn.take()
            o1 = rows1[0:1, 12:14, :].rearrange("a s p -> a (s p)")[:, 0:TP]
            mp = PE.do(lambda e, bank=bank: e.matmul(bank[0:TP, 0:ET], o1, row, start=True, stop=True), fr, m)
            m = turn.free[i] = DVE.do(lambda e, bank=bank: e.tensor_copy(snB[0:TP, :], bank[0:TP, 0:ET]), mp, free)
            links.append(m)

        def seg_scan(data, res, kind, back, m):
            ops = (ALU.add, ALU.max) if kind == 0 else (ALU.mult, ALU.add)
            init = -BIG if kind == 0 else 0.0
            gate = linkp if kind == 0 else link
            if back:
                g, x, o = gate[:, SEQ:0:-1], data[:, ::-1], res[:, ::-1]
                last = res[:, 0:1]
            else:
                g, x, o = gate[:, 0:SEQ], data, res
                last = res[:, SEQ - 1:SEQ]
            m = DVE.do(lambda e: e.tensor_tensor_scan(o, g, x, init, *ops), m)
            i, bank, free = turn.take()
            mp = PE.do(lambda e: e.transpose(bank[0:1, 0:HC], last, ident[0:HC, 0:HC]), m, free)
            bh = bank[0:1, 0:HC].rearrange("a (h c) -> a h c", h=H)
            hand, lk, car = 4 + 2 * kind + back, (2 if kind == 0 else 0) + back, 8 + 2 * kind + back
            if back:
                m = DVE.do(lambda e: e.tensor_copy(hc(hand)[:, :, 0:NCH - 1], bh[:, :, 1:NCH]), mp, links)
                m1 = DVE.do(lambda e: e.tensor_tensor_scan(rows1[:, car, ::-1], rows1[:, lk, ::-1],
                                                           rows1[:, hand, ::-1], init, *ops), m)
            else:
                m = DVE.do(lambda e: e.tensor_copy(hc(hand)[:, :, 1:NCH], bh[:, :, 0:NCH - 1]), mp, links)
                m1 = DVE.do(lambda e: e.tensor_tensor_scan(rows1[:, car, :], rows1[:, lk, :], rows1[:, hand, :],
                                                           init, *ops), m)
            turn.free[i] = m
            i, bank2, free = turn.take()
            mp = PE.do(lambda e: e.transpose(bank2[0:HC, 0:1], rows1[0:1, car, :], ident[0:1, 0:1]), m1, free)
            cc = small[0:HC, 40 + 2 * kind + back:41 + 2 * kind + back]
            m = DVE.do(lambda e: e.tensor_copy(cc, bank2[0:HC, 0:1]), mp)
            turn.free[i] = m
            return DVE.do(lambda e: e.tensor_tensor_scan(o, g, x, cc, *ops), m)

        def join(l, fix_m, edges, rest):
            stored = [c.mark() for c in sct_ch] + [rest]
            part = [G[0:TP, 4 * i:4 * i + 4, :] for i in range(2)]
            base = (AGG_F, AGG_L)
            pl = [load(c_join[i], part[i], aggd[l][base[i]:base[i] + ET, :].rearrange("(b p) d -> p b d", p=TP),
                       stored, edges) for i in range(2)]
            if l == 0:
                shared_setup([edges, mix_end["done"]])
            flat = lambda ap: ap.rearrange("p j k -> p (j k)")
            X, Z, W_ = (ap[:, 0:SEQ] for ap in (sA, sB, sC))
            m = seg_scan(flat(fixm[:, :, :]), X, 0, 0, [fix_m, edges, links])
            m = seg_scan(X, Z, 0, 1, m)
            m = DVE.do(lambda e: e.tensor_tensor(X, flat(fixm[:, :, :]), Z, ALU.subtract), m)
            m = ACTQ.do(lambda e: e.activation(X, X, ACT.Exp), m)
            X3 = X.rearrange("p (j k) -> p j k", k=2)
            m = DVE.do(lambda e: e.tensor_tensor(X, X, flat(fixl[:, :, :]), ALU.mult), m)
            Z3 = Z.rearrange("p (j k) -> p j k", k=2)
            m2 = DVE.do(lambda e: e.tensor_copy(Z, X), m)
            m2 = DVE.do(lambda e: e.tensor_tensor(Z3[:, :, 1], X3[:, :, 1], link[:, 1:SEQ:2], ALU.mult), m2)
            m2 = DVE.do(lambda e: e.tensor_tensor(Z3[:, :, 1], X3[:, :, 1], Z3[:, :, 1], ALU.subtract), m2)
            m = seg_scan(Z, W_, 1, 0, m2)
            m = DVE.do(lambda e: e.scalar_tensor_tensor(out=W_, in0=link[:, 1:SEQ + 1], scalar=1.0, in1=W_,
                                                        op0=ALU.subtract, op1=ALU.mult), m)
            m = seg_scan(W_, Z, 1, 1, m)
            m = DVE.do(lambda e: e.tensor_scalar(Z, Z, -1.0, 1e-16, ALU.mult, ALU.add), m)
            m = DVE.do(lambda e: e.reciprocal(Z, Z), m)
            m = DVE.do(lambda e: e.tensor_tensor(X, X, Z, ALU.mult), m)
            fac = small[0:TP, 0:64 - 0].rearrange("p (k b h) -> p k b h", k=2, b=TB)
            i, bank, free = turn.take()
            for k in range(2):
                for b in range(TB):
                    iw, hb, hfree = wk.take()
                    lhs = hb[0:HC, 0:TP]
                    m2 = DVE.do(lambda e, k=k, b=b, lhs=lhs: e.tensor_tensor(
                        lhs.rearrange("p (c j) -> p c j", c=2), X3[:, :, k].unsqueeze(1).to_broadcast([HC, 2, NJ]),
                        maskC[:, 2 * b:2 * b + 2].unsqueeze(2).to_broadcast([HC, 2, NJ]), ALU.mult), m, mask_m, hfree)
                    o = (k * TB + b) * H
                    mp = wk.free[iw] = PE.do(lambda e, lhs=lhs, o=o, bank=bank: e.matmul(
                        bank[0:TP, o:o + H], lhs, selH[:, :], start=True, stop=True), m2, free)
            mf = turn.free[i] = DVE.do(lambda e, bank=bank: e.tensor_copy(small[0:TP, 0:64], bank[0:TP, 0:64]), mp)
            banks = [dense.take() for _ in range(TB)]
            for k in range(2):
                for b in range(TB):
                    mr = DVE.do(lambda e, k=k, b=b: e.tensor_tensor(
                        h8(part[k][:, b, :]), h8(part[k][:, b, :]),
                        fac[:, k, b, :].unsqueeze(2).to_broadcast([TP, H, DH]), ALU.mult), mf, pl[k])
                    iw, hb, hfree = wk.take()
                    node = (nodeF, nodeL)[k]
                    ms = DVE.do(lambda e, hb=hb, node=node, b=b: e.tensor_scalar(
                        hb[0:TP, 0:ET], snB[0:TP, :], node[:, b:b + 1], None, ALU.is_equal), hfree, links)
                    for q in range(TB):
                        _, bank, free = banks[q]
                        mp = PE.do(lambda e, k=k, b=b, q=q, bank=bank, hb=hb: e.matmul(
                            bank[0:TP, :], hb[0:TP, q * TP:(q + 1) * TP], part[k][:, b, :],
                            start=(k == 0 and b == 0), stop=(k == 1 and b == TB - 1)), ms, mr, free)
                    wk.free[iw] = mp
            for q in range(TB):
                i, bank, _ = banks[q]
                k, sbuf, sfree = stg.take()
                me = dense.free[i] = ACTQ.do(lambda e, sbuf=sbuf, bank=bank: e.activation(sbuf[0:TP, :], bank[0:TP, :],
                                                                                          ACT.Copy), mp, sfree)
                stg.free[k] = sct_ch[k].send(POOL, lambda e, sbuf=sbuf, q=q: e.indirect_dma_start(
                    out=aggd[l][:, :], out_offset=bass.IndirectOffsetOnAxis(ap=runrow[:, q:q + 1], axis=0),
                    in_=sbuf[0:TP, :], in_offset=None, bounds_check=AGG_ROWS - 1, oob_is_err=False), me, runrow_m, stored)
            return [c.mark() for c in sct_ch], [mp, edges]

        st4 = st[:, :].rearrange("p (f c s) -> p f c s", f=4, c=7)

        def norm_coeffs(l, cg, cb, m):
            for f in range(4):
                m2 = DVE.do(lambda e, f=f: e.bn_aggr(out=mv[:, f, :], in_=st4[:, f, :, :]), m)
            sc, off = small[:, 0:4], small[:, 4:8]
            m = DVE.do(lambda e: e.tensor_scalar(sc, mv[:, 0:4, 1], EPS, None, ALU.add), m2)
            m = ACTQ.do(lambda e: e.activation(sc, sc, ACT.Sqrt), m)
            m = DVE.do(lambda e: e.reciprocal(sc, sc), m)
            m = DVE.do(lambda e: e.tensor_tensor(sc, sc, vec[:, cg + 4 * l:cg + 4 * l + 4], ALU.mult), m, ldv)
            m = DVE.do(lambda e: e.tensor_tensor(off, mv[:, 0:4, 0], sc, ALU.mult), m)
            return DVE.do(lambda e: e.tensor_tensor(off, vec[:, cb + 4 * l:cb + 4 * l + 4], off, ALU.subtract), m)

        def normalise(c, m):
            c0, cn = CHUNKS[c]
            for f in range(4):
                m2 = DVE.do(lambda e, f=f: e.tensor_scalar(xT[:, f, c0:c0 + cn], xT[:, f, c0:c0 + cn], small[:, f:f + 1],
                                                           small[:, 4 + f:5 + f], ALU.mult, ALU.add), m)
            return m2

        c_agg = [chan(f"c_agg{i}") for i in range(5)]

        def finish_layer(l, agg_ready, g_free, x_free, Wo, W1, W2, wready, meanwhile=None):
            aggT = [G[:, 0:4, :], G[:, 4:8, :]]
            rows = Ring([G[:, 8 + s, :] for s in range(4)])
            t_free = [None, None]
            got = {}

            def fetch(t):
                if t < NT:
                    s, buf, free = rows.take()
                    got[t] = (s, buf, load(c_agg[s], buf[0:ROWS[t], :], aggd[l][P * t:P * t + ROWS[t], :],
                                           agg_ready, g_free, free))

            for t in range(3):
                fetch(t)
            for c, (c0, cn) in enumerate(CHUNKS):
                dst = aggT[c % 2]
                for t in range(4 * c, min(4 * c + 4, NT)):
                    fetch(t + 3)
                    r = ROWS[t]
                    s, row, ml = got.pop(t)
                    it, bank, free = turn.take()
                    for f in range(4):
                        g = lambda e, f=f, bank=bank, row=row, r=r: e.transpose(
                            bank[:, f * P:f * P + r], row[0:r, f * P:(f + 1) * P], ident[0:r, 0:r])
                        if f < 3:
                            PE.quiet(g, free, ml)
                        else:
                            mp = PE.do(g)
                    rows.free[s] = mp
                    o0 = P * t - c0
                    bk = bank[:, :].rearrange("p (k n) -> p k n", k=4)
                    turn.free[it] = mt_ = ACTQ.do(lambda e, bk=bk, dst=dst, o0=o0, r=r: e.activation(
                        dst[:, :, o0:o0 + r], bk[:, :, 0:r], ACT.Copy), mp, t_free[c % 2], g_free)
                for f in range(4):
                    i, bank, free = dense.take()
                    for k in range(4):
                        g = lambda e, k=k, f=f, bank=bank, dst=dst, cn=cn: e.matmul(
                            bank[:, 0:cn], Wo[:, k, f * P:(f + 1) * P], dst[:, k, 0:cn], start=(k == 0), stop=(k == 3))
                        if k < 3:
                            PE.quiet(g, free, mt_, wready)
                        else:
                            mp = PE.do(g)
                    m = DVE.do(lambda e, f=f, bank=bank, c0=c0, cn=cn: e.scalar_tensor_tensor(
                        out=xT[:, f, c0:c0 + cn], in0=bank[:, 0:cn], scalar=vec[:, C_BO + 4 * l + f:C_BO + 4 * l + f + 1],
                        in1=xT[:, f, c0:c0 + cn], op0=ALU.add, op1=ALU.add), mp, x_free, ldv)
                    dense.free[i] = m
                    m = DVE.do(lambda e, f=f, c=c, c0=c0, cn=cn: e.bn_stats(out=st4[:, f, c, :], in_=xT[:, f, c0:c0 + cn]), m)
                t_free[c % 2] = mp
            co = norm_coeffs(l, C_G1, C_E1, m)
            g_done = mp
            if meanwhile:
                meanwhile(g_done)
            nx = {0: normalise(0, co)}
            for c, (c0, cn) in enumerate(CHUNKS):
                if c + 1 < len(CHUNKS):
                    nx[c + 1] = normalise(c + 1, co)
                i, bank, free = dense.take()
                for k in range(4):
                    g = lambda e, k=k, bank=bank, c0=c0, cn=cn: e.matmul(
                        bank[:, 0:cn], W1[:, k, :], xT[:, k, c0:c0 + cn], start=(k == 0), stop=(k == 3))
                    if k < 3:
                        PE.quiet(g, free, nx[c])
                    else:
                        mp = PE.do(g)
                iw, hb, hfree = wk.take()
                mh = ACTQ.do(lambda e, bank=bank, hb=hb, cn=cn: e.activation(
                    hb[:, 0:cn], bank[:, 0:cn], ACT.Relu, bias=vec[:, C_B1 + l:C_B1 + l + 1]), mp, hfree)
                dense.free[i] = mh
                for f in range(4):
                    i, bank, free = dense.take()
                    mp = PE.do(lambda e, f=f, bank=bank, hb=hb, cn=cn: e.matmul(
                        bank[:, 0:cn], W2[:, f * P:(f + 1) * P], hb[:, 0:cn], start=True, stop=True), free, mh)
                    m = DVE.do(lambda e, f=f, bank=bank, c0=c0, cn=cn: e.scalar_tensor_tensor(
                        out=xT[:, f, c0:c0 + cn], in0=bank[:, 0:cn], scalar=vec[:, C_B2 + 4 * l + f:C_B2 + 4 * l + f + 1],
                        in1=xT[:, f, c0:c0 + cn], op0=ALU.add, op1=ALU.add), mp)
                    dense.free[i] = m
                    m = DVE.do(lambda e, f=f, c=c, c0=c0, cn=cn: e.bn_stats(out=st4[:, f, c, :], in_=xT[:, f, c0:c0 + cn]), m)
                wk.free[iw] = mp
            co = norm_coeffs(l, C_G2, C_E2, m)
            marks = [normalise(c, co) for c in range(len(CHUNKS))]
            return (lambda t: marks[t // 4]), g_done

        def load_layer(l, m):
            load(c_wa, WA[:, 0], kpo(A["WoT"][l]), m)
            load(c_wa, WA[:, 1].rearrange("p k (a o) -> p (k a) o", o=P)[:, 0:4, :], kpo(A["W1T"][l]), m)
            mk = load(c_wa, WA[:, 2, 0, :], A["W2T"][l], m)
            return WA[:, 0], WA[:, 1].rearrange("p k (a o) -> p (k a) o", o=P)[:, 0:4, :], WA[:, 2, 0, :], mk

        side = mix(lambda t: xT_ready[t], x_read, pre_read)
        edges, mark0 = attend(0, kv_ready + [zeroed], [link_m, x_read], side)
        for _ in side:
            pass
        mix_done, mix_ready = mix_end["done"], mix_end["stores"]
        dense.free = [mix_done] * 4
        Wl = load_layer(0, mix_done)
        rest = crowded(0, edges)
        agg_ready, g_ok = join(0, mark0, edges, rest)
        row1 = load_row(0, A["gbq"][1], mix_done)
        parts = {}

        def cut_weights(g_done):
            area.close()
            Wh, raw = tensor("Wh", [P, 3, 4, 512], F32R), tensor("Wraw", [P, 3, 4, 512])
            tensor("gap", [P, 512])
            Wl_ = tensor("Wl", [P, 3, 4, 512], F32R)
            xs = tensor("xs", [P, 2, 2, 4, P], F32R)
            got = load_qkv(1, raw, [edges, rest, g_ok])
            for w in range(3):
                for k in range(4):
                    parts["ready"] = split(raw[:, w, k, :], Wh[:, w, k, :], Wl_[:, w, k, :], got, g_done, rest)
            parts["all"] = (Wh, Wl_, [(xs[:, u, 0], xs[:, u, 1]) for u in range(2)])

        x_ready, g_ok = finish_layer(0, agg_ready, g_ok, [x_read, mix_done], *Wl, cut_weights)
        kv_ready, x_read1 = qkv(1, parts["ready"], x_ready, row1, 0, parts["all"], g_ok)
        area.close()
        Y = area.enter_context(nc.sbuf_tensor("Y2", [P, 12800], F32))
        G = area.enter_context(nc.sbuf_tensor("G2", [P, 16, 512], F32))
        Yt, kvs, sA, sB, sC, wts = views(Y, G)
        Wl = load_layer(1, x_read1)
        edges, mark0 = attend(1, kv_ready + [zeroed], [g_ok, x_read1], None)
        agg_ready, g_ok = join(1, mark0, edges, crowded(1, edges))
        y_done = edges
        x_ready, g_done = finish_layer(1, agg_ready, g_ok, x_read1, *Wl)
        pv = [(PE.sem, PE.n), (DVE.sem, DVE.n)]

        rl = [load_row(1, A["ln_g"], agg_ready), load_row(2, A["ln_b"], agg_ready)][-1]
        Wm1 = G[:, 0:8, :].rearrange("p a b -> p (a b)").rearrange("p (k e f) -> p k e f", k=4, e=8)
        Wm2 = G[:, 8:16, :]
        for k in range(4):
            load(c_g, Wm1[:, k], A["EW1"][:, k * P:(k + 1) * P, :].rearrange("e p f -> p e f"), g_done)
        wmoe = load(c_g, Wm2, A["EW2"].rearrange("e f o -> f e o"), g_done)
        c_moe = chan("c_moe")
        wg = router[:, 0, 0:32].rearrange("p (k e) -> p k e", k=4)
        load(c_moe, wg, A["Wg"].rearrange("(k p) e -> p k e", p=P), g_done)
        load(c_moe, bgr, A["bg"].partition_broadcast(P), g_done)
        b2row = work[0:8, 0, :]
        rmoe = load(c_moe, b2row, A["Eb2"], (PE.sem, PE.n))

        tail = DVE.do(lambda e: e.memset(Yt[:, NT - 1, :], 0.0), x_read1, y_done)
        xin = Ring([stage[:, s, :] for s in range(2)])
        min_ = Ring([stage[:, 2 + s, :] for s in range(2)])
        got = {}

        def fetch_res(t):
            if t < NT:
                r = ROWS[t]
                a, xb, xf = xin.take()
                b, mb_, mf = min_.take()
                got[t] = (a, xb, b, mb_, load(stg_ch[a], xb[0:r, :], A["x"][P * t:P * t + r, :], xf, agg_ready),
                          load(stg_ch[2 + b], mb_[0:r, :], mixd[P * t:P * t + r, :], mf, mix_ready, agg_ready))

        fetch_res(0)
        fetch_res(1)
        x2, xf_ready, mc = [None] * NT, [None] * NT, [None] * NT
        fx = Ring([work[:, 1, :], work[:, 2, :], mt[:, 2048:2560], mt[:, 2560:3072]])
        fx.free = [pv] * 4
        lgb = PS[6]
        mz = DVE.do(lambda e: e.memset(lgb[:, 0:200], 0.0), edge.free)
        pr, ta, tb_, tc, comb = (router[:, 1 + s, :].rearrange("p (t e) -> p t e", t=NT) for s in range(5))
        lg3 = lgb[:, 0:200].rearrange("p (t e) -> p t e", t=NT)
        kx = POOL.do(lambda e: e.iota(tc, pattern=[[0, NT], [-1, 8]], base=8, channel_multiplier=0,
                                      allow_small_or_imprecise_dtypes=True), g_done)
        cT = WA[0:8].rearrange("p w k o -> p (w k o)")[:, 2048:2048 + N]

        def front(tiles):
            ymark, fmark = {}, {}
            for t in tiles:
                r = ROWS[t]
                i, bank, free = turn.take()
                for k in range(4):
                    f = lambda e, k=k, t=t, r=r, bank=bank: e.transpose(
                        bank[0:r, k * P:(k + 1) * P], xT[:, k, P * t:P * t + r], ident[:, :])
                    if k < 3:
                        PE.quiet(f, free, x_ready(t))
                    else:
                        mp = PE.do(f)
                turn.free[i] = ymark[t] = ACTQ.do(lambda e, t=t, r=r, bank=bank: e.activation(
                    Yt[0:r, t, :], bank[0:r, :], ACT.Copy), mp, tail, y_done)
                fmark[t] = mp
                if t % 2:
                    yield
            yield
            m = ln_stats(tiles, lambda t: ymark[t])
            yield
            for t in tiles:
                r = ROWS[t]
                a, xb, b, mb_, la, lb = got.pop(t)
                m1 = POOL.do(lambda e, xb=xb, mb_=mb_, r=r: e.tensor_tensor(xb[0:r, :], xb[0:r, :], mb_[0:r, :], ALU.add),
                             la, lb)
                min_.free[b] = m1
                m1 = POOL.do(lambda e, xb=xb, r=r: e.tensor_tensor(xb[0:r, :], xb[0:r, :], rowsb[0:r, 2, :], ALU.add), m1, rl)
                m2 = DVE.do(lambda e, t=t, r=r: e.scalar_tensor_tensor(
                    out=Yt[0:r, t, :], in0=Yt[0:r, t, :], scalar=mv[0:r, t, 0:1], in1=rowsb[0:r, 1, :],
                    op0=ALU.subtract, op1=ALU.mult), m, rl)
                x2[t] = DVE.do(lambda e, t=t, r=r, xb=xb: e.scalar_tensor_tensor(
                    out=Yt[0:r, t, :], in0=Yt[0:r, t, :], scalar=rs[0:r, t:t + 1], in1=xb[0:r, :],
                    op0=ALU.mult, op1=ALU.add), m2, m1)
                xin.free[a] = x2[t]
                fetch_res(t + 2)
                if t % 2:
                    yield
            m = ln_stats(tiles, lambda t: x2[t])
            yield
            normed = []
            for t in tiles:
                i, buf, free = fx.take()
                normed.append((t, i, buf, DVE.do(lambda e, t=t, buf=buf: e.tensor_scalar(
                    buf, Yt[:, t, :], mv[:, t, 0:1], rs[:, t:t + 1], ALU.subtract, ALU.mult), m, free)))
            yield
            for t, i, buf, mn in normed:
                xf_ready[t], fx.free[i] = to_features(t, buf, mn, fmark[t])
                if t % 2:
                    yield
            for t in tiles:
                r = ROWS[t]
                for k in range(4):
                    f = lambda e, k=k, t=t, r=r: e.matmul(lgb[0:r, 8 * t:8 * t + 8], xT[:, k, P * t:P * t + r], wg[:, k, :],
                                                          start=(k == 0), stop=(k == 3))
                    if k < 3:
                        PE.quiet(f, xf_ready[t], rmoe, mz)
                    else:
                        mp = PE.do(f)
                if t % 2:
                    yield
            n, a = len(tiles), tiles[0]
            one = small[:, a:a + n]
            wide = one.unsqueeze(2).to_broadcast([P, n, 8])
            pr_, ta_, tx_, tc_, cb_ = (v[:, a:a + n, :] for v in (pr, ta, tb_, tc, comb))

            def tt(o, x, y, op, *marks):
                return DVE.do(lambda e: e.tensor_tensor(o, x, y, op), *marks)

            def red(x, op, *marks):
                return DVE.do(lambda e: e.tensor_reduce(one, x, AXX, op), *marks)

            m = tt(pr_, lg3[:, a:a + n, :], bgr.unsqueeze(1).to_broadcast([P, n, 8]), ALU.add, mp, kx)
            m = red(pr_, ALU.max, m)
            m = tt(pr_, pr_, wide, ALU.subtract, m)
            m = ACTQ.do(lambda e: e.activation(pr_, pr_, ACT.Exp), m)
            yield
            m = red(pr_, ALU.add, m)
            m = DVE.do(lambda e: e.reciprocal(one, one), m)
            m = tt(pr_, pr_, wide, ALU.mult, m)
            m = DVE.do(lambda e: e.tensor_copy(ta_, pr_), m)
            for turn_no in range(2):
                m = red(ta_, ALU.max, m)
                m = tt(tx_, ta_, wide, ALU.is_equal, m)
                m = tt(tx_, tx_, tc_, ALU.mult, m, kx)
                m = red(tx_, ALU.max, m)
                m = tt(tx_, tc_, wide, ALU.is_equal, m)
                if turn_no == 0:
                    m = DVE.do(lambda e: e.tensor_copy(cb_, tx_), m)
                    m = DVE.do(lambda e: e.scalar_tensor_tensor(out=ta_, in0=tx_, scalar=-4.0, in1=ta_,
                                                                op0=ALU.mult, op1=ALU.add), m)
            m = tt(cb_, cb_, tx_, ALU.add, m)
            cm = tt(cb_, cb_, pr_, ALU.mult, m)
            yield
            for t in tiles:
                r = ROWS[t]
                i, bank, free = turn.take()
                mp = PE.do(lambda e, t=t, r=r, bank=bank: e.transpose(bank[0:8, 0:r], comb[0:r, t, :], ident[0:r, 0:r]), free, cm)
                turn.free[i] = mc[t] = ACTQ.do(lambda e, t=t, r=r, bank=bank: e.activation(
                    cT[:, P * t:P * t + r], bank[0:8, 0:r], ACT.Copy), mp, pv)
            yield

        node_tiles = [list(range(4 * c, min(4 * c + 4, NT))) for c in range(len(CHUNKS))]
        for _ in front(node_tiles[0]):
            pass
        hid = Ring([mt[:, 512 * s:512 * (s + 1)] for s in range(4)])
        hid.free = [pv] * 4
        c_out = [chan(f"c_out{i}") for i in range(4)]
        acc = x2
        ups, down = Ring([PS[2], PS[7]]), Ring([PS[0], PS[1], PS[3]])
        ups.free = [dense.free[2], edge.free[1]]
        down.free = [dense.free[0], dense.free[1], dense.free[3]]
        for c, (c0, cn) in enumerate(CHUNKS):
            tiles = node_tiles[c]
            ahead = front(node_tiles[c + 1]) if c + 1 < len(CHUNKS) else iter(())
            next(ahead, None)
            for t in tiles:
                r = ROWS[t]
                i, bank, free = down.take()
                mp = PE.do(lambda e, t=t, r=r, bank=bank: e.matmul(bank[0:r, :], cT[:, P * t:P * t + r], b2row,
                                                                   start=True, stop=True), free, mc[t], rmoe)
                acc[t] = down.free[i] = DVE.do(lambda e, t=t, r=r, bank=bank: e.tensor_tensor(
                    Yt[0:r, t, :], bank[0:r, :], Yt[0:r, t, :], ALU.add), mp, acc[t])
            def up(x):
                i, bank, free = ups.take()
                for k in range(4):
                    f = lambda e, k=k: e.matmul(bank[:, 0:cn], Wm1[:, k, x, :], xT[:, k, c0:c0 + cn],
                                                start=(k == 0), stop=(k == 3))
                    if k < 3:
                        PE.quiet(f, free, wmoe, [xf_ready[t] for t in tiles])
                    else:
                        mp = PE.do(f)
                ih, hb, hfree = hid.take()
                ups.free[i] = ACTQ.do(lambda e: e.activation(
                    hb[:, 0:cn], bank[:, 0:cn], ACT.Gelu_apprx_tanh, bias=vec[:, C_MB1 + x:C_MB1 + x + 1]), mp, hfree)
                return ih, hb, ups.free[i]

            nxt_up = up(0)
            for x in range(8):
                ih, hb, mh = nxt_up
                if x < 7:
                    nxt_up = up(x + 1)
                next(ahead, None)
                for t in tiles:
                    r, o0 = ROWS[t], P * t - c0
                    i, bank, free = down.take()
                    mp = PE.do(lambda e, x=x, r=r, o0=o0, bank=bank, hb=hb: e.matmul(
                        bank[0:r, :], hb[:, o0:o0 + r], Wm2[:, x, :], start=True, stop=True), free, mh)
                    acc[t] = down.free[i] = DVE.do(lambda e, t=t, x=x, r=r, bank=bank: e.scalar_tensor_tensor(
                        out=Yt[0:r, t, :], in0=bank[0:r, :], scalar=comb[0:r, t, x:x + 1], in1=Yt[0:r, t, :],
                        op0=ALU.mult, op1=ALU.add), mp, acc[t])
                    if t % 4 == 1:
                        next(ahead, None)
                hid.free[ih] = mp
            for t in tiles:
                r = ROWS[t]
                load(c_out[t % 4], out[P * t:P * t + r, :], Yt[0:r, t, :], acc[t])
            for _ in ahead:
                pass
        SP.wait(*[c.mark() for c in c_out])
        SP.wait(*[c.mark() for c in stg_ch])
        SP.wait(*[c.mark() for c in wd_ch])
        area.close()


def kernel(**inputs):
    import numpy as np
    import concourse.bacc as bacc
    from concourse.bass_utils import run_bass_kernel_spmd

    a = {k: np.asarray(v) for k, v in inputs.items()}
    t = lambda w: np.ascontiguousarray(np.swapaxes(w, -1, -2))
    cols = lambda v: np.concatenate([x.reshape(4, P).T for x in v], axis=1)
    it = a["dst"].dtype
    arrays = {
        "x": a["x"],
        "src": np.concatenate([a["src"], np.zeros(EP - NE, a["src"].dtype)]),
        "dst": np.concatenate([np.full(1, -1, it), a["dst"], np.full(EP - NE, N, it), np.full(1, N + 1, it)]),
        "WqT": t(a["L0_gnn_Wq"]), "WkT": t(a["L0_gnn_Wk"]), "WvT": t(a["L0_gnn_Wv"]), "WoT": t(a["L0_gnn_Wo"]),
        "W1T": t(a["L0_gnn_W1"]), "W2T": t(a["L0_gnn_W2"]), "gbq": a["L0_gnn_bq"],
        "MqT": t(a["L0_mix_Wq"]), "MkT": t(a["L0_mix_Wk"]), "MvT": t(a["L0_mix_Wv"]), "MpT": t(a["L0_mix_Wp"]),
        "mbq": a["L0_mix_bq"], "mbk": a["L0_mix_bk"], "mbv": a["L0_mix_bv"], "mbp": a["L0_mix_bp"],
        "ln_g": a["L0_gnn_ln_g"], "ln_b": a["L0_gnn_ln_b"],
        "Wg": a["L0_ffn_Wg"], "bg": a["L0_ffn_bg"], "EW1": a["L0_ffn_W1"], "EW2": a["L0_ffn_W2"], "Eb2": a["L0_ffn_b2"],
        "vec": np.concatenate([cols(a["L0_gnn_" + n]) for n in ("bo", "b2", "g1", "beta1", "g2", "beta2")]
                              + [a["L0_gnn_b1"].T, a["L0_ffn_b1"].T], axis=1),
    }
    nc = bacc.Bacc("TRN2", target_bir_lowering=False, num_devices=1)
    feed, A = {}, {}
    for name, v in arrays.items():
        v = np.ascontiguousarray(v)
        feed["in_" + name] = v
        A[name] = nc.dram_tensor("in_" + name, v.shape, mybir.dt.from_np(v.dtype), kind="ExternalInput").ap()
    out = nc.dram_tensor("out", (N, D), F32, kind="ExternalOutput").ap()
    build(nc, A, out)
    r = run_bass_kernel_spmd(nc, [feed], core_ids=[0])
    return r.results[0]["out"]
```
